# Optimizing a Trainium2 kernel written in Bass

```python
import numpy as np
import jax
import jax.numpy as jnp

def _softmax(x, axis=-1):
    return jax.nn.softmax(x, axis=axis)

def _gelu(x):
    return jax.nn.gelu(x, approximate=True)

def _silu(x):
    return jax.nn.silu(x)

def _sigmoid(x):
    return jax.nn.sigmoid(x)

def _layernorm(x, axis=-1, eps=1e-05):
    m = jnp.mean(x, axis=axis, keepdims=True)
    v = jnp.var(x, axis=axis, keepdims=True)
    return (x - m) / jnp.sqrt(v + eps)

def _scatter_add(tgt, idx, src, axis=0):
    return tgt.at[idx].add(src)

def _segment_sum(src, seg, n):
    return jax.ops.segment_sum(src, seg, n)
kernel_name = 'mk_gnn_resnorm_d4_gnn_r32_d49208'

def setup_inputs(seed: int=0):
    np.random.seed(seed)
    _w = jnp.asarray

    def _rec_inputs():
        import jax
        import jax.numpy as jnp
        _gk = jax.random.key(seed)
        x = -0.0003713 + 1 * jax.random.normal(jax.random.fold_in(_gk, 1), (3125, 256), jnp.float32)
        _s = jax.random.randint(jax.random.fold_in(_gk, 2), (25000,), 0, 3125, jnp.int32)
        _d = jax.random.randint(jax.random.fold_in(_gk, 3), (25000,), 0, 3125, jnp.int32)
        _loop = jnp.arange(3125, dtype=jnp.int32)
        src = jnp.concatenate([_s, _d, _loop])
        dst = jnp.concatenate([_d, _s, _loop])
        _o = jnp.argsort(dst, stable=True)
        src = src[_o]
        dst = dst[_o]
        edge_attr_64 = 0.000151818 + 1.00006 * jax.random.normal(jax.random.fold_in(_gk, 12), (53125, 64), jnp.float32)
        edge_type_16 = jax.random.randint(jax.random.fold_in(_gk, 14), (53125,), 0, 16, jnp.int32)
        edge_weight = jax.random.uniform(jax.random.fold_in(_gk, 15), (53125,), jnp.float32, 0.0, 4.99999)
        return (x, src, dst, edge_attr_64, edge_type_16, edge_weight)
    x, src, dst, edge_attr_64, edge_type_16, edge_weight = _rec_inputs()

    def _L0_gnn_setup():
        import jax, jax.numpy as jnp
        import numpy as np
        N_NODES = 50000
        N_EDGES = 50000
        D_IN = 256
        D_HID = 256

        def _gcn_norm(edge_index, num_nodes):
            loops = jnp.arange(num_nodes, dtype=edge_index.dtype)
            src = jnp.concatenate([edge_index[0], loops])
            dst = jnp.concatenate([edge_index[1], loops])
            ones = jnp.ones_like(src, dtype=jnp.float32)
            deg = jax.ops.segment_sum(ones, dst, num_segments=num_nodes)
            dinv = jnp.where(deg > 0, jax.lax.rsqrt(deg), 0.0)
            norm = dinv[src] * dinv[dst]
            return (src, dst, norm)

        def _gcn_layer(x, W, b, src, dst, norm, num_nodes):
            h = x @ W
            msg = h[src] * norm[:, None]
            agg = jax.ops.segment_sum(msg, dst, num_segments=num_nodes)
            return agg + b
        key = jax.random.key(seed)
        k_x, k_e, k_w1, k_w2 = jax.random.split(key, 4)
        glorot = lambda k, fi, fo: jax.random.uniform(k, (fi, fo), jnp.float32, -jnp.sqrt(6.0 / (fi + fo)), jnp.sqrt(6.0 / (fi + fo)))
        return {'x': jax.random.normal(k_x, (N_NODES, D_IN), jnp.float32), 'edge_index': jax.random.randint(k_e, (2, N_EDGES), 0, N_NODES, jnp.int64), 'W1': glorot(k_w1, D_IN, D_HID), 'b1': jnp.zeros((D_HID,), jnp.float32), 'W2': glorot(k_w2, D_HID, D_HID), 'b2': jnp.zeros((D_HID,), jnp.float32)}
    _L0_gnn_all = _L0_gnn_setup()
    _L0_gnn_in = {k: v for k, v in _L0_gnn_all.items() if k in ('W1', 'b1', 'W2', 'b2')}
    del _L0_gnn_all

    def _L1_gnn_setup():
        import jax, jax.numpy as jnp
        import numpy as np
        N_NODES = 50000
        N_EDGES = 25000
        HDIM = 256
        NUMRELS = 16

        def _gru_cell(x, h, w_ih, w_hh, b_ih, b_hh):
            gi = x @ w_ih.T + b_ih
            gh = h @ w_hh.T + b_hh
            i_r, i_z, i_n = jnp.split(gi, 3, axis=-1)
            h_r, h_z, h_n = jnp.split(gh, 3, axis=-1)
            r = jax.nn.sigmoid(i_r + h_r)
            z = jax.nn.sigmoid(i_z + h_z)
            n = jnp.tanh(i_n + r * h_n)
            return (1.0 - z) * n + z * h
        key = jax.random.key(seed)
        ks = jax.random.split(key, 9)
        h = jax.random.normal(ks[0], (N_NODES, HDIM), dtype=jnp.float32)
        relvectors = jax.random.normal(ks[1], (NUMRELS, HDIM), dtype=jnp.float32)
        s = 1.0 / np.sqrt(HDIM)
        w_ih = jax.random.uniform(ks[2], (3 * HDIM, HDIM), minval=-s, maxval=s, dtype=jnp.float32)
        w_hh = jax.random.uniform(ks[3], (3 * HDIM, HDIM), minval=-s, maxval=s, dtype=jnp.float32)
        b_ih = jax.random.uniform(ks[4], (3 * HDIM,), minval=-s, maxval=s, dtype=jnp.float32)
        b_hh = jax.random.uniform(ks[5], (3 * HDIM,), minval=-s, maxval=s, dtype=jnp.float32)
        edge_src = jax.random.randint(ks[6], (N_EDGES,), 0, N_NODES, dtype=jnp.int32)
        edge_dst = jax.random.randint(ks[7], (N_EDGES,), 0, N_NODES, dtype=jnp.int32)
        edge_rel = jax.random.randint(ks[8], (N_EDGES,), 0, NUMRELS, dtype=jnp.int32)
        return {'h': h, 'relvectors': relvectors, 'w_ih': w_ih, 'w_hh': w_hh, 'b_ih': b_ih, 'b_hh': b_hh, 'edge_src': edge_src, 'edge_dst': edge_dst, 'edge_rel': edge_rel}
    _L1_gnn_all = _L1_gnn_setup()
    _L1_gnn_in = {k: v for k, v in _L1_gnn_all.items() if k in ('relvectors', 'w_ih', 'w_hh', 'b_ih', 'b_hh')}
    del _L1_gnn_all

    def _L2_gnn_setup():
        import jax, jax.numpy as jnp
        import numpy as np
        H = 256
        R = 64
        N = 625
        E = 10000
        CUTOFF_LO = 0.0
        CUTOFF_UP = 5.0
        LN_EPS = 1e-05

        def _layernorm(x, g, b):
            mu = jnp.mean(x, axis=-1, keepdims=True)
            var = jnp.var(x, axis=-1, keepdims=True)
            return (x - mu) * jax.lax.rsqrt(var + LN_EPS) * g + b

        def _cosine_cutoff(r):
            c = 0.5 * (jnp.cos(r * (jnp.pi / CUTOFF_UP)) + 1.0)
            return c * (r < CUTOFF_UP).astype(r.dtype)
        key = jax.random.key(seed)
        ks = jax.random.split(key, 16)

        def xavier(k, shape):
            fan_in, fan_out = (shape[1], shape[0])
            lim = np.sqrt(6.0 / (fan_in + fan_out))
            return jax.random.uniform(k, shape, jnp.float32, -lim, lim)
        x = jax.random.normal(ks[0], (N, H), jnp.float32)
        edge_index = jax.random.randint(ks[1], (2, E), 0, N, jnp.int64)
        edge_weight = jax.random.uniform(ks[2], (E,), jnp.float32, 0.0, CUTOFF_UP)
        edge_attr = jax.random.normal(ks[3], (E, R), jnp.float32)
        return {'x': x, 'edge_index': edge_index, 'edge_weight': edge_weight, 'edge_attr': edge_attr, 'ln_g': jnp.ones((H,), jnp.float32), 'ln_b': jnp.zeros((H,), jnp.float32), 'Wq': xavier(ks[4], (H, H)), 'bq': jnp.zeros((H,), jnp.float32), 'Wk': xavier(ks[5], (H, H)), 'bk': jnp.zeros((H,), jnp.float32), 'Wv': xavier(ks[6], (H, H)), 'bv': jnp.zeros((H,), jnp.float32), 'Wo': xavier(ks[7], (H, H)), 'bo': jnp.zeros((H,), jnp.float32), 'Wdk': xavier(ks[8], (H, R)), 'bdk': jnp.zeros((H,), jnp.float32), 'Wdv': xavier(ks[9], (H, R)), 'bdv': jnp.zeros((H,), jnp.float32)}
    _L2_gnn_all = _L2_gnn_setup()
    _L2_gnn_in = {k: v for k, v in _L2_gnn_all.items() if k in ('ln_g', 'ln_b', 'Wq', 'bq', 'Wk', 'bk', 'Wv', 'bv', 'Wo', 'bo', 'Wdk', 'bdk', 'Wdv', 'bdv')}
    del _L2_gnn_all

    def _L3_gnn_setup():
        import jax, jax.numpy as jnp
        import numpy as np
        N_NODES = 50000
        N_EDGES = 25000
        D_IN = 256
        D_OUT = 256
        key = jax.random.key(seed)
        k1, k2, k3, k4 = jax.random.split(key, 4)
        x = jax.random.normal(k1, (N_NODES, D_IN), dtype=jnp.float32)
        edge_index = jax.random.randint(k2, (2, N_EDGES), 0, N_NODES, dtype=jnp.int64)
        W = jax.random.normal(k3, (D_OUT, D_IN), dtype=jnp.float32) * (1.0 / np.sqrt(D_IN))
        b = jax.random.normal(k4, (D_OUT,), dtype=jnp.float32) * 0.01
        return {'x': x, 'edge_index': edge_index, 'W': W, 'b': b}
    _L3_gnn_all = _L3_gnn_setup()
    _L3_gnn_in = {k: v for k, v in _L3_gnn_all.items() if k in ('W', 'b')}
    del _L3_gnn_all
    return {'x': x, 'src': src, 'dst': dst, 'edge_attr_64': edge_attr_64, 'edge_type_16': edge_type_16, 'edge_weight': edge_weight, 'L0_gnn_W1': _L0_gnn_in['W1'], 'L0_gnn_b1': _L0_gnn_in['b1'], 'L0_gnn_W2': _L0_gnn_in['W2'], 'L0_gnn_b2': _L0_gnn_in['b2'], 'L1_gnn_relvectors': _L1_gnn_in['relvectors'], 'L1_gnn_w_ih': _L1_gnn_in['w_ih'], 'L1_gnn_w_hh': _L1_gnn_in['w_hh'], 'L1_gnn_b_ih': _L1_gnn_in['b_ih'], 'L1_gnn_b_hh': _L1_gnn_in['b_hh'], 'L2_gnn_ln_g': _L2_gnn_in['ln_g'], 'L2_gnn_ln_b': _L2_gnn_in['ln_b'], 'L2_gnn_Wq': _L2_gnn_in['Wq'], 'L2_gnn_bq': _L2_gnn_in['bq'], 'L2_gnn_Wk': _L2_gnn_in['Wk'], 'L2_gnn_bk': _L2_gnn_in['bk'], 'L2_gnn_Wv': _L2_gnn_in['Wv'], 'L2_gnn_bv': _L2_gnn_in['bv'], 'L2_gnn_Wo': _L2_gnn_in['Wo'], 'L2_gnn_bo': _L2_gnn_in['bo'], 'L2_gnn_Wdk': _L2_gnn_in['Wdk'], 'L2_gnn_bdk': _L2_gnn_in['bdk'], 'L2_gnn_Wdv': _L2_gnn_in['Wdv'], 'L2_gnn_bdv': _L2_gnn_in['bdv'], 'L3_gnn_W': _L3_gnn_in['W'], 'L3_gnn_b': _L3_gnn_in['b']}

def reference(x, src, dst, edge_attr_64, edge_type_16, edge_weight, L0_gnn_W1, L0_gnn_b1, L0_gnn_W2, L0_gnn_b2, L1_gnn_relvectors, L1_gnn_w_ih, L1_gnn_w_hh, L1_gnn_b_ih, L1_gnn_b_hh, L2_gnn_ln_g, L2_gnn_ln_b, L2_gnn_Wq, L2_gnn_bq, L2_gnn_Wk, L2_gnn_bk, L2_gnn_Wv, L2_gnn_bv, L2_gnn_Wo, L2_gnn_bo, L2_gnn_Wdk, L2_gnn_bdk, L2_gnn_Wdv, L2_gnn_bdv, L3_gnn_W, L3_gnn_b):
    import jax
    import jax.numpy as jnp

    def _L0_gnn_ref(x, edge_index, W1, b1, W2, b2):
        import jax, jax.numpy as jnp
        import numpy as np
        N_NODES = 50000
        N_EDGES = 50000
        D_IN = 256
        D_HID = 256

        def _gcn_norm(edge_index, num_nodes):
            loops = jnp.arange(num_nodes, dtype=edge_index.dtype)
            src = jnp.concatenate([edge_index[0], loops])
            dst = jnp.concatenate([edge_index[1], loops])
            ones = jnp.ones_like(src, dtype=jnp.float32)
            deg = jax.ops.segment_sum(ones, dst, num_segments=num_nodes)
            dinv = jnp.where(deg > 0, jax.lax.rsqrt(deg), 0.0)
            norm = dinv[src] * dinv[dst]
            return (src, dst, norm)

        def _gcn_layer(x, W, b, src, dst, norm, num_nodes):
            h = x @ W
            msg = h[src] * norm[:, None]
            agg = jax.ops.segment_sum(msg, dst, num_segments=num_nodes)
            return agg + b
        num_nodes = x.shape[0]
        src, dst, norm = _gcn_norm(edge_index, num_nodes)
        z = jax.nn.relu(_gcn_layer(x, W1, b1, src, dst, norm, num_nodes))
        z = jax.nn.relu(_gcn_layer(z, W2, b2, src, dst, norm, num_nodes))
        return z

    def _L1_gnn_ref(h, relvectors, w_ih, w_hh, b_ih, b_hh, edge_src, edge_dst, edge_rel):
        import jax, jax.numpy as jnp
        import numpy as np
        N_NODES = 50000
        N_EDGES = 25000
        HDIM = 256
        NUMRELS = 16

        def _gru_cell(x, h, w_ih, w_hh, b_ih, b_hh):
            gi = x @ w_ih.T + b_ih
            gh = h @ w_hh.T + b_hh
            i_r, i_z, i_n = jnp.split(gi, 3, axis=-1)
            h_r, h_z, h_n = jnp.split(gh, 3, axis=-1)
            r = jax.nn.sigmoid(i_r + h_r)
            z = jax.nn.sigmoid(i_z + h_z)
            n = jnp.tanh(i_n + r * h_n)
            return (1.0 - z) * n + z * h
        msg = h[edge_src] + relvectors[edge_rel]
        red = jax.ops.segment_sum(msg, edge_dst, num_segments=h.shape[0])
        return _gru_cell(red, h, w_ih, w_hh, b_ih, b_hh)

    def _L2_gnn_ref(x, edge_index, edge_weight, edge_attr, ln_g, ln_b, Wq, bq, Wk, bk, Wv, bv, Wo, bo, Wdk, bdk, Wdv, bdv):
        import jax, jax.numpy as jnp
        import numpy as np
        H = 256
        R = 64
        N = 625
        E = 10000
        CUTOFF_LO = 0.0
        CUTOFF_UP = 5.0
        LN_EPS = 1e-05

        def _layernorm(x, g, b):
            mu = jnp.mean(x, axis=-1, keepdims=True)
            var = jnp.var(x, axis=-1, keepdims=True)
            return (x - mu) * jax.lax.rsqrt(var + LN_EPS) * g + b

        def _cosine_cutoff(r):
            c = 0.5 * (jnp.cos(r * (jnp.pi / CUTOFF_UP)) + 1.0)
            return c * (r < CUTOFF_UP).astype(r.dtype)
        src = edge_index[0]
        dst = edge_index[1]
        x_norm = _layernorm(x, ln_g, ln_b)
        q = x_norm @ Wq.T + bq
        k = x_norm @ Wk.T + bk
        v = x_norm @ Wv.T + bv
        dk = jax.nn.silu(edge_attr @ Wdk.T + bdk)
        dv = jax.nn.silu(edge_attr @ Wdv.T + bdv)
        q_i = q[dst]
        k_j = k[src]
        v_j = v[src]
        attn = jnp.sum(q_i * k_j * dk, axis=1)
        attn = jax.nn.silu(attn) * _cosine_cutoff(edge_weight)
        msg = v_j * dv * attn[:, None]
        agg = jax.ops.segment_sum(msg, dst, num_segments=x.shape[0])
        out = agg @ Wo.T + bo
        return x + out

    def _L3_gnn_ref(x, edge_index, W, b):
        import jax, jax.numpy as jnp
        import numpy as np
        N_NODES = 50000
        N_EDGES = 25000
        D_IN = 256
        D_OUT = 256
        N = x.shape[0]
        loop = jnp.arange(N, dtype=edge_index.dtype)
        row = jnp.concatenate([edge_index[0], loop])
        col = jnp.concatenate([edge_index[1], loop])
        ew = jnp.ones(row.shape[0], dtype=x.dtype)
        deg = jax.ops.segment_sum(ew, col, num_segments=N)
        dinv = jnp.where(deg > 0, jax.lax.rsqrt(deg), jnp.zeros_like(deg))
        norm = dinv[row] * dinv[col]
        msg = x[row] * norm[:, None]
        agg = jax.ops.segment_sum(msg, col, num_segments=N)
        return agg @ W.T + b
    edge_index = jnp.stack([src, dst])
    x = _layernorm(x + _L0_gnn_ref(x, edge_index, L0_gnn_W1, L0_gnn_b1, L0_gnn_W2, L0_gnn_b2), axis=-1)
    x = _layernorm(x + _L1_gnn_ref(x, L1_gnn_relvectors, L1_gnn_w_ih, L1_gnn_w_hh, L1_gnn_b_ih, L1_gnn_b_hh, src, dst, edge_type_16), axis=-1)
    x = _layernorm(x + _L2_gnn_ref(x, edge_index, edge_weight, edge_attr_64, L2_gnn_ln_g, L2_gnn_ln_b, L2_gnn_Wq, L2_gnn_bq, L2_gnn_Wk, L2_gnn_bk, L2_gnn_Wv, L2_gnn_bv, L2_gnn_Wo, L2_gnn_bo, L2_gnn_Wdk, L2_gnn_bdk, L2_gnn_Wdv, L2_gnn_bdv), axis=-1)
    x = _layernorm(x + _L3_gnn_ref(x, edge_index, L3_gnn_W, L3_gnn_b), axis=-1)
    return x

_drawn_inputs = setup_inputs


def setup_inputs(seed=0):
    import zlib

    import numpy as np

    out = dict(_drawn_inputs(seed))
    spreads = {'L0_gnn_b1': (0.0, 0.1),
     'L0_gnn_b2': (0.0, 0.1),
     'L2_gnn_ln_g': (1.0, 0.2),
     'L2_gnn_ln_b': (0.0, 0.1),
     'L2_gnn_bq': (0.0, 0.1),
     'L2_gnn_bk': (0.0, 0.1),
     'L2_gnn_bv': (0.0, 0.1),
     'L2_gnn_bo': (0.0, 0.1),
     'L2_gnn_bdk': (0.0, 0.1),
     'L2_gnn_bdv': (0.0, 0.1)}
    factors = {'L1_gnn_b_ih': 5.692, 'L1_gnn_b_hh': 7.394, 'L3_gnn_b': 6.426}
    for name, (base, spread) in spreads.items():
        noise = np.random.default_rng([zlib.crc32(name.encode()), seed]).standard_normal(out[name].shape)
        drawn = base * np.exp(spread * noise) if base else spread * noise
        out[name] = jnp.asarray(drawn.astype(out[name].dtype))
    for name, factor in factors.items():
        out[name] = (out[name] * factor).astype(out[name].dtype)
    return out
```

```python
from contextlib import ExitStack

import numpy as np

import concourse.bass as bass
import concourse.mybir as mybir

F32 = mybir.dt.float32
F16 = mybir.dt.float16
BF16 = mybir.dt.bfloat16
I32 = mybir.dt.int32
ALU = mybir.AluOpType
ACT = mybir.ActivationFunctionType
AX = mybir.AxisListType

P = 128
NODES = 3125
EDGES = 53125
D = 256
HALF = D // P
ATTR = 64
RELS = 16
NODE_TILES = -(-NODES // P)
NODES_P = NODE_TILES * P
EDGE_TILES = -(-EDGES // P)
EDGES_P = EDGE_TILES * P
NO_NODE = 4095
SEL_J = 4
SEL_P = EDGE_TILES // SEL_J
BUILD_W = 8
BUILD_WINDOWS = NODES_P // BUILD_W
BUILD_STEPS = EDGE_TILES + BUILD_WINDOWS
EDGE_STEPS = EDGE_TILES + NODE_TILES - 1
CHUNK = 400
CHUNKS = NODES_P // CHUNK
LN_EPS = 1e-5


class Chain:

    def __init__(self, engine, sem):
        self.engine, self.sem, self.n = engine, sem, 0

    def __call__(self, instruction):
        self.n += 1
        instruction.then_inc(self.sem, 1)
        self.engine.wait_ge(self.sem, self.n)


class Scope:

    def __init__(self, nc, name):
        self.nc, self.name, self.stack, self.semaphores = nc, name, ExitStack(), []

    def __enter__(self):
        self.stack.__enter__()
        return self

    def __exit__(self, *a):
        self.stack.__exit__(*a)
        if self.semaphores:
            self.nc.clear_and_free_semaphores(self.semaphores)
            self.nc.all_engine_barrier()

    def sb(self, name, shape, dt=F32):
        return self.stack.enter_context(self.nc.sbuf_tensor(f"{self.name}_{name}", list(shape), dt))

    def ps(self, name, shape, dt=F32):
        return self.stack.enter_context(self.nc.psum_tensor(f"{self.name}_{name}", list(shape), dt))

    def sem(self, name):
        self.semaphores.append(self.nc.alloc_semaphore(name=f"{self.name}_{name}"))
        return self.semaphores[-1]

    def sems(self, name, n):
        return [self.sem(f"{name}{k}") for k in range(n)]

    def block(self):
        return self.stack.enter_context(self.nc.Block())


def staircase_steps(nc, name, io, window, steps, kept, more=None):
    shift = window.bit_length() - 1
    parts = -(-steps // 512)
    width = -(-steps // parts)
    with Scope(nc, name) as sc:
        src_i = sc.sb("src_i", [SEL_P, SEL_J, P], I32)
        dst_i = sc.sb("dst_i", [SEL_P, SEL_J, P], I32)
        next_i = sc.sb("next_i", [SEL_P, SEL_J], I32)
        first_i = sc.sb("first_i", [SEL_P, SEL_J], I32)
        wts = sc.sb("wts", [SEL_P, SEL_J, P])
        src_f = sc.sb("src_f", [SEL_P, SEL_J, P])
        dst_f = sc.sb("dst_f", [SEL_P, SEL_J, P])
        tile_f = sc.sb("tile_f", [SEL_P, SEL_J, P])
        starts = sc.sb("starts", [SEL_P, 2, SEL_J])
        step_no = sc.sb("step_no", [P, steps])
        after = sc.sb("after", [SEL_P, steps])
        select = sc.sb("select", [SEL_P, SEL_J, steps])
        sums = [sc.ps(f"sums{v}", [P, parts, 512]) for v in range(3 if parts > 1 else 4)]
        loaded, iotas, selected, picked, dve_own = (
            sc.sem(n) for n in ("loaded", "iotas", "selected", "picked", "dve_own"))
        values = [src_f, dst_f, tile_f, wts][:len(sums)]
        block = sc.block()
        if more is not None:
            more(block)

        @block.sync
        def _(sp):
            by_tile = lambda a: a.rearrange("(p j) e -> p j e", j=SEL_J)
            sp.dma_start(src_i[:, :, :], by_tile(io["src_t"][0:EDGE_TILES])).then_inc(loaded, 16)
            sp.dma_start(dst_i[:, :, :], by_tile(io["dst_t"][0:EDGE_TILES])).then_inc(loaded, 16)
            sp.dma_start(next_i[:, :], io["next_t"].rearrange("(p j) -> p j", j=SEL_J)).then_inc(loaded, 16)
            sp.dma_start(wts[:, :, :], by_tile(io["wts_t"][0:EDGE_TILES])).then_inc(loaded, 16)

        @block.gpsimd
        def _(pool):
            nc.gpsimd.iota(step_no[:, :], pattern=[[1, steps]], base=0, channel_multiplier=0,
                           allow_small_or_imprecise_dtypes=True).then_inc(iotas, 1)
            nc.gpsimd.iota(tile_f[:, :, :], pattern=[[1, SEL_J], [0, P]], base=0, channel_multiplier=SEL_J,
                           allow_small_or_imprecise_dtypes=True).then_inc(iotas, 1)

        @block.vector
        def _(dve):
            own = Chain(dve, dve_own)
            dve.wait_ge(loaded, 64)
            dve.wait_ge(iotas, 2)
            own(nc.vector.tensor_copy(first_i[:, :], dst_i[:, :, 0]))
            own(nc.vector.memset(first_i[0:1, 0:1], 0))
            own(nc.vector.tensor_scalar(first_i[:, :], first_i[:, :], shift, None, ALU.logical_shift_right))
            own(nc.vector.tensor_scalar(next_i[:, :], next_i[:, :], shift, None, ALU.logical_shift_right))
            own(nc.vector.tensor_tensor(starts[:, 0, :], first_i[:, :], tile_f[:, :, 0], ALU.add))
            own(nc.vector.scalar_tensor_tensor(starts[:, 1, :], next_i[:, :], 1.0, tile_f[:, :, 0],
                                               ALU.add, ALU.add))
            own(nc.vector.tensor_copy(src_f[:, :, :], src_i[:, :, :]))
            own(nc.vector.tensor_copy(dst_f[:, :, :], dst_i[:, :, :]))
            for j in range(SEL_J):
                own(nc.vector.tensor_scalar(after[:, :], step_no[0:SEL_P, :], starts[:, 1, j:j + 1], None,
                                            ALU.is_ge))
                last = nc.vector.scalar_tensor_tensor(select[:, j, :], step_no[0:SEL_P, :], starts[:, 0, j:j + 1],
                                                      after[:, :], ALU.is_ge, ALU.subtract)
                own(last)
            nc.vector.nop().then_inc(selected, 1)
            dve.wait_ge(picked, 1)
            kept(sc, dve, own, [[s[:, h, 0:width] for h in range(parts)] for s in sums], step_no, width)

        @block.tensor
        def _(pe):
            pe.wait_ge(selected, 1)
            for v, value in enumerate(values):
                for h in range(parts):
                    for j in range(SEL_J):
                        last = nc.tensor.matmul(sums[v][:, h, 0:width], value[:, j, :],
                                                select[:, j, h * width:(h + 1) * width],
                                                start=(j == 0), stop=(j == SEL_J - 1))
            last.then_inc(picked, 1)


def build_steps(nc, io, keep):

    def kept(sc, dve, own, cols, step_no, width):
        own(nc.vector.memset(keep["cells"][:, BUILD_STEPS:, :], -1.0))
        raw = sc.sb("raw", [P, width], I32)
        win = sc.sb("win", [P, width])
        col = sc.sb("col", [P, width])
        ok = sc.sb("ok", [P, width])
        ok2 = sc.sb("ok2", [P, width])
        for h, (src, dst, tile) in enumerate(zip(*cols)):
            at = slice(h * width, (h + 1) * width)
            own(nc.vector.tensor_copy(raw[:, :], src))
            own(nc.vector.tensor_scalar(raw[:, :], raw[:, :], P - 1, None, ALU.bitwise_and))
            own(nc.vector.tensor_copy(keep["cells"][:, at, 0], raw[:, :]))
            own(nc.vector.tensor_tensor(col[:, :], src, keep["cells"][:, at, 0], ALU.subtract))
            own(nc.vector.tensor_tensor(win[:, :], step_no[:, at], tile, ALU.subtract))
            own(nc.vector.tensor_scalar(keep["window"][0:1, at], win[0:1, :], float(BUILD_WINDOWS - 1),
                                        float(BUILD_W), ALU.min, ALU.mult))
            own(nc.vector.scalar_tensor_tensor(win[:, :], win[:, :], -float(BUILD_W), dst, ALU.mult, ALU.add))
            own(nc.vector.tensor_scalar(ok[:, :], win[:, :], 0.0, None, ALU.is_ge))
            own(nc.vector.scalar_tensor_tensor(ok2[:, :], win[:, :], float(BUILD_W), ok[:, :], ALU.is_lt,
                                               ALU.mult))
            own(nc.vector.scalar_tensor_tensor(col[:, :], col[:, :], BUILD_W / P, win[:, :], ALU.mult, ALU.add))
            own(nc.vector.scalar_tensor_tensor(col[:, :], col[:, :], 1.0, ok2[:, :], ALU.add, ALU.mult))
            own(nc.vector.tensor_scalar(keep["cells"][:, at, 1], col[:, :], 1.0, None, ALU.subtract))

    staircase_steps(nc, "bsteps", io, BUILD_W, BUILD_STEPS, kept)


class RowHots:

    def __init__(self, sc):
        self.hot = sc.sb("row_hot", [P, 16, P], F16)
        self.now = sc.sb("row_now", [P, 2, 8])
        self.distance = sc.sb("distance", [P, 2, 8, P], F16)
        self.copied, self.apart, self.ready, self.tick = (
            sc.sem(n) for n in ("row_copied", "row_apart", "row_ready", "row_tick"))

    def on_scalar(self, nc, act, keep, cells, steps, used):
        act.sem_inc(self.ready, 2)
        with act.Fori(0, steps // 16) as i:
            for n in range(2):
                act.wait_ge(self.ready, i * 2 + n + 1)
                act.sem_inc(self.tick, 1)
                nc.scalar.activation(self.now[:, n, :], cells[:, bass.ds(i * 16 + n * 8, 8), 0],
                                     ACT.Copy).then_inc(self.copied, 1)
                act.wait_ge(self.copied, i * 2 + n + 1)
                for k in range(8):
                    nc.scalar.activation(self.distance[:, n, k, :], keep["iota"][:, 0:P], ACT.Abs,
                                         bias=self.now[:, n, k:k + 1], scale=-1.0).then_inc(self.apart, 1)
                act.wait_ge(self.apart, i * 16 + n * 8 + 8)
                act.sem_inc(self.tick, 1)
                act.wait_ge(used, i * 16 + n * 8 + 8)
                nc.scalar.activation(self.hot[:, n * 8:n * 8 + 8, :].rearrange("p k e -> p (k e)"),
                                     self.distance[:, n, :, :].rearrange("p k e -> p (k e)"), ACT.Relu, bias=1.0,
                                     scale=-1.0).then_inc(self.ready, 1)


def histogram(nc, io, keep):
    GROUP = 8
    with Scope(nc, "hist") as sc:
        dst_i = sc.sb("dst_i", [P, EDGE_TILES], I32)
        rel_i = sc.sb("rel_i", [P, EDGE_TILES], I32)
        high = sc.sb("high", [P, EDGE_TILES])
        cells = sc.sb("cells", [P, EDGE_TILES + GROUP, 2])
        now = sc.sb("now", [P, GROUP, 2])
        root = sc.sb("root", [P, NODE_TILES])
        copied, celled = sc.sem("copied"), sc.sem("celled")
        rows = RowHots(sc)
        key_hot = sc.sb("key_hot", [P, GROUP, NODE_TILES * RELS], F16)
        counts = sc.sb("counts", [P, NODE_TILES * RELS])
        deg = sc.sb("deg", [P, NODE_TILES])
        rel_rows = sc.sb("rel_rows", [RELS, NODES_P])
        zero = sc.sb("zero", [P, NODE_TILES * RELS], F16)
        ps = sc.ps("counts_ps", [P, NODE_TILES * RELS])
        tr = sc.ps("rel_ps", [P, 2, 512])
        loaded, ready, used, dve_own, iotas, summed, counted, rooted, turned, moved, stored, zeroed, tick = (
            sc.sem(n) for n in ("loaded", "ready", "used", "dve_own", "iotas", "summed", "counted", "rooted",
                                "turned", "moved", "stored", "zeroed", "tick"))
        block = sc.block()
        groups = -(-NODE_TILES // 4)

        @block.sync
        def _(sp):
            sp.dma_start(dst_i[:, :], io["dst_p"]).then_inc(loaded, 16)
            sp.dma_start(rel_i[:, :], io["rel_p"]).then_inc(loaded, 16)
            sp.wait_ge(moved, groups)
            sp.dma_start(io["rel_counts"], rel_rows[:, :]).then_inc(stored, 16)
            sp.wait_ge(stored, 16)

        @block.gpsimd
        def _(pool):
            nc.gpsimd.iota(keep["iota"][:, :], pattern=[[1, NODE_TILES * RELS]], base=0, channel_multiplier=0,
                           allow_small_or_imprecise_dtypes=True).then_inc(iotas, 1)
            nc.gpsimd.memset(zero[:, :], 0.0).then_inc(zeroed, 1)
            nc.gpsimd.memset(keep["ident"][:, :], 0.0).then_inc(iotas, 1)
            pool.wait_ge(iotas, 2)
            nc.gpsimd.affine_select(out=keep["ident"][:, :], in_=keep["ident"][:, :], compare_op=ALU.not_equal,
                                    fill=1.0, base=0, pattern=[[-1, P]], channel_multiplier=1).then_inc(iotas, 1)
            nc.gpsimd.memset(keep["adj"][:, 0:12, :], 0.0).then_inc(zeroed, 1)

        @block.vector
        def _(dve):
            own = Chain(dve, dve_own)
            dve.wait_ge(loaded, 32)
            dve.wait_ge(iotas, 3)
            raw = high[:, :].bitcast(I32)
            low, key = cells[:, 0:EDGE_TILES, 0], cells[:, 0:EDGE_TILES, 1]
            own(nc.vector.memset(cells[:, EDGE_TILES:, :], -1.0))
            own(nc.vector.tensor_scalar(raw, dst_i[:, :], P - 1, None, ALU.bitwise_and))
            own(nc.vector.tensor_copy(low, raw))
            own(nc.vector.tensor_copy(key, dst_i[:, :]))
            own(nc.vector.tensor_tensor(high[:, :], key, low, ALU.subtract))
            own(nc.vector.scalar_tensor_tensor(key, high[:, :], RELS / P, rel_i[:, :], ALU.mult, ALU.add))
            nc.vector.tensor_copy(now[:, :, :], cells[:, 0:GROUP, :]).then_inc(copied, 1)
            nc.vector.nop().then_inc(celled, 1)
            with dve.Fori(0, EDGE_TILES // GROUP) as i:
                dve.wait_ge(copied, i + 1)
                for n in range(2):
                    dve.wait_ge(used, i * GROUP + (n + 1) * GROUP // 2 + 8)
                    for k in range(n * GROUP // 2, (n + 1) * GROUP // 2):
                        nc.vector.tensor_scalar(key_hot[:, k, :], keep["iota"][:, :], now[:, k, 1:2], None,
                                                ALU.is_equal).then_inc(ready, 1)
                dve.wait_ge(ready, i * GROUP + GROUP)
                nc.vector.tensor_copy(now[:, :, :], cells[:, bass.ds(i * GROUP + GROUP, GROUP), :]).then_inc(copied, 1)
            dve.wait_ge(summed, 1)
            own(nc.vector.tensor_copy(counts[:, :], ps[:, :]))
            nc.vector.nop().then_inc(counted, 1)
            own(nc.vector.reduce_sum(deg[:, :], counts[:, :].rearrange("p (w r) -> p w r", r=RELS), axis=AX.X))
            own(nc.vector.tensor_scalar(deg[:, :], deg[:, :], 1.0, None, ALU.add))
            nc.vector.nop().then_inc(counted, 1)
            dve.wait_ge(rooted, 1)
            own(nc.vector.reciprocal(keep["dinv"][:, :], root[:, :]))
            for g in range(groups):
                n = min(4, NODE_TILES - 4 * g) * P
                dve.wait_ge(turned, g + 1)
                nc.vector.tensor_copy(rel_rows[:, g * 512:g * 512 + n], tr[0:RELS, g % 2, 0:n]).then_inc(moved, 1)
            nc.vector.memset(keep["adj"][:, 12:NODE_TILES, :], 0.0)

        @block.scalar
        def _(act):
            act.wait_ge(celled, 1)
            rows.on_scalar(nc, act, keep, cells, EDGE_TILES, used)
            act.wait_ge(counted, 2)
            nc.scalar.activation(root[:, :], deg[:, :], ACT.Sqrt).then_inc(rooted, 1)

        @block.tensor
        def _(pe):
            pe.wait_ge(zeroed, 1)
            nc.tensor.matmul(ps[:, :], zero[:, 0:P], zero[:, :], start=True, stop=False).then_inc(used, 16)
            with pe.Fori(0, EDGE_TILES // 16) as i:
                for k in range(16):
                    if k % 8 == 0:
                        pe.wait_ge(rows.ready, i * 2 + k // 8 + 3)
                        pe.sem_inc(tick, 1)
                    pe.wait_ge(ready, i * 16 + k + 1)
                    nc.tensor.matmul(ps[:, :], rows.hot[:, k, :], key_hot[:, k % GROUP, :], start=False,
                                     stop=False).then_inc(used, 1)
            nc.tensor.matmul(ps[:, :], zero[:, 0:P], zero[:, :], start=False, stop=True).then_inc(summed, 1)
            pe.wait_ge(counted, 1)
            pe.wait_ge(iotas, 3)
            for g in range(groups):
                if g >= 2:
                    pe.wait_ge(moved, g - 1)
                for b in range(min(4, NODE_TILES - 4 * g)):
                    t = 4 * g + b
                    last = nc.tensor.transpose(tr[0:RELS, g % 2, b * P:(b + 1) * P],
                                               counts[:, t * RELS:(t + 1) * RELS], keep["ident"][:, :])
                last.then_inc(turned, 1)


def change_loops(nc, dve, keep, how, looped):
    with dve.Fori(0, NODE_TILES) as t:
        block = keep["adj"][:, bass.ds(t, 1), bass.ds(t * P, P)].rearrange("p a d -> p (a d)")
        nc.vector.tensor_tensor(block, block, keep["ident"][:, :], how).then_inc(looped, 1)


def build_matrix(nc, io, keep):
    GROUP = 8
    with Scope(nc, "build") as sc:
        rows = RowHots(sc)
        col_hot = sc.sb("col_hot", [P, GROUP, NODE_TILES * BUILD_W], F16)
        part = sc.ps("part", [P, GROUP, 512])
        now = sc.sb("now", [P, GROUP, 2])
        hots_ready, multiplied, own, looped, tick = (
            sc.sem(n) for n in ("hots_ready", "multiplied", "own", "looped", "tick"))
        block = sc.block()

        @block.vector
        def _(dve):
            adj = keep["adj"]
            def one_hots(k):
                nc.vector.tensor_scalar(col_hot[:, k, :], keep["iota"][:, 0:NODE_TILES * BUILD_W], now[:, k, 1:2],
                                        None, ALU.is_equal).then_inc(hots_ready, 1)

            nc.vector.tensor_copy(now[:, :, :], keep["cells"][:, 0:GROUP, :]).then_inc(own, 1)
            dve.wait_ge(own, 1)
            for k in range(GROUP):
                one_hots(k)
            dve.sem_clear(own)
            with dve.Fori(0, BUILD_STEPS // GROUP) as i:
                _, columns = nc.values_load_multi_w_load_instructions(
                    keep["window"][0:1, bass.ds(i * GROUP, GROUP)], engines=[mybir.EngineType.DVE], min_val=0,
                    max_val=NODES_P - BUILD_W,
                    skip_runtime_bounds_check_because="the columns are the chip's own, held to the last window")
                dve.wait_ge(hots_ready, i * GROUP + GROUP)
                nc.vector.tensor_copy(now[:, :, :], keep["cells"][:, bass.ds(i * GROUP + GROUP, GROUP), :]).then_inc(
                    own, 1)
                dve.wait_ge(multiplied, i * GROUP + GROUP + 16)
                for k in range(GROUP):
                    at = adj[:, :, bass.ds(columns[k], BUILD_W)]
                    dve.wait_ge(own, k + 1)
                    nc.vector.tensor_tensor(at, at, part[:, k, 0:NODE_TILES * BUILD_W].rearrange(
                        "p (s w) -> p s w", w=BUILD_W), ALU.add).then_inc(own, 1)
                    one_hots(k)
                dve.wait_ge(own, GROUP + 1)
                dve.sem_clear(own)
            change_loops(nc, dve, keep, ALU.add, looped)

        @block.scalar
        def _(act):
            rows.on_scalar(nc, act, keep, keep["cells"], BUILD_STEPS, multiplied)

        @block.tensor
        def _(pe):
            pe.sem_inc(multiplied, 16)
            with pe.Fori(0, BUILD_STEPS // 16) as i:
                for k in range(16):
                    if k % 8 == 0:
                        pe.wait_ge(rows.ready, i * 2 + k // 8 + 3)
                        pe.sem_inc(tick, 1)
                    pe.wait_ge(hots_ready, i * 16 + k + 1)
                    nc.tensor.matmul(part[:, k % GROUP, 0:NODE_TILES * BUILD_W], rows.hot[:, k, :],
                                     col_hot[:, k % GROUP, :], start=True, stop=True).then_inc(multiplied, 1)


def aggregate(nc, io, keep, name, source, scaled=False, relations=False, save=False, load=False):
    SLOTS = 5
    with Scope(nc, name) as sc:
        parts = sc.sb("parts", [P, NODE_TILES, 3, D], BF16)
        raw = sc.sb("raw", [P, SLOTS, D])
        staged = sc.sb("staged", [P, HALF, CHUNK])
        ps = sc.ps("sums", [P, 2, HALF, 512])
        if relations:
            counts = sc.sb("counts", [RELS, CHUNK])
            vectors = sc.sb("vectors", [RELS, D])
            rel_loaded, vec_loaded, looped = sc.sem("rel_loaded"), sc.sem("vec_loaded"), sc.sem("looped")
        loaded = sc.sems("loaded", SLOTS)
        prepared, high_done, rest_done, mid_done, low_done, summed, out0, out1, free, tick = (
            sc.sem(n) for n in ("prepared", "high_done", "rest_done", "mid_done", "low_done", "summed", "out0",
                                "out1", "free", "tick"))
        stored = sc.sems("stored", HALF)
        saved = sc.sem("saved")
        restored = sc.sems("restored", 5) if load else []
        block = sc.block()
        adj = keep["adj"]
        rows = source.rearrange("(t p) f -> t p f", p=P)

        @block.sync
        def _(sp):
            for k in range(SLOTS):
                sp.dma_start(raw[:, k, :], rows[k]).then_inc(loaded[k], 16)
            if relations:
                sp.dma_start(vectors[:, :], io["relvectors"]).then_inc(vec_loaded, 16)
            if load:
                for g in range(5):
                    sp.dma_start(adj[:, 5 * g:5 * g + 5, :], io["adj_copy"][:, 5 * g:5 * g + 5, :]).then_inc(
                        restored[g], 16)
            with sp.Fori(1, NODE_TILES // SLOTS) as i:
                for k in range(SLOTS):
                    sp.wait_ge(low_done, (i - 1) * SLOTS + k + 1)
                    sp.dma_start(raw[:, k, :], source[bass.ds((i * SLOTS + k) * P, P), :]).then_inc(loaded[k], 16)
            if save:
                for g in range(5):
                    sp.dma_start(io["adj_copy"][:, 5 * g:5 * g + 5, :], adj[:, 5 * g:5 * g + 5, :]).then_inc(saved, 16)
            with sp.Fori(0, CHUNKS) as c:
                if relations:
                    sp.wait_ge(summed, c + 1)
                    sp.dma_start(counts[:, :], io["rel_counts"][:, bass.ds(c * CHUNK, CHUNK)]).then_inc(rel_loaded, 16)
                for h, out in enumerate((out0, out1)):
                    sp.wait_ge(out, c + 3)
                    sp.dma_start(io["agg_t"][h, :, bass.ds(c * CHUNK, CHUNK)], staged[:, h, :]).then_inc(stored[h], 16)
                for h in range(HALF):
                    sp.wait_ge(stored[h], (c + 1) * 16)
                sp.sem_inc(free, 1)
            if save:
                sp.wait_ge(saved, 80)

        @block.vector
        def _(dve):
            if relations:
                change_loops(nc, dve, keep, ALU.subtract, looped)
            with dve.Fori(0, NODE_TILES // SLOTS) as i:
                for k in range(SLOTS):
                    dve.wait_ge(loaded[k], i * 16 + 16)
                    if scaled:
                        nc.vector.tensor_scalar(raw[:, k, :], raw[:, k, :],
                                                keep["dinv"][:, bass.ds(i * SLOTS + k, 1)], None,
                                                ALU.mult).then_inc(prepared, 1)
                    else:
                        dve.sem_inc(prepared, 1)
                for k in range(SLOTS):
                    dve.wait_ge(high_done, i * SLOTS + k + 1)
                    nc.vector.tensor_tensor(raw[:, k, :], raw[:, k, :], parts[:, bass.ds(i * SLOTS + k, 1), 0, :].rearrange(
                        "p a f -> p (a f)"), ALU.subtract).then_inc(rest_done, 1)
                for k in range(SLOTS):
                    dve.wait_ge(mid_done, i * SLOTS + k + 1)
                    nc.vector.tensor_tensor(parts[:, bass.ds(i * SLOTS + k, 1), 2, :].rearrange("p a f -> p (a f)"),
                                            raw[:, k, :], parts[:, bass.ds(i * SLOTS + k, 1), 1, :].rearrange(
                        "p a f -> p (a f)"), ALU.subtract).then_inc(low_done, 1)
            with dve.Fori(0, CHUNKS // 2) as j:
                for par in range(2):
                    dve.wait_ge(free, j * 2 + par + 1)
                    dve.wait_ge(summed, j * 2 + par + 2)
                    nc.vector.tensor_copy(staged[:, 1, :], ps[:, par, 1, 0:CHUNK]).then_inc(out1, 1)

        @block.scalar
        def _(act):
            act.sem_inc(out0, 2)
            act.sem_inc(out1, 2)
            act.sem_inc(free, 1)
            act.sem_inc(summed, 1)
            with act.Fori(0, NODE_TILES // SLOTS) as i:
                for part, before, after in ((0, prepared, high_done), (1, rest_done, mid_done)):
                    for k in range(SLOTS):
                        act.wait_ge(before, i * SLOTS + k + 1)
                        act.sem_inc(tick, 1)
                        nc.scalar.activation(parts[:, bass.ds(i * SLOTS + k, 1), part, :].rearrange("p a f -> p (a f)"),
                                             raw[:, k, :], ACT.Copy).then_inc(after, 1)
            with act.Fori(0, CHUNKS // 2) as j:
                for par in range(2):
                    act.wait_ge(free, j * 2 + par + 1)
                    act.sem_inc(tick, 1)
                    act.wait_ge(summed, j * 2 + par + 2)
                    nc.scalar.activation(staged[:, 0, :], ps[:, par, 0, 0:CHUNK], ACT.Copy).then_inc(out0, 1)

        @block.tensor
        def _(pe):
            if relations:
                pe.wait_ge(vec_loaded, 16)
                pe.wait_ge(looped, NODE_TILES)
            with pe.Fori(0, CHUNKS // 2) as j:
                for par in range(2):
                    pe.wait_ge(out0, j * 2 + par + 1)
                    pe.sem_inc(tick, 1)
                    pe.wait_ge(out1, j * 2 + par + 1)
                    pe.sem_inc(tick, 1)
                    for s in range(NODE_TILES):
                        pe.wait_ge(low_done, s + 1)
                        if load and s % 5 == 0:
                            pe.wait_ge(restored[s // 5], 16)
                        for h in range(HALF):
                            for part in range(3):
                                last = nc.tensor.matmul(ps[:, par, h, 0:CHUNK], parts[:, s, part, h * P:(h + 1) * P],
                                                        adj[:, s, bass.ds((j * 2 + par) * CHUNK, CHUNK)],
                                                        start=(s == 0 and part == 0),
                                                        stop=(s == NODE_TILES - 1 and part == 2 and not relations))
                    if relations:
                        pe.wait_ge(rel_loaded, (j * 2 + par + 1) * 16)
                        pe.sem_inc(tick, 1)
                        for h in range(HALF):
                            last = nc.tensor.matmul(ps[:, par, h, 0:CHUNK], vectors[:, h * P:(h + 1) * P],
                                                    counts[:, :], start=False, stop=True)
                    last.then_inc(summed, 1)


SLOTS = 5
ROUNDS = NODE_TILES // SLOTS


def each(engine, i, waits, emit, done, tick=None):
    for k in range(SLOTS):
        for w in waits:
            engine.wait_ge(w, i * SLOTS + k + 1)
            if tick is not None:
                engine.sem_inc(tick, 1)
        emit(k).then_inc(done, 1)


def load_slots(sp, loads, loaded, stored, per_store):
    for k in range(SLOTS):
        for to, source in loads:
            sp.dma_start(to(k), source(k)).then_inc(loaded[k], 16)
    with sp.Fori(1, ROUNDS) as i:
        for k in range(SLOTS):
            sp.wait_ge(stored[k], i * (16 * per_store))
            for to, source in loads:
                sp.dma_start(to(k), source(i * SLOTS + k)).then_inc(loaded[k], 16)


def store_slots(pool, stores, ready, stored, tick):
    with pool.Fori(0, ROUNDS) as i:
        for k in range(SLOTS):
            pool.wait_ge(ready, i * SLOTS + k + 1)
            pool.sem_inc(tick, 1)
            for dest, what in stores:
                pool.dma_start(dest(i * SLOTS + k), what(k)).then_inc(stored[k], 16)
    for k in range(SLOTS):
        pool.wait_ge(stored[k], 16 * len(stores) * ROUNDS)


def tile_rows(a):
    return lambda t: a[bass.ds(t * P, P), :]


class Norm:

    def __init__(self, sc):
        self.stats = sc.sb("stats", [P, SLOTS, 6])
        self.mean_var = sc.sb("mean_var", [P, SLOTS, 2])
        self.spread = sc.sb("spread", [P, SLOTS])
        self.inverse = sc.sb("inverse", [P, SLOTS])
        self.power = sc.sb("power", [P, 1])
        (self.stat_done, self.mean_done, self.spread_done, self.inverse_done, self.power_set,
         self.tick) = (sc.sem(n) for n in ("stat_done", "mean_done", "spread_done", "inverse_done", "power_set",
                                           "norm_tick"))

    def set_power(self, nc, pool):
        nc.gpsimd.memset(self.power[:, :], -0.5).then_inc(self.power_set, 1)
        pool.wait_ge(self.power_set, 1)

    def on_vector(self, nc, dve, i, y, before, out, done):
        each(dve, i, [before], lambda k: nc.vector.bn_stats(self.stats[:, k, :], y(k)), self.stat_done)
        each(dve, i, [self.stat_done], lambda k: nc.vector.bn_aggr(self.mean_var[:, k, :], self.stats[:, k, :]),
             self.mean_done, self.tick)
        each(dve, i, [self.mean_done], lambda k: nc.vector.tensor_scalar(
            self.spread[:, k:k + 1], self.mean_var[:, k, 1:2], LN_EPS, None, ALU.add), self.spread_done)
        each(dve, i, [self.inverse_done], lambda k: nc.vector.tensor_scalar(
            out(k), y(k), self.mean_var[:, k, 0:1], self.inverse[:, k:k + 1], ALU.subtract, ALU.mult), done)

    def on_pool(self, nc, pool, i):
        each(pool, i, [self.spread_done], lambda k: nc.gpsimd.tensor_tensor(
            self.inverse[:, k:k + 1], self.spread[:, k:k + 1], self.power[:, :], ALU.pow), self.inverse_done)


def norm_and_store(nc, pool, norm, stores, ready, stored, tick):
    norm.set_power(nc, pool)
    with pool.Fori(0, ROUNDS) as i:
        norm.on_pool(nc, pool, i)
        for k in range(SLOTS):
            pool.wait_ge(ready, i * SLOTS + k + 1)
            pool.sem_inc(tick, 1)
            for dest, what in stores:
                pool.dma_start(dest(i * SLOTS + k), what(k)).then_inc(stored[k], 16)
    for k in range(SLOTS):
        pool.wait_ge(stored[k], 16 * len(stores) * ROUNDS)


def agg_tiles(io):
    return lambda t: io["agg_t"][:, :, bass.ds(t * P, P)].rearrange("h p n -> p h n")


def gcn_update(nc, io, keep, name, weight, bias, dest, residual=None, relu=True):
    with Scope(nc, name) as sc:
        w = sc.sb("w", [P, HALF, D])
        b = sc.sb("b", [P, D])
        agg = sc.sb("agg", [P, SLOTS, HALF, P])
        y = sc.sb("y", [P, SLOTS, D])
        ps = sc.ps("ps", [P, SLOTS, 512])
        norm = Norm(sc) if residual is not None else None
        x = sc.sb("x", [P, SLOTS, D]) if norm else None
        loaded, stored = sc.sems("loaded", SLOTS), sc.sems("stored", SLOTS)
        consts, multiplied, biased, activated, ready, tick = (
            sc.sem(n) for n in ("consts", "multiplied", "biased", "activated", "ready", "tick"))
        block = sc.block()
        dinv = lambda i, k: keep["dinv"][:, bass.ds(i * SLOTS + k, 1)]
        loads = [(lambda k: agg[:, k, :, :], agg_tiles(io))]
        if norm:
            loads.append((lambda k: x[:, k, :], tile_rows(residual)))

        @block.sync
        def _(sp):
            sp.dma_start(w[:, :, :], weight.rearrange("(h p) n -> p h n", p=P)).then_inc(consts, 16)
            sp.dma_start(b[:, :], bias).then_inc(consts, 16)
            load_slots(sp, loads, loaded, stored, 1)

        @block.tensor
        def _(pe):
            pe.wait_ge(consts, 32)
            with pe.Fori(0, ROUNDS) as i:
                for k in range(SLOTS):
                    pe.wait_ge(loaded[k], i * (16 * len(loads)) + 16 * len(loads))
                    pe.sem_inc(tick, 1)
                    for h in range(HALF):
                        last = nc.tensor.matmul(ps[:, k, 0:D], agg[:, k, h, :], w[:, h, :], start=(h == 0),
                                                stop=(h == HALF - 1))
                    last.then_inc(multiplied, 1)

        @block.vector
        def _(dve):
            dve.wait_ge(consts, 32)
            with dve.Fori(0, ROUNDS) as i:
                each(dve, i, [multiplied], lambda k: nc.vector.scalar_tensor_tensor(
                    y[:, k, :], ps[:, k, 0:D], dinv(i, k), b[:, :], ALU.mult, ALU.add), biased)
                if norm is None:
                    each(dve, i, [biased], lambda k: nc.vector.tensor_scalar(
                        y[:, k, :], y[:, k, :], 0.0, dinv(i, k), ALU.max, ALU.mult), ready)
                else:
                    if relu:
                        each(dve, i, [biased], lambda k: nc.vector.scalar_tensor_tensor(
                            y[:, k, :], y[:, k, :], 0.0, x[:, k, :], ALU.max, ALU.add), activated)
                    else:
                        each(dve, i, [biased], lambda k: nc.vector.tensor_tensor(
                            y[:, k, :], y[:, k, :], x[:, k, :], ALU.add), activated)
                    norm.on_vector(nc, dve, i, lambda k: y[:, k, :], activated, lambda k: y[:, k, :], ready)

        @block.gpsimd
        def _(pool):
            stores = [(tile_rows(dest), lambda k: y[:, k, :])]
            if norm:
                norm_and_store(nc, pool, norm, stores, ready, stored, tick)
            else:
                store_slots(pool, stores, ready, stored, tick)


def gru_update(nc, io, keep):
    PS = 3
    with Scope(nc, "gru") as sc:
        w_in = sc.sb("w_in", [P, HALF, 3 * D])
        w_hid = sc.sb("w_hid", [P, HALF, 3 * D])
        b_in = sc.sb("b_in", [P, 3 * D])
        b_hid = sc.sb("b_hid", [P, 3 * D])
        gate_bias = sc.sb("gate_bias", [P, 4 * D])
        agg = sc.sb("agg", [P, SLOTS, HALF, P])
        x = sc.sb("x", [P, SLOTS, D])
        x_t = sc.sb("x_t", [P, SLOTS, HALF, P])
        gates = sc.sb("gates", [P, SLOTS, 2 * D])
        y = sc.sb("y", [P, SLOTS, D])
        turned_ps = sc.ps("turned_ps", [P, 2, 512])
        ps = sc.ps("ps", [P, PS, 2, 512])
        norm = Norm(sc)
        loaded, stored = sc.sems("loaded", SLOTS), sc.sems("stored", SLOTS)
        (consts, turned, x_ready, multiplied, taken, new_taken, gated, reset, summed, tanned, kept, mixed, grown,
         added, ready, tick, own_sem) = (sc.sem(n) for n in (
             "consts", "turned", "x_ready", "multiplied", "taken", "new_taken", "gated", "reset", "summed",
             "tanned", "kept", "mixed", "grown", "added", "ready", "tick", "own"))
        news = sc.sb("news", [P, SLOTS, 2 * D])
        block = sc.block()
        loads = [(lambda k: agg[:, k, :, :], agg_tiles(io)), (lambda k: x[:, k, :], tile_rows(io["x1"]))]

        @block.sync
        def _(sp):
            for to, source in ((w_in, io["w_in"]), (w_hid, io["w_hid"])):
                sp.dma_start(to[:, :, :], source.rearrange("(h p) n -> p h n", p=P)).then_inc(consts, 16)
            sp.dma_start(b_in[:, :], io["b_in"]).then_inc(consts, 16)
            sp.dma_start(b_hid[:, :], io["b_hid"]).then_inc(consts, 16)
            load_slots(sp, loads, loaded, stored, 1)

        @block.tensor
        def _(pe):
            pe.wait_ge(consts, 64)
            with pe.Fori(0, ROUNDS) as i:
                for k in range(SLOTS):
                    pe.wait_ge(loaded[k], i * 32 + 32)
                    pe.sem_inc(tick, 1)
                    pe.wait_ge(x_ready, i * SLOTS + k + (2 if k == 0 else 1))
                    pe.sem_inc(tick, 1)
                    for h in range(HALF):
                        last = nc.tensor.transpose(turned_ps[:, k % 2, h * P:(h + 1) * P],
                                                   x[:, k, h * P:(h + 1) * P], keep["ident"][:, :])
                    last.then_inc(turned, 1)
                    back = PS if k >= PS else (SLOTS if k >= SLOTS - PS else SLOTS - PS)
                    pe.wait_ge(new_taken, i * SLOTS + k + 1 + SLOTS - back)
                    pe.sem_inc(tick, 1)
                    pe.wait_ge(x_ready, i * SLOTS + k + 3)
                    pe.sem_inc(tick, 1)
                    operands = [(agg, w_in, 0), (agg, w_in, 1), (x_t, w_hid, 0), (x_t, w_hid, 1)]
                    for n, (a, w, h) in enumerate(operands):
                        nc.tensor.matmul(ps[:, k % PS, 0, 0:2 * D], a[:, k, h, :], w[:, h, 0:2 * D],
                                         start=(n == 0), stop=(n == 3))
                    for n, (a, w, h) in enumerate(operands):
                        at = (n // 2) * D
                        last = nc.tensor.matmul(ps[:, k % PS, 1, at:at + D], a[:, k, h, :], w[:, h, 2 * D:3 * D],
                                                start=(h == 0), stop=(h == 1))
                    last.then_inc(multiplied, 1)

        @block.scalar
        def _(act):
            act.sem_inc(x_ready, 2)
            with act.Fori(0, ROUNDS) as i:
                each(act, i, [turned], lambda k: nc.scalar.activation(
                    x_t[:, k, :, :].rearrange("p h n -> p (h n)"), turned_ps[:, k % 2, 0:D], ACT.Copy), x_ready)
                each(act, i, [taken], lambda k: nc.scalar.activation(gates[:, k, :], gates[:, k, :], ACT.Sigmoid), gated)
                each(act, i, [summed], lambda k: nc.scalar.activation(news[:, k, 0:D], news[:, k, 0:D], ACT.Tanh), tanned)

        @block.vector
        def _(dve):
            own = Chain(dve, own_sem)
            dve.sem_inc(new_taken, SLOTS)
            dve.wait_ge(consts, 64)
            own(nc.vector.tensor_tensor(gate_bias[:, 0:2 * D], b_in[:, 0:2 * D], b_hid[:, 0:2 * D], ALU.add))
            own(nc.vector.tensor_copy(gate_bias[:, 2 * D:3 * D], b_in[:, 2 * D:3 * D]))
            own(nc.vector.tensor_copy(gate_bias[:, 3 * D:4 * D], b_hid[:, 2 * D:3 * D]))
            with dve.Fori(0, ROUNDS) as i:
                for k in range(SLOTS):
                    dve.wait_ge(multiplied, i * SLOTS + k + 1)
                    nc.vector.tensor_tensor(gates[:, k, :], ps[:, k % PS, 0, :], gate_bias[:, 0:2 * D],
                                            ALU.add).then_inc(taken, 1)
                    nc.vector.tensor_tensor(news[:, k, :], ps[:, k % PS, 1, :], gate_bias[:, 2 * D:4 * D],
                                            ALU.add).then_inc(new_taken, 1)
                dve.wait_ge(new_taken, i * SLOTS + 2 * SLOTS)
                each(dve, i, [gated], lambda k: nc.vector.tensor_tensor(
                    news[:, k, D:2 * D], news[:, k, D:2 * D], gates[:, k, 0:D], ALU.mult), reset)
                each(dve, i, [reset], lambda k: nc.vector.tensor_tensor(
                    news[:, k, 0:D], news[:, k, 0:D], news[:, k, D:2 * D], ALU.add), summed)
                each(dve, i, [tanned], lambda k: nc.vector.tensor_tensor(
                    y[:, k, :], x[:, k, :], news[:, k, 0:D], ALU.subtract), kept)
                each(dve, i, [kept], lambda k: nc.vector.tensor_tensor(
                    y[:, k, :], y[:, k, :], gates[:, k, D:2 * D], ALU.mult), mixed)
                each(dve, i, [mixed], lambda k: nc.vector.tensor_tensor(
                    y[:, k, :], y[:, k, :], news[:, k, 0:D], ALU.add), grown)
                each(dve, i, [grown], lambda k: nc.vector.tensor_tensor(
                    y[:, k, :], y[:, k, :], x[:, k, :], ALU.add), added)
                norm.on_vector(nc, dve, i, lambda k: y[:, k, :], added, lambda k: y[:, k, :], ready)

        @block.gpsimd
        def _(pool):
            norm_and_store(nc, pool, norm, [(tile_rows(io["x2"]), lambda k: y[:, k, :])], ready, stored, tick)


def attention_inputs(nc, io, keep):
    with Scope(nc, "qkv") as sc:
        w = sc.sb("w", [P, HALF, 3 * D])
        b = sc.sb("b", [P, 3 * D])
        gain = sc.sb("gain", [P, D])
        shift = sc.sb("shift", [P, D])
        x = sc.sb("x", [P, SLOTS, D])
        x_t = sc.sb("x_t", [P, SLOTS, HALF, P])
        y = sc.sb("y", [P, SLOTS, 3 * D])
        turned_ps = sc.ps("turned_ps", [P, 2, 512])
        ps = sc.ps("ps", [P, 3, 2, 512])
        norm = Norm(sc)
        loaded, stored = sc.sems("loaded", SLOTS), sc.sems("stored", SLOTS)
        consts, normed, gained, shifted, turned, x_ready, multiplied, q_taken, ready, tick = (
            sc.sem(n) for n in ("consts", "normed", "gained", "shifted", "turned", "x_ready", "multiplied", "q_taken",
                                "ready", "tick"))
        block = sc.block()
        PS = 3

        @block.sync
        def _(sp):
            sp.dma_start(w[:, :, :], io["w_qkv"].rearrange("(h p) n -> p h n", p=P)).then_inc(consts, 16)
            sp.dma_start(b[:, :], io["b_qkv"]).then_inc(consts, 16)
            sp.dma_start(gain[:, :], io["ln_g"]).then_inc(consts, 16)
            sp.dma_start(shift[:, :], io["ln_b"]).then_inc(consts, 16)
            load_slots(sp, [(lambda k: x[:, k, :], tile_rows(io["x2"]))], loaded, stored, 2)

        @block.vector
        def _(dve):
            dve.sem_inc(ready, SLOTS)
            dve.wait_ge(consts, 64)
            with dve.Fori(0, ROUNDS) as i:
                for k in range(SLOTS):
                    dve.wait_ge(loaded[k], i * 16 + 16)
                    nc.vector.bn_stats(norm.stats[:, k, :], x[:, k, :]).then_inc(norm.stat_done, 1)
                each(dve, i, [norm.stat_done], lambda k: nc.vector.bn_aggr(
                    norm.mean_var[:, k, :], norm.stats[:, k, :]), norm.mean_done, norm.tick)
                each(dve, i, [norm.mean_done], lambda k: nc.vector.tensor_scalar(
                    norm.spread[:, k:k + 1], norm.mean_var[:, k, 1:2], LN_EPS, None, ALU.add), norm.spread_done)
                each(dve, i, [norm.inverse_done], lambda k: nc.vector.tensor_scalar(
                    x[:, k, :], x[:, k, :], norm.mean_var[:, k, 0:1], norm.inverse[:, k:k + 1], ALU.subtract,
                    ALU.mult), normed)
                each(dve, i, [normed], lambda k: nc.vector.tensor_tensor(
                    x[:, k, :], x[:, k, :], gain[:, :], ALU.mult), gained)
                each(dve, i, [gained], lambda k: nc.vector.tensor_tensor(
                    x[:, k, :], x[:, k, :], shift[:, :], ALU.add), shifted)
                for k in range(SLOTS):
                    dve.wait_ge(multiplied, i * SLOTS + k + 1)
                    nc.vector.tensor_tensor(y[:, k, 0:D], ps[:, k % PS, 0, 0:D], b[:, 0:D], ALU.add)
                    nc.vector.tensor_tensor(y[:, k, D:3 * D], ps[:, k % PS, 1, :], b[:, D:3 * D],
                                            ALU.add).then_inc(ready, 1)

        @block.tensor
        def _(pe):
            with pe.Fori(0, ROUNDS) as i:
                for k in range(SLOTS):
                    pe.wait_ge(shifted, i * SLOTS + k + 1)
                    pe.sem_inc(tick, 1)
                    pe.wait_ge(x_ready, i * SLOTS + k + (2 if k == 0 else 1))
                    pe.sem_inc(tick, 1)
                    for h in range(HALF):
                        last = nc.tensor.transpose(turned_ps[:, k % 2, h * P:(h + 1) * P],
                                                   x[:, k, h * P:(h + 1) * P], keep["ident"][:, :])
                    last.then_inc(turned, 1)
                    back = PS if k >= PS else (SLOTS if k >= SLOTS - PS else SLOTS - PS)
                    pe.wait_ge(ready, i * SLOTS + k + 1 + SLOTS - back)
                    pe.sem_inc(tick, 1)
                    pe.wait_ge(x_ready, i * SLOTS + k + 3)
                    pe.sem_inc(tick, 1)
                    for h in range(HALF):
                        nc.tensor.matmul(ps[:, k % PS, 0, 0:D], x_t[:, k, h, :], w[:, h, 0:D], start=(h == 0),
                                         stop=(h == 1))
                    for h in range(HALF):
                        last = nc.tensor.matmul(ps[:, k % PS, 1, :], x_t[:, k, h, :], w[:, h, D:3 * D],
                                                start=(h == 0), stop=(h == 1))
                    last.then_inc(multiplied, 1)

        @block.scalar
        def _(act):
            act.sem_inc(x_ready, 2)
            act.wait_ge(consts, 64)
            with act.Fori(0, ROUNDS) as i:
                each(act, i, [turned], lambda k: nc.scalar.activation(
                    x_t[:, k, :, :].rearrange("p h n -> p (h n)"), turned_ps[:, k % 2, 0:D], ACT.Copy), x_ready)

        @block.gpsimd
        def _(pool):
            norm.set_power(nc, pool)
            with pool.Fori(0, ROUNDS) as i:
                norm.on_pool(nc, pool, i)
                for k in range(SLOTS):
                    pool.wait_ge(ready, i * SLOTS + k + 1 + SLOTS)
                    pool.sem_inc(tick, 1)
                    pool.dma_start(io["q"][bass.ds((i * SLOTS + k) * P, P), :], y[:, k, 0:D]).then_inc(stored[k], 16)
                    pool.dma_start(io["kv"][bass.ds((i * SLOTS + k) * P, P), :], y[:, k, D:3 * D]).then_inc(stored[k], 16)
            for k in range(SLOTS):
                pool.wait_ge(stored[k], 32 * ROUNDS)


def attention_edges(nc, io, keep):
    G = 4
    with Scope(nc, "edges") as outer:
        dst_place = outer.sb("dst_place", [P, EDGE_STEPS])
        cutoff = outer.sb("cutoff", [P, EDGE_STEPS])
        src_row = outer.sb("src_row", [P, EDGE_STEPS], I32)
        dst_row = outer.sb("dst_row", [P, EDGE_STEPS], I32)
        column = outer.sb("column", [1, EDGE_STEPS], I32)
        window = outer.sb("window", [1, EDGE_STEPS], I32)

        def kept(sc, dve, own, cols, step_no, width):
            src, dst, tile, weight = (c[0] for c in cols)
            under = sc.sb("under", [P, width])
            own(nc.vector.tensor_copy(src_row[:, :], src))
            own(nc.vector.tensor_scalar(dst_row[:, :], dst, float(NODES - 1), None, ALU.min))
            own(nc.vector.tensor_scalar(column[0:1, :], tile[0:1, :], float(P), None, ALU.mult))
            own(nc.vector.tensor_tensor(cutoff[:, :], step_no[:, :], tile, ALU.subtract))
            own(nc.vector.tensor_copy(window[0:1, :], cutoff[0:1, :]))
            own(nc.vector.scalar_tensor_tensor(dst_place[:, :], cutoff[:, :], -float(P), dst, ALU.mult, ALU.add))
            own(nc.vector.tensor_scalar(under[:, :], weight, 5.0, None, ALU.is_lt))
            own(nc.vector.tensor_scalar(cutoff[:, :], weight, 5.0, 0.0, ALU.min, ALU.max))
            own(nc.vector.tensor_scalar(cutoff[:, :], cutoff[:, :], -float(np.pi) / 5.0, float(np.pi) / 2.0,
                                        ALU.mult, ALU.add))
            nc.vector.nop().then_inc(angle, 1)
            dve.wait_ge(sine, 1)
            own(nc.vector.tensor_scalar(cutoff[:, :], cutoff[:, :], 0.5, 0.5, ALU.mult, ALU.add))
            own(nc.vector.tensor_tensor(cutoff[:, :], cutoff[:, :], under[:, :], ALU.mult))

        angle, sine = outer.sem("angle"), outer.sem("sine")

        def sine_on_scalar(block):
            @block.scalar
            def _(act):
                act.wait_ge(angle, 1)
                nc.scalar.activation(cutoff[:, :], cutoff[:, :], ACT.Sin).then_inc(sine, 1)

        staircase_steps(nc, "esteps", io, P, EDGE_STEPS, kept, sine_on_scalar)

        with Scope(nc, "edge") as sc:
            w = sc.sb("w", [ATTR + 1, 2 * D])
            place_no = sc.sb("place_no", [P, P])
            total = sc.sb("total", [P, NODE_TILES, D])
            attr = sc.sb("attr", [ATTR + 1, 2 * G, P])
            q = sc.sb("q", [P, 2 * G, D])
            kv = sc.sb("kv", [P, 2 * G, 2 * D])
            src_now = sc.sb("src_now", [P, 2 * G], I32)
            dst_now = sc.sb("dst_now", [P, 2 * G], I32)
            d_kv = sc.sb("d_kv", [P, 2 * G, 2 * D])
            hot = sc.sb("hot", [P, 2 * G, P])
            prod = sc.sb("prod", [P, 2 * G, D])
            message = sc.sb("message", [P, 2 * G, D])
            score = sc.sb("score", [P, 2 * G])
            attn = sc.sb("attn", [P, 2 * G])
            ps_d = sc.ps("ps_d", [P, 4, 512])
            ps_m = sc.ps("ps_m", [P, 4, 512])
            gathered, attr_in = sc.sems("gathered", 2 * G), sc.sems("attr_in", 2 * G)
            (consts, set_up, copied, multiplied, activated, hots, paired, scored, weighted, messaged, scattered, added,
             stored, tick) = (sc.sem(n) for n in (
                 "consts", "set_up", "copied", "multiplied", "activated", "hots", "paired", "scored", "weighted",
                 "messaged", "scattered", "added", "stored", "tick"))
            block = sc.block()
            U = 2 * G

            def load_attr(sp, k, at):
                t = sp.value_load(column[0:1, at], min_val=0, max_val=EDGES_P - P)
                sp.dma_start(attr[:, k, :], io["attr_t"][:, bass.ds(t, P)]).then_inc(attr_in[k], 16)

            @block.sync
            def _(sp):
                sp.dma_start(w[:, :], io["w_dkv"]).then_inc(consts, 16)
                for k in range(U):
                    load_attr(sp, k, slice(k, k + 1))
                with sp.Fori(1, EDGE_STEPS // U) as i:
                    for k in range(U):
                        sp.wait_ge(multiplied, i * U + k + 1 - U)
                        sp.sem_inc(tick, 1)
                        load_attr(sp, k, bass.ds(i * U + k, 1))
                sp.wait_ge(added, EDGE_STEPS + U)
                sp.dma_start(io["edge_sum"].rearrange("(t p) f -> p t f", p=P), total[:, :, :]).then_inc(stored, 16)
                sp.wait_ge(stored, 16)

            @block.gpsimd
            def _(pool):
                nc.gpsimd.iota(place_no[:, :], pattern=[[1, P]], base=0, channel_multiplier=0,
                               allow_small_or_imprecise_dtypes=True).then_inc(set_up, 1)
                nc.gpsimd.memset(total[:, :, :], 0.0).then_inc(set_up, 1)
                with pool.Fori(0, EDGE_STEPS // U) as i:
                    for n in range(2):
                        pool.wait_ge(messaged, i * U + n * G + G)
                        pool.sem_inc(tick, 1)
                        nc.gpsimd.tensor_copy(src_now[:, n * G:n * G + G], src_row[:, bass.ds(i * U + n * G, G)])
                        nc.gpsimd.tensor_copy(dst_now[:, n * G:n * G + G],
                                              dst_row[:, bass.ds(i * U + n * G, G)]).then_inc(copied, 1)
                        pool.wait_ge(copied, i * 2 + n + 1)
                        pool.sem_inc(tick, 1)
                        for k in range(n * G, n * G + G):
                            nc.gpsimd.indirect_dma_start(
                                q[:, k, :], None, io["q"], bass.IndirectOffsetOnAxis(ap=dst_now[:, k:k + 1], axis=0),
                                bounds_check=NODES_P - 1).then_inc(gathered[k], 16)
                            nc.gpsimd.indirect_dma_start(
                                kv[:, k, :], None, io["kv"], bass.IndirectOffsetOnAxis(ap=src_now[:, k:k + 1], axis=0),
                                bounds_check=NODES_P - 1).then_inc(gathered[k], 16)

            @block.tensor
            def _(pe):
                pe.wait_ge(consts, 16)
                with pe.Fori(0, EDGE_STEPS // U) as i:
                    for n in range(2):
                        for k in range(n * G, n * G + G):
                            pe.wait_ge(attr_in[k], i * 16 + 16)
                            pe.sem_inc(tick, 1)
                            pe.wait_ge(activated, i * U + k + 1 + U - 4)
                            pe.sem_inc(tick, 1)
                            nc.tensor.matmul(ps_d[:, k % 4, :], attr[:, k, :], w[:, :], start=True,
                                             stop=True).then_inc(multiplied, 1)
                        for k in range(n * G, n * G + G):
                            pe.wait_ge(added, i * U + k + 1 + U - 4)
                            pe.sem_inc(tick, 1)
                            pe.wait_ge(messaged, i * U + k + 1 + U)
                            pe.sem_inc(tick, 1)
                            nc.tensor.matmul(ps_m[:, k % 4, 0:D], hot[:, k, :], message[:, k, :], start=True,
                                             stop=True).then_inc(scattered, 1)

            @block.scalar
            def _(act):
                act.sem_inc(activated, U)
                with act.Fori(0, EDGE_STEPS // U) as i:
                    for n in range(2):
                        for k in range(n * G, n * G + G):
                            act.wait_ge(messaged, i * U + k + 1)
                            act.sem_inc(tick, 1)
                            act.wait_ge(multiplied, i * U + k + 1)
                            nc.scalar.activation(d_kv[:, k, :], ps_d[:, k % 4, :], ACT.Silu).then_inc(activated, 1)
                        for k in range(n * G, n * G + G):
                            act.wait_ge(scored, i * U + k + 1)
                            nc.scalar.activation(attn[:, k:k + 1], score[:, k:k + 1], ACT.Silu).then_inc(weighted, 1)

            @block.vector
            def _(dve):
                dve.sem_inc(messaged, U)
                dve.sem_inc(added, U)
                dve.wait_ge(set_up, 2)
                with dve.Fori(0, EDGE_STEPS // U) as i:
                    for n in range(2):
                        ks = range(n * G, n * G + G)
                        for k in ks:
                            dve.wait_ge(added, i * U + k + 1)
                            nc.vector.tensor_scalar(hot[:, k, :], place_no[:, :], dst_place[:, bass.ds(i * U + k, 1)],
                                                    cutoff[:, bass.ds(i * U + k, 1)], ALU.is_equal, ALU.mult)
                            dve.wait_ge(gathered[k], i * 32 + 32)
                            nc.vector.tensor_tensor(prod[:, k, :], q[:, k, :], kv[:, k, 0:D], ALU.mult).then_inc(paired, 1)
                        for k in ks:
                            dve.wait_ge(paired, i * U + k + 1)
                            dve.wait_ge(activated, i * U + k + 1 + U)
                            nc.vector.scalar_tensor_tensor(prod[:, k, :], prod[:, k, :], 1.0, d_kv[:, k, 0:D], ALU.mult,
                                                           ALU.mult, accum_out=score[:, k:k + 1]).then_inc(scored, 1)
                        for k in ks:
                            dve.wait_ge(weighted, i * U + k + 1)
                            nc.vector.scalar_tensor_tensor(message[:, k, :], kv[:, k, D:2 * D], attn[:, k:k + 1],
                                                           d_kv[:, k, D:2 * D], ALU.mult, ALU.mult).then_inc(messaged, 1)
                        for k in ks:
                            at = dve.value_load(window[0:1, bass.ds(i * U + k, 1)], min_val=0, max_val=NODE_TILES - 1)
                            acc = total[:, bass.ds(at, 1), :].rearrange("p a f -> p (a f)")
                            dve.wait_ge(scattered, i * U + k + 1)
                            dve.wait_ge(added, i * U + k + U)
                            nc.vector.tensor_tensor(acc, acc, ps_m[:, k % 4, 0:D], ALU.add).then_inc(added, 1)


def attention_update(nc, io, keep):
    with Scope(nc, "attn") as sc:
        w = sc.sb("w", [P, HALF, D])
        b = sc.sb("b", [P, D])
        s = sc.sb("s", [P, SLOTS, D])
        x = sc.sb("x", [P, SLOTS, D])
        s_t = sc.sb("s_t", [P, SLOTS, HALF, P])
        y = sc.sb("y", [P, SLOTS, D])
        turned_ps = sc.ps("turned_ps", [P, 2, 512])
        ps = sc.ps("ps", [P, SLOTS, 512])
        norm = Norm(sc)
        loaded, stored = sc.sems("loaded", SLOTS), sc.sems("stored", SLOTS)
        consts, turned, s_ready, multiplied, biased, added, ready, tick = (
            sc.sem(n) for n in ("consts", "turned", "s_ready", "multiplied", "biased", "added", "ready", "tick"))
        block = sc.block()

        @block.sync
        def _(sp):
            sp.dma_start(w[:, :, :], io["w_out"].rearrange("(h p) n -> p h n", p=P)).then_inc(consts, 16)
            sp.dma_start(b[:, :], io["b_out"]).then_inc(consts, 16)
            load_slots(sp, [(lambda k: s[:, k, :], tile_rows(io["edge_sum"])),
                            (lambda k: x[:, k, :], tile_rows(io["x2"]))], loaded, stored, 1)

        @block.tensor
        def _(pe):
            pe.wait_ge(consts, 32)
            with pe.Fori(0, ROUNDS) as i:
                for k in range(SLOTS):
                    pe.wait_ge(loaded[k], i * 32 + 32)
                    pe.sem_inc(tick, 1)
                    pe.wait_ge(s_ready, i * SLOTS + k + (2 if k == 0 else 1))
                    pe.sem_inc(tick, 1)
                    for h in range(HALF):
                        last = nc.tensor.transpose(turned_ps[:, k % 2, h * P:(h + 1) * P],
                                                   s[:, k, h * P:(h + 1) * P], keep["ident"][:, :])
                    last.then_inc(turned, 1)
                    pe.wait_ge(s_ready, i * SLOTS + k + 3)
                    pe.sem_inc(tick, 1)
                    for h in range(HALF):
                        last = nc.tensor.matmul(ps[:, k, 0:D], s_t[:, k, h, :], w[:, h, :], start=(h == 0), stop=(h == 1))
                    last.then_inc(multiplied, 1)

        @block.scalar
        def _(act):
            act.sem_inc(s_ready, 2)
            with act.Fori(0, ROUNDS) as i:
                each(act, i, [turned], lambda k: nc.scalar.activation(
                    s_t[:, k, :, :].rearrange("p h n -> p (h n)"), turned_ps[:, k % 2, 0:D], ACT.Copy), s_ready)

        @block.vector
        def _(dve):
            dve.wait_ge(consts, 32)
            with dve.Fori(0, ROUNDS) as i:
                each(dve, i, [multiplied], lambda k: nc.vector.tensor_tensor(
                    y[:, k, :], ps[:, k, 0:D], b[:, :], ALU.add), biased)
                each(dve, i, [biased], lambda k: nc.vector.scalar_tensor_tensor(
                    y[:, k, :], x[:, k, :], 2.0, y[:, k, :], ALU.mult, ALU.add), added)
                norm.on_vector(nc, dve, i, lambda k: y[:, k, :], added, lambda k: y[:, k, :], ready)

        @block.gpsimd
        def _(pool):
            norm_and_store(nc, pool, norm, [(tile_rows(io["x3"]), lambda k: y[:, k, :])], ready, stored, tick)


def program(nc, io):
    with Scope(nc, "all") as sc:
        keep = {
            "dinv": sc.sb("dinv", [P, NODE_TILES]),
            "ident": sc.sb("ident", [P, P]),
            "iota": sc.sb("iota", [P, NODE_TILES * RELS], F16),
        }
        with Scope(nc, "first") as held:
            keep["adj"] = held.sb("adj", [P, NODE_TILES, NODES_P], F16)
            with Scope(nc, "steps") as st:
                keep["cells"] = st.sb("cells", [P, BUILD_STEPS + 8, 2])
                keep["window"] = st.sb("window", [1, BUILD_STEPS], I32)
                build_steps(nc, io, keep)
                histogram(nc, io, keep)
                build_matrix(nc, io, keep)
            aggregate(nc, io, keep, "agg0", io["x"], scaled=True, save=True)
            gcn_update(nc, io, keep, "gcn0", io["w1"], io["b1"], io["z1"])
            aggregate(nc, io, keep, "agg1", io["z1"])
            gcn_update(nc, io, keep, "gcn1", io["w2"], io["b2"], io["x1"], residual=io["x"])
            aggregate(nc, io, keep, "agg2", io["x1"], relations=True)
        gru_update(nc, io, keep)
        attention_inputs(nc, io, keep)
        attention_edges(nc, io, keep)
        attention_update(nc, io, keep)
        with Scope(nc, "second") as held:
            keep["adj"] = held.sb("adj", [P, NODE_TILES, NODES_P], F16)
            aggregate(nc, io, keep, "agg3", io["x3"], scaled=True, load=True)
        gcn_update(nc, io, keep, "gcn3", io["w3"], io["b3"], io["out"], residual=io["x3"], relu=False)


def kernel(**inputs):
    import concourse.bacc as bacc
    from concourse.bass_utils import run_bass_kernel_spmd

    a = {k: np.asarray(v) for k, v in inputs.items()}
    nc = bacc.Bacc("TRN2", target_bir_lowering=False, num_devices=1)
    arrays, io = {}, {}

    def give(name, array):
        array = np.ascontiguousarray(array)
        arrays[name] = array
        io[name] = nc.dram_tensor(name, list(array.shape), mybir.dt.from_np(array.dtype), kind="ExternalInput").ap()

    def edges(v, fill):
        return np.concatenate([v, np.full(EDGES_P - EDGES, fill, v.dtype)]).reshape(EDGE_TILES, P)

    src, dst = edges(a["src"], 0), edges(a["dst"], NO_NODE)
    give("src_t", src)
    give("dst_t", dst)
    give("next_t", np.concatenate([dst[1:, 0], np.full(1, NO_NODE, dst.dtype)]))
    give("wts_t", edges(a["edge_weight"], 0))
    give("dst_p", dst.T)
    give("rel_p", edges(a["edge_type_16"], 0).T)

    def scratch(name, shape, dt=F32, kind="Internal"):
        io[name] = nc.dram_tensor(name, list(shape), dt, kind=kind).ap()

    def nodes(v):
        return np.concatenate([v, np.zeros((NODES_P - NODES, D), v.dtype)])

    def rows(v):
        return np.broadcast_to(v.reshape(1, -1), (P, v.size))

    give("x", nodes(a["x"]))
    give("attr_t", np.concatenate([np.concatenate([a["edge_attr_64"].T, np.zeros((ATTR, EDGES_P - EDGES), np.float32)], 1),
                                   np.ones((1, EDGES_P), np.float32)]))
    give("w_dkv", np.concatenate([
        np.concatenate([a["L2_gnn_Wdk"].T, a["L2_gnn_Wdv"].T], 1),
        np.concatenate([a["L2_gnn_bdk"], a["L2_gnn_bdv"]])[None]]))
    give("relvectors", a["L1_gnn_relvectors"])
    give("w1", a["L0_gnn_W1"])
    give("b1", rows(a["L0_gnn_b1"]))
    give("w2", a["L0_gnn_W2"])
    give("b2", rows(a["L0_gnn_b2"]))
    give("w3", a["L3_gnn_W"].T)
    give("b3", rows(a["L3_gnn_b"]))
    give("w_in", a["L1_gnn_w_ih"].T)
    give("b_in", rows(a["L1_gnn_b_ih"]))
    give("w_hid", a["L1_gnn_w_hh"].T)
    give("b_hid", rows(a["L1_gnn_b_hh"]))
    give("w_qkv", np.concatenate([a["L2_gnn_Wq"].T, a["L2_gnn_Wk"].T, a["L2_gnn_Wv"].T], 1))
    give("b_qkv", rows(np.concatenate([a["L2_gnn_bq"], a["L2_gnn_bk"], a["L2_gnn_bv"]])))
    give("w_out", a["L2_gnn_Wo"].T)
    give("b_out", rows(a["L2_gnn_bo"]))
    give("ln_g", rows(a["L2_gnn_ln_g"]))
    give("ln_b", rows(a["L2_gnn_ln_b"]))

    scratch("rel_counts", [RELS, NODES_P])
    scratch("adj_copy", [P, NODE_TILES, NODES_P], F16)
    scratch("agg_t", [HALF, P, NODES_P])
    for name in ("z1", "x1", "x2", "x3", "q", "edge_sum"):
        scratch(name, [NODES_P, D])
    scratch("kv", [NODES_P, 2 * D])
    scratch("out", [NODES_P, D], kind="ExternalOutput")
    program(nc, io)
    r = run_bass_kernel_spmd(nc, [arrays], core_ids=[0])
    return r.results[0]["out"][0:NODES]
```

```python
from contextlib import ExitStack

import numpy as np

import concourse.bass as bass
import concourse.mybir as mybir

F32 = mybir.dt.float32
F16 = mybir.dt.float16
BF16 = mybir.dt.bfloat16
I32 = mybir.dt.int32
ALU = mybir.AluOpType
ACT = mybir.ActivationFunctionType
AX = mybir.AxisListType

P = 128
NODES = 3125
EDGES = 53125
D = 256
HALF = D // P
ATTR = 64
RELS = 16
NODE_TILES = -(-NODES // P)
NODES_P = NODE_TILES * P
EDGE_TILES = -(-EDGES // P)
EDGES_P = EDGE_TILES * P
NO_NODE = 4095
SEL_J = 4
SEL_P = EDGE_TILES // SEL_J
BUILD_W = 8
BUILD_WINDOWS = NODES_P // BUILD_W
BUILD_STEPS = EDGE_TILES + BUILD_WINDOWS
EDGE_STEPS = EDGE_TILES + NODE_TILES - 1
CHUNK = 400
CHUNKS = NODES_P // CHUNK
LN_EPS = 1e-5
NORMED_SCALE = 1024.0


class Chain:

    def __init__(self, engine, sem):
        self.engine, self.sem, self.n = engine, sem, 0

    def __call__(self, instruction):
        self.n += 1
        instruction.then_inc(self.sem, 1)
        self.engine.wait_ge(self.sem, self.n)


class Scope:

    def __init__(self, nc, name):
        self.nc, self.name, self.stack, self.semaphores = nc, name, ExitStack(), []

    def __enter__(self):
        self.stack.__enter__()
        return self

    def __exit__(self, *a):
        self.stack.__exit__(*a)
        if self.semaphores:
            self.nc.clear_and_free_semaphores(self.semaphores)
            self.nc.all_engine_barrier()

    def sb(self, name, shape, dt=F32):
        return self.stack.enter_context(self.nc.sbuf_tensor(f"{self.name}_{name}", list(shape), dt))

    def ps(self, name, shape, dt=F32):
        return self.stack.enter_context(self.nc.psum_tensor(f"{self.name}_{name}", list(shape), dt))

    def sem(self, name):
        self.semaphores.append(self.nc.alloc_semaphore(name=f"{self.name}_{name}"))
        return self.semaphores[-1]

    def sems(self, name, n):
        return [self.sem(f"{name}{k}") for k in range(n)]

    def block(self):
        return self.stack.enter_context(self.nc.Block())


def staircase_steps(nc, name, io, window, steps, kept, more=None):
    shift = window.bit_length() - 1
    parts = -(-steps // 512)
    width = -(-steps // parts)
    with Scope(nc, name) as sc:
        src_i = sc.sb("src_i", [SEL_P, SEL_J, P], I32)
        dst_i = sc.sb("dst_i", [SEL_P, SEL_J, P], I32)
        next_i = sc.sb("next_i", [SEL_P, SEL_J], I32)
        first_i = sc.sb("first_i", [SEL_P, SEL_J], I32)
        wts = sc.sb("wts", [SEL_P, SEL_J, P])
        src_f = sc.sb("src_f", [SEL_P, SEL_J, P])
        dst_f = sc.sb("dst_f", [SEL_P, SEL_J, P])
        tile_f = sc.sb("tile_f", [SEL_P, SEL_J, P])
        starts = sc.sb("starts", [SEL_P, 2, SEL_J])
        step_no = sc.sb("step_no", [P, steps])
        after = sc.sb("after", [SEL_P, steps])
        select = sc.sb("select", [SEL_P, SEL_J, steps])
        sums = [sc.ps(f"sums{v}", [P, parts, 512]) for v in range(3 if parts > 1 else 4)]
        loaded, iotas, selected, picked, dve_own = (
            sc.sem(n) for n in ("loaded", "iotas", "selected", "picked", "dve_own"))
        values = [src_f, dst_f, tile_f, wts][:len(sums)]
        block = sc.block()
        if more is not None:
            more(block)

        @block.sync
        def _(sp):
            by_tile = lambda a: a.rearrange("(p j) e -> p j e", j=SEL_J)
            sp.dma_start(src_i[:, :, :], by_tile(io["src_t"][0:EDGE_TILES])).then_inc(loaded, 16)
            sp.dma_start(dst_i[:, :, :], by_tile(io["dst_t"][0:EDGE_TILES])).then_inc(loaded, 16)
            sp.dma_start(next_i[:, :], io["next_t"].rearrange("(p j) -> p j", j=SEL_J)).then_inc(loaded, 16)
            sp.dma_start(wts[:, :, :], by_tile(io["wts_t"][0:EDGE_TILES])).then_inc(loaded, 16)

        @block.gpsimd
        def _(pool):
            nc.gpsimd.iota(step_no[:, :], pattern=[[1, steps]], base=0, channel_multiplier=0,
                           allow_small_or_imprecise_dtypes=True).then_inc(iotas, 1)
            nc.gpsimd.iota(tile_f[:, :, :], pattern=[[1, SEL_J], [0, P]], base=0, channel_multiplier=SEL_J,
                           allow_small_or_imprecise_dtypes=True).then_inc(iotas, 1)

        @block.vector
        def _(dve):
            own = Chain(dve, dve_own)
            dve.wait_ge(loaded, 64)
            dve.wait_ge(iotas, 2)
            own(nc.vector.tensor_copy(first_i[:, :], dst_i[:, :, 0]))
            own(nc.vector.memset(first_i[0:1, 0:1], 0))
            own(nc.vector.tensor_scalar(first_i[:, :], first_i[:, :], shift, None, ALU.logical_shift_right))
            own(nc.vector.tensor_scalar(next_i[:, :], next_i[:, :], shift, None, ALU.logical_shift_right))
            own(nc.vector.tensor_tensor(starts[:, 0, :], first_i[:, :], tile_f[:, :, 0], ALU.add))
            own(nc.vector.scalar_tensor_tensor(starts[:, 1, :], next_i[:, :], 1.0, tile_f[:, :, 0],
                                               ALU.add, ALU.add))
            own(nc.vector.tensor_copy(src_f[:, :, :], src_i[:, :, :]))
            own(nc.vector.tensor_copy(dst_f[:, :, :], dst_i[:, :, :]))
            for j in range(SEL_J):
                own(nc.vector.tensor_scalar(after[:, :], step_no[0:SEL_P, :], starts[:, 1, j:j + 1], None,
                                            ALU.is_ge))
                last = nc.vector.scalar_tensor_tensor(select[:, j, :], step_no[0:SEL_P, :], starts[:, 0, j:j + 1],
                                                      after[:, :], ALU.is_ge, ALU.subtract)
                own(last)
            nc.vector.nop().then_inc(selected, 1)
            dve.wait_ge(picked, 1)
            kept(sc, dve, own, [[s[:, h, 0:width] for h in range(parts)] for s in sums], step_no, width)

        @block.tensor
        def _(pe):
            pe.wait_ge(selected, 1)
            for v, value in enumerate(values):
                for h in range(parts):
                    for j in range(SEL_J):
                        last = nc.tensor.matmul(sums[v][:, h, 0:width], value[:, j, :],
                                                select[:, j, h * width:(h + 1) * width],
                                                start=(j == 0), stop=(j == SEL_J - 1))
            last.then_inc(picked, 1)


def build_steps(nc, io, keep):

    def kept(sc, dve, own, cols, step_no, width):
        own(nc.vector.memset(keep["cells"][:, BUILD_STEPS:, :], -1.0))
        raw = sc.sb("raw", [P, width], I32)
        win = sc.sb("win", [P, width])
        col = sc.sb("col", [P, width])
        ok = sc.sb("ok", [P, width])
        ok2 = sc.sb("ok2", [P, width])
        for h, (src, dst, tile) in enumerate(zip(*cols)):
            at = slice(h * width, (h + 1) * width)
            own(nc.vector.tensor_copy(raw[:, :], src))
            own(nc.vector.tensor_scalar(raw[:, :], raw[:, :], P - 1, None, ALU.bitwise_and))
            own(nc.vector.tensor_copy(keep["cells"][:, at, 0], raw[:, :]))
            own(nc.vector.tensor_tensor(col[:, :], src, keep["cells"][:, at, 0], ALU.subtract))
            own(nc.vector.tensor_tensor(win[:, :], step_no[:, at], tile, ALU.subtract))
            own(nc.vector.tensor_scalar(keep["window"][0:1, at], win[0:1, :], float(BUILD_WINDOWS - 1),
                                        float(BUILD_W), ALU.min, ALU.mult))
            own(nc.vector.scalar_tensor_tensor(win[:, :], win[:, :], -float(BUILD_W), dst, ALU.mult, ALU.add))
            own(nc.vector.tensor_scalar(ok[:, :], win[:, :], 0.0, None, ALU.is_ge))
            own(nc.vector.scalar_tensor_tensor(ok2[:, :], win[:, :], float(BUILD_W), ok[:, :], ALU.is_lt,
                                               ALU.mult))
            own(nc.vector.scalar_tensor_tensor(col[:, :], col[:, :], BUILD_W / P, win[:, :], ALU.mult, ALU.add))
            own(nc.vector.scalar_tensor_tensor(col[:, :], col[:, :], 1.0, ok2[:, :], ALU.add, ALU.mult))
            own(nc.vector.tensor_scalar(keep["cells"][:, at, 1], col[:, :], 1.0, None, ALU.subtract))

    staircase_steps(nc, "bsteps", io, BUILD_W, BUILD_STEPS, kept)


class RowHots:

    def __init__(self, sc):
        self.hot = sc.sb("row_hot", [P, 16, P], F16)
        self.now = sc.sb("row_now", [P, 2, 8])
        self.distance = sc.sb("distance", [P, 2, 8, P], F16)
        self.copied, self.apart, self.ready, self.tick = (
            sc.sem(n) for n in ("row_copied", "row_apart", "row_ready", "row_tick"))

    def on_scalar(self, nc, act, keep, cells, steps, used, halves=2):
        act.sem_inc(self.ready, halves)
        with act.Fori(0, steps // 16) as i:
            for n in range(halves):
                act.wait_ge(self.ready, i * halves + n + 1)
                act.sem_inc(self.tick, 1)
                nc.scalar.activation(self.now[:, n, :], cells[:, bass.ds(i * 16 + n * 8, 8), 0],
                                     ACT.Copy).then_inc(self.copied, 1)
                act.wait_ge(self.copied, i * halves + n + 1)
                for k in range(8):
                    nc.scalar.activation(self.distance[:, n, k, :], keep["iota"][:, 0:P], ACT.Abs,
                                         bias=self.now[:, n, k:k + 1], scale=-1.0).then_inc(self.apart, 1)
                act.wait_ge(self.apart, i * (8 * halves) + n * 8 + 8)
                act.sem_inc(self.tick, 1)
                act.wait_ge(used, i * 16 + n * 8 + 8)
                nc.scalar.activation(self.hot[:, n * 8:n * 8 + 8, :].rearrange("p k e -> p (k e)"),
                                     self.distance[:, n, :, :].rearrange("p k e -> p (k e)"), ACT.Relu, bias=1.0,
                                     scale=-1.0).then_inc(self.ready, 1)


def histogram(nc, io, keep):
    GROUP = 8
    with Scope(nc, "hist") as sc:
        dst_i = sc.sb("dst_i", [P, EDGE_TILES], I32)
        rel_i = sc.sb("rel_i", [P, EDGE_TILES], I32)
        high = sc.sb("high", [P, EDGE_TILES])
        cells = sc.sb("cells", [P, EDGE_TILES + 16, 2])
        now = sc.sb("now", [P, 16, 2])
        root = sc.sb("root", [P, NODE_TILES])
        copied, celled = sc.sem("copied"), sc.sem("celled")
        rows = RowHots(sc)
        key_hot = sc.sb("key_hot", [P, GROUP, NODE_TILES * RELS], F16)
        counts = sc.sb("counts", [P, NODE_TILES * RELS])
        deg = sc.sb("deg", [P, NODE_TILES])
        rel_rows = sc.sb("rel_rows", [RELS, NODES_P])
        zero = sc.sb("zero", [P, NODE_TILES * RELS], F16)
        ps = sc.ps("counts_ps", [P, NODE_TILES * RELS])
        tr = sc.ps("rel_ps", [P, 2, 512])
        loaded, ready, used, dve_own, iotas, summed, counted, rooted, turned, moved, stored, zeroed, tick = (
            sc.sem(n) for n in ("loaded", "ready", "used", "dve_own", "iotas", "summed", "counted", "rooted",
                                "turned", "moved", "stored", "zeroed", "tick"))
        block = sc.block()
        groups = -(-NODE_TILES // 4)

        @block.sync
        def _(sp):
            sp.dma_start(dst_i[:, :], io["dst_p"]).then_inc(loaded, 16)
            sp.dma_start(rel_i[:, :], io["rel_p"]).then_inc(loaded, 16)
            sp.wait_ge(moved, groups)
            sp.dma_start(io["rel_counts"], rel_rows[:, :]).then_inc(stored, 16)
            sp.wait_ge(stored, 16)

        @block.gpsimd
        def _(pool):
            nc.gpsimd.iota(keep["iota"][:, :], pattern=[[1, NODE_TILES * RELS]], base=0, channel_multiplier=0,
                           allow_small_or_imprecise_dtypes=True).then_inc(iotas, 1)
            nc.gpsimd.memset(zero[:, :], 0.0).then_inc(zeroed, 1)
            nc.gpsimd.memset(keep["ident"][:, :], 0.0).then_inc(iotas, 1)
            pool.wait_ge(iotas, 2)
            nc.gpsimd.affine_select(out=keep["ident"][:, :], in_=keep["ident"][:, :], compare_op=ALU.not_equal,
                                    fill=1.0, base=0, pattern=[[-1, P]], channel_multiplier=1).then_inc(iotas, 1)
            for part in range(0, NODE_TILES, 5):
                nc.gpsimd.memset(keep["adj"][:, part:part + 5, :], 0.0).then_inc(zeroed, 1)

        @block.vector
        def _(dve):
            own = Chain(dve, dve_own)
            dve.wait_ge(loaded, 32)
            dve.wait_ge(iotas, 3)
            raw = high[:, :].bitcast(I32)
            low, key = cells[:, 0:EDGE_TILES, 0], cells[:, 0:EDGE_TILES, 1]
            own(nc.vector.memset(cells[:, EDGE_TILES:, :], -1.0))
            own(nc.vector.tensor_scalar(raw, dst_i[:, :], P - 1, None, ALU.bitwise_and))
            own(nc.vector.tensor_copy(low, raw))
            own(nc.vector.tensor_copy(key, dst_i[:, :]))
            own(nc.vector.tensor_tensor(high[:, :], key, low, ALU.subtract))
            own(nc.vector.scalar_tensor_tensor(key, high[:, :], RELS / P, rel_i[:, :], ALU.mult, ALU.add))
            nc.vector.tensor_copy(now[:, :, :], cells[:, 0:16, :]).then_inc(copied, 1)
            nc.vector.nop().then_inc(celled, 1)
            with dve.Fori(0, EDGE_TILES // 16) as i:
                dve.wait_ge(copied, i + 1)
                for k in range(16):
                    if k % 4 == 0:
                        dve.wait_ge(used, i * 16 + k + 12)
                    if k >= 8:
                        nc.vector.tensor_scalar(rows.hot[:, k, :], keep["iota"][:, 0:P], now[:, k, 0:1], None,
                                                ALU.is_equal)
                    nc.vector.tensor_scalar(key_hot[:, k % GROUP, :], keep["iota"][:, :], now[:, k, 1:2], None,
                                            ALU.is_equal).then_inc(ready, 1)
                dve.wait_ge(ready, i * 16 + 16)
                nc.vector.tensor_copy(now[:, :, :], cells[:, bass.ds(i * 16 + 16, 16), :]).then_inc(copied, 1)
            dve.wait_ge(summed, 1)
            own(nc.vector.tensor_copy(counts[:, :], ps[:, :]))
            nc.vector.nop().then_inc(counted, 1)
            own(nc.vector.reduce_sum(deg[:, :], counts[:, :].rearrange("p (w r) -> p w r", r=RELS), axis=AX.X))
            own(nc.vector.tensor_scalar(deg[:, :], deg[:, :], 1.0, None, ALU.add))
            nc.vector.nop().then_inc(counted, 1)
            dve.wait_ge(rooted, 1)
            own(nc.vector.reciprocal(keep["dinv"][:, :], root[:, :]))
            for g in range(groups):
                n = min(4, NODE_TILES - 4 * g) * P
                dve.wait_ge(turned, g + 1)
                nc.vector.tensor_copy(rel_rows[:, g * 512:g * 512 + n], tr[0:RELS, g % 2, 0:n]).then_inc(moved, 1)

        @block.scalar
        def _(act):
            act.wait_ge(celled, 1)
            rows.on_scalar(nc, act, keep, cells, EDGE_TILES, used, halves=1)
            act.wait_ge(counted, 2)
            nc.scalar.activation(root[:, :], deg[:, :], ACT.Sqrt).then_inc(rooted, 1)

        @block.tensor
        def _(pe):
            pe.wait_ge(zeroed, 1)
            nc.tensor.matmul(ps[:, :], zero[:, 0:P], zero[:, :], start=True, stop=False).then_inc(used, 16)
            with pe.Fori(0, EDGE_TILES // 16) as i:
                for k in range(16):
                    if k == 0:
                        pe.wait_ge(rows.ready, i + 2)
                        pe.sem_inc(tick, 1)
                    pe.wait_ge(ready, i * 16 + k + 1)
                    nc.tensor.matmul(ps[:, :], rows.hot[:, k, :], key_hot[:, k % GROUP, :], start=False,
                                     stop=False).then_inc(used, 1)
            nc.tensor.matmul(ps[:, :], zero[:, 0:P], zero[:, :], start=False, stop=True).then_inc(summed, 1)
            pe.wait_ge(counted, 1)
            pe.wait_ge(iotas, 3)
            for g in range(groups):
                if g >= 2:
                    pe.wait_ge(moved, g - 1)
                for b in range(min(4, NODE_TILES - 4 * g)):
                    t = 4 * g + b
                    last = nc.tensor.transpose(tr[0:RELS, g % 2, b * P:(b + 1) * P],
                                               counts[:, t * RELS:(t + 1) * RELS], keep["ident"][:, :])
                last.then_inc(turned, 1)


def change_loops(nc, keep, how, looped):
    flat = keep["adj"][:, :, :].rearrange("p t d -> p (t d)")
    most = (NODE_TILES - 1) * (NODES_P + P)
    blocks = flat[:, 0:most].rearrange("p (t d) -> p t d", d=NODES_P + P)[:, :, 0:P]
    ones = keep["ident"][:, :].unsqueeze(1).broadcast_to([P, NODE_TILES - 1, P])
    nc.vector.tensor_tensor(blocks, blocks, ones, how).then_inc(looped, 1)
    nc.vector.tensor_tensor(flat[:, most:most + P], flat[:, most:most + P], keep["ident"][:, :], how).then_inc(looped, 1)


class PowerScale:

    def __init__(self, sc, scales):
        self.scales = scales
        self.peak = sc.sb("peak", [P, 1])
        self.top = sc.sb("top", [P, 1])
        self.bits = sc.sb("bits", [P, 1], I32)
        self.exponent = sc.sb("exponent", [P, 2], I32)
        self.peaked, self.topped = sc.sem("peaked"), sc.sem("topped")

    def on_pool(self, nc, pool):
        pool.wait_ge(self.peaked, 1)
        nc.gpsimd.partition_all_reduce(self.top[:, :], self.peak[:, :], P, bass.bass_isa.ReduceOp.max).then_inc(
            self.topped, 1)

    def on_vector(self, nc, dve, own):
        dve.wait_ge(self.topped, 1)
        own(nc.vector.tensor_scalar(self.top[:, :], self.top[:, :], 2.0 ** -100, None, ALU.max))
        own(nc.vector.tensor_scalar(self.bits[:, :], self.top[:, :].bitcast(I32), 23, None, ALU.logical_shift_right))
        own(nc.vector.tensor_scalar(self.exponent[:, 0:1], self.bits[:, :], -1.0, 268.0, ALU.mult, ALU.add))
        own(nc.vector.tensor_scalar(self.exponent[:, 1:2], self.bits[:, :], 14.0, None, ALU.subtract))
        own(nc.vector.tensor_scalar(self.scales.bitcast(I32), self.exponent[:, :], 23, None, ALU.logical_shift_left))


def build_matrix(nc, io, keep):
    GROUP = 8
    ROUND = 16
    with Scope(nc, "build") as sc:
        rows = RowHots(sc)
        col_hot = sc.sb("col_hot", [P, GROUP, NODE_TILES * BUILD_W], F16)
        part = sc.ps("part", [P, GROUP, 512])
        now = sc.sb("now", [P, ROUND, 2])
        hots_ready, multiplied, own, looped, tick = (
            sc.sem(n) for n in ("hots_ready", "multiplied", "own", "looped", "tick"))
        x_all = sc.sb("x_all", [P, NODE_TILES, D])
        x_loaded, chain_sem = sc.sem("x_loaded"), sc.sem("chain")
        scale = PowerScale(sc, keep["x_scale"][:, :])
        block = sc.block()

        @block.sync
        def _(sp):
            sp.dma_start(x_all[:, :, :], io["x"].rearrange("(t p) f -> p t f", p=P)).then_inc(x_loaded, 16)

        @block.gpsimd
        def _(pool):
            scale.on_pool(nc, pool)

        @block.vector
        def _(dve):
            adj = keep["adj"]
            chain = Chain(dve, chain_sem)
            def one_hots(k):
                nc.vector.tensor_scalar(col_hot[:, k % GROUP, :], keep["iota"][:, 0:NODE_TILES * BUILD_W], now[:, k, 1:2],
                                        None, ALU.is_equal).then_inc(hots_ready, 1)

            nc.vector.tensor_copy(now[:, 0:GROUP, :], keep["cells"][:, 0:GROUP, :]).then_inc(own, 1)
            dve.wait_ge(own, 1)
            for k in range(GROUP):
                one_hots(k)
            dve.sem_clear(own)
            with dve.Fori(0, BUILD_STEPS // ROUND) as i:
                _, columns = nc.values_load_multi_w_load_instructions(
                    keep["window"][0:1, bass.ds(i * ROUND, ROUND)], engines=[mybir.EngineType.DVE], min_val=0,
                    max_val=NODES_P - BUILD_W,
                    skip_runtime_bounds_check_because="the columns are the chip's own, held to the last window")
                dve.wait_ge(hots_ready, i * ROUND + GROUP)
                nc.vector.tensor_copy(now[:, :, :], keep["cells"][:, bass.ds(i * ROUND + GROUP, ROUND), :]).then_inc(
                    own, 1)
                for k in range(ROUND):
                    at = adj[:, :, bass.ds(columns[k], BUILD_W)]
                    if k % 4 == 0:
                        dve.wait_ge(multiplied, i * ROUND + k + 4 + 16)
                    dve.wait_ge(own, k + 1)
                    nc.vector.tensor_tensor(at, at, part[:, k % GROUP, 0:NODE_TILES * BUILD_W].rearrange(
                        "p (s w) -> p s w", w=BUILD_W), ALU.add).then_inc(own, 1)
                    one_hots(k)
                dve.wait_ge(own, ROUND + 1)
                dve.sem_clear(own)
            dve.wait_ge(x_loaded, 16)
            chain(nc.vector.tensor_reduce(scale.peak[:, :], x_all[:, :, :], AX.XY, ALU.max, apply_absolute_value=True))
            nc.vector.nop().then_inc(scale.peaked, 1)
            change_loops(nc, keep, ALU.add, looped)
            scale.on_vector(nc, dve, chain)

        @block.scalar
        def _(act):
            rows.on_scalar(nc, act, keep, keep["cells"], BUILD_STEPS, multiplied)

        @block.tensor
        def _(pe):
            pe.sem_inc(multiplied, 16)
            with pe.Fori(0, BUILD_STEPS // 16) as i:
                for k in range(16):
                    if k % 8 == 0:
                        pe.wait_ge(rows.ready, i * 2 + k // 8 + 3)
                        pe.sem_inc(tick, 1)
                    pe.wait_ge(hots_ready, i * 16 + k + 1)
                    nc.tensor.matmul(part[:, k % GROUP, 0:NODE_TILES * BUILD_W], rows.hot[:, k, :],
                                     col_hot[:, k % GROUP, :], start=True, stop=True).then_inc(multiplied, 1)


def aggregate(nc, io, keep, name, source, scaled=False, relations=False, save=False, scales=None):
    SLOTS = 5
    with Scope(nc, name) as sc:
        grow, shrink = (NORMED_SCALE, 1.0 / NORMED_SCALE) if scales is None else (scales[:, 0:1], scales[:, 1:2])
        parts = sc.sb("parts", [P, NODE_TILES, 2, D], F16)
        raw = sc.sb("raw", [P, SLOTS, D])
        staged = sc.sb("staged", [P, HALF, CHUNK])
        ps = sc.ps("sums", [P, 2, HALF, 512])
        if relations:
            counts = sc.sb("counts", [RELS, CHUNK])
            vectors = sc.sb("vectors", [RELS, D])
            rel_loaded, vec_loaded, looped = sc.sem("rel_loaded"), sc.sem("vec_loaded"), sc.sem("looped")
        loaded = sc.sems("loaded", SLOTS)
        prepared, high_done, low_done, summed, out0, out1, free, tick = (
            sc.sem(n) for n in ("prepared", "high_done", "low_done", "summed", "out0",
                                "out1", "free", "tick"))
        stored = sc.sems("stored", HALF)
        saved = sc.sem("saved")
        block = sc.block()
        adj = keep["adj"]
        rows = source.rearrange("(t p) f -> t p f", p=P)

        @block.sync
        def _(sp):
            for k in range(SLOTS):
                sp.dma_start(raw[:, k, :], rows[k]).then_inc(loaded[k], 16)
            if relations:
                sp.dma_start(vectors[:, :], io["relvectors"]).then_inc(vec_loaded, 16)
            with sp.Fori(1, NODE_TILES // SLOTS) as i:
                for k in range(SLOTS):
                    sp.wait_ge(low_done, (i - 1) * SLOTS + k + 1)
                    sp.dma_start(raw[:, k, :], source[bass.ds((i * SLOTS + k) * P, P), :]).then_inc(loaded[k], 16)
            if save:
                for g in range(5):
                    sp.dma_start(io["adj_copy"][:, 5 * g:5 * g + 5, :], adj[:, 5 * g:5 * g + 5, :]).then_inc(saved, 16)
            with sp.Fori(0, CHUNKS) as c:
                if relations:
                    sp.wait_ge(summed, c + 1)
                    sp.dma_start(counts[:, :], io["rel_counts"][:, bass.ds(c * CHUNK, CHUNK)]).then_inc(rel_loaded, 16)
                for h, out in enumerate((out0, out1)):
                    sp.wait_ge(out, c + 3)
                    sp.dma_start(io["agg_t"][h, :, bass.ds(c * CHUNK, CHUNK)], staged[:, h, :]).then_inc(stored[h], 16)
                for h in range(HALF):
                    sp.wait_ge(stored[h], (c + 1) * 16)
                sp.sem_inc(free, 1)
            if save:
                sp.wait_ge(saved, 80)

        @block.vector
        def _(dve):
            if relations:
                change_loops(nc, keep, ALU.subtract, looped)
                dve.wait_ge(vec_loaded, 16)
                nc.vector.tensor_scalar(vectors[:, :], vectors[:, :], NORMED_SCALE, None, ALU.mult).then_inc(looped, 1)
            with dve.Fori(0, NODE_TILES // SLOTS) as i:
                for k in range(SLOTS):
                    dve.wait_ge(loaded[k], i * 16 + 16)
                    if scaled:
                        nc.vector.tensor_scalar(raw[:, k, :], raw[:, k, :],
                                                keep["dinv"][:, bass.ds(i * SLOTS + k, 1)], grow,
                                                ALU.mult, ALU.mult).then_inc(prepared, 1)
                    else:
                        nc.vector.tensor_scalar(raw[:, k, :], raw[:, k, :], grow, None, ALU.mult).then_inc(prepared, 1)
                for k in range(SLOTS):
                    dve.wait_ge(high_done, i * SLOTS + k + 1)
                    both = parts[:, bass.ds(i * SLOTS + k, 1), :, :].rearrange("p a b f -> p (a b) f")
                    nc.vector.tensor_tensor(both[:, 1, :], raw[:, k, :], both[:, 0, :], ALU.subtract).then_inc(low_done, 1)
            with dve.Fori(0, CHUNKS // 2) as j:
                for par in range(2):
                    dve.wait_ge(free, j * 2 + par + 1)
                    dve.wait_ge(summed, j * 2 + par + 2)
                    nc.vector.tensor_scalar(staged[:, 1, :], ps[:, par, 1, 0:CHUNK], shrink, None,
                                            ALU.mult).then_inc(out1, 1)

        @block.scalar
        def _(act):
            act.sem_inc(out0, 2)
            act.sem_inc(out1, 2)
            act.sem_inc(free, 1)
            act.sem_inc(summed, 1)
            with act.Fori(0, NODE_TILES // SLOTS) as i:
                for k in range(SLOTS):
                    act.wait_ge(prepared, i * SLOTS + k + 1)
                    act.sem_inc(tick, 1)
                    nc.scalar.activation(parts[:, bass.ds(i * SLOTS + k, 1), 0, :].rearrange("p a f -> p (a f)"),
                                         raw[:, k, :], ACT.Copy).then_inc(high_done, 1)
            with act.Fori(0, CHUNKS // 2) as j:
                for par in range(2):
                    act.wait_ge(free, j * 2 + par + 1)
                    act.sem_inc(tick, 1)
                    act.wait_ge(summed, j * 2 + par + 2)
                    nc.scalar.activation(staged[:, 0, :], ps[:, par, 0, 0:CHUNK], ACT.Identity,
                                         scale=shrink).then_inc(out0, 1)

        @block.tensor
        def _(pe):
            if relations:
                pe.wait_ge(looped, 3)
            with pe.Fori(0, CHUNKS // 2) as j:
                for par in range(2):
                    pe.wait_ge(out0, j * 2 + par + 1)
                    pe.sem_inc(tick, 1)
                    pe.wait_ge(out1, j * 2 + par + 1)
                    pe.sem_inc(tick, 1)
                    for s in range(NODE_TILES):
                        pe.wait_ge(low_done, s + 1)
                        for h in range(HALF):
                            for part in range(2):
                                last = nc.tensor.matmul(ps[:, par, h, 0:CHUNK], parts[:, s, part, h * P:(h + 1) * P],
                                                        adj[:, s, bass.ds((j * 2 + par) * CHUNK, CHUNK)],
                                                        start=(s == 0 and part == 0),
                                                        stop=(s == NODE_TILES - 1 and part == 1 and not relations))
                    if relations:
                        pe.wait_ge(rel_loaded, (j * 2 + par + 1) * 16)
                        pe.sem_inc(tick, 1)
                        for h in range(HALF):
                            last = nc.tensor.matmul(ps[:, par, h, 0:CHUNK], vectors[:, h * P:(h + 1) * P],
                                                    counts[:, :], start=False, stop=True)
                    last.then_inc(summed, 1)


SLOTS = 5
ROUNDS = NODE_TILES // SLOTS


def each(engine, i, waits, emit, done, tick=None):
    for k in range(SLOTS):
        for w in waits:
            engine.wait_ge(w, i * SLOTS + k + 1)
            if tick is not None:
                engine.sem_inc(tick, 1)
        emit(k).then_inc(done, 1)


def load_slots(sp, loads, loaded):
    for k in range(SLOTS):
        for to, source, _, _ in loads:
            sp.dma_start(to(k), source(k)).then_inc(loaded[k], 16)
    with sp.Fori(1, ROUNDS) as i:
        for to, source, free, ahead in loads:
            for k in range(SLOTS):
                sp.wait_ge(free, (i - 1) * SLOTS + k + 1 + ahead)
                sp.dma_start(to(k), source(i * SLOTS + k)).then_inc(loaded[k], 16)


def tile_rows(a):
    return lambda t: a[bass.ds(t * P, P), :]


class Norm:

    def __init__(self, sc):
        self.stats = sc.sb("stats", [P, SLOTS, 6])
        self.mean_var = sc.sb("mean_var", [P, SLOTS, 2])
        self.spread = sc.sb("spread", [P, SLOTS])
        self.inverse = sc.sb("inverse", [P, SLOTS])
        self.power = sc.sb("power", [P, SLOTS])
        (self.stat_done, self.mean_done, self.spread_done, self.inverse_done, self.power_set,
         self.tick) = (sc.sem(n) for n in ("stat_done", "mean_done", "spread_done", "inverse_done", "power_set",
                                           "norm_tick"))

    def statistics(self, nc, dve, i):
        each(dve, i, [self.stat_done], lambda k: nc.vector.bn_aggr(self.mean_var[:, k, :], self.stats[:, k, :]),
             self.mean_done, self.tick)
        dve.wait_ge(self.mean_done, i * SLOTS + SLOTS)
        nc.vector.tensor_scalar(self.spread[:, :], self.mean_var[:, :, 1], LN_EPS, None,
                                ALU.add).then_inc(self.spread_done, 1)
        dve.wait_ge(self.inverse_done, i + 1)

    def on_vector(self, nc, dve, i, y, before, out, done):
        each(dve, i, [before], lambda k: nc.vector.bn_stats(self.stats[:, k, :], y(k)), self.stat_done)
        self.statistics(nc, dve, i)
        for k in range(SLOTS):
            nc.vector.tensor_scalar(out(k), y(k), self.mean_var[:, k, 0:1], self.inverse[:, k:k + 1], ALU.subtract,
                                    ALU.mult).then_inc(done, 1)

    def set_power(self, nc, pool):
        nc.gpsimd.memset(self.power[:, :], -0.5).then_inc(self.power_set, 1)
        pool.wait_ge(self.power_set, 1)

    def on_pool(self, nc, pool, i):
        pool.wait_ge(self.spread_done, i + 1)
        nc.gpsimd.tensor_tensor(self.inverse[:, :], self.spread[:, :], self.power[:, :],
                                ALU.pow).then_inc(self.inverse_done, 1)


def round_rows(a, i):
    return a[bass.ds(i * (SLOTS * P), SLOTS * P), :].rearrange("(k p) f -> p k f", p=P)


def finish_rounds(nc, pool, norm, stores, ready, ahead, stored, tick):
    if norm:
        norm.set_power(nc, pool)
    with pool.Fori(0, ROUNDS) as i:
        if norm:
            norm.on_pool(nc, pool, i)
        pool.wait_ge(ready, i * SLOTS + SLOTS + ahead)
        pool.sem_inc(tick, 1)
        for dest, what in stores:
            pool.dma_start(round_rows(dest, i), what(i)).then_inc(stored, 16)
    pool.wait_ge(stored, 16 * len(stores) * ROUNDS)


def agg_tiles(io):
    return lambda t: io["agg_t"][:, :, bass.ds(t * P, P)].rearrange("h p n -> p h n")


def gcn_update(nc, io, keep, name, weight, bias, dest, residual=None, relu=True, scales=None):
    with Scope(nc, name) as sc:
        w = sc.sb("w", [P, HALF, D])
        b = sc.sb("b", [P, D])
        agg = sc.sb("agg", [P, SLOTS, HALF, P])
        y = sc.sb("y", [P, SLOTS, D])
        result = sc.sb("result", [P, NODE_TILES, D])
        ps = sc.ps("ps", [P, SLOTS, 512])
        norm = Norm(sc) if residual is not None else None
        x = sc.sb("x", [P, SLOTS, D]) if norm else None
        loaded = sc.sems("loaded", SLOTS)
        consts, multiplied, biased, activated, ready, stored, tick = (
            sc.sem(n) for n in ("consts", "multiplied", "biased", "activated", "ready", "stored", "tick"))
        if scales is not None:
            scale = PowerScale(sc, scales)
            peaks = sc.sb("peaks", [P, ROUNDS])
            chain_sem, round_peak = sc.sem("chain"), sc.sem("round_peak")
        block = sc.block()
        dinv = lambda i, k: keep["dinv"][:, bass.ds(i * SLOTS + k, 1)]
        out = lambda i, k: result[:, bass.ds(i * SLOTS + k, 1), :].rearrange("p a f -> p (a f)")
        loads = [(lambda k: agg[:, k, :, :], agg_tiles(io), multiplied, 0)]
        if norm:
            loads.append((lambda k: x[:, k, :], tile_rows(residual), activated, 0))

        @block.sync
        def _(sp):
            sp.dma_start(w[:, :, :], weight.rearrange("(h p) n -> p h n", p=P)).then_inc(consts, 16)
            sp.dma_start(b[:, :], bias).then_inc(consts, 16)
            load_slots(sp, loads, loaded)

        @block.tensor
        def _(pe):
            pe.wait_ge(consts, 32)
            with pe.Fori(0, ROUNDS) as i:
                for k in range(SLOTS):
                    pe.wait_ge(loaded[k], i * (16 * len(loads)) + 16 * len(loads))
                    pe.sem_inc(tick, 1)
                    pe.wait_ge(biased, i * SLOTS + k + 1)
                    pe.sem_inc(tick, 1)
                    for h in range(HALF):
                        last = nc.tensor.matmul(ps[:, k, 0:D], agg[:, k, h, :], w[:, h, :], start=(h == 0),
                                                stop=(h == HALF - 1))
                    last.then_inc(multiplied, 1)

        @block.vector
        def _(dve):
            dve.sem_inc(ready, SLOTS)
            dve.sem_inc(biased, SLOTS)
            dve.wait_ge(consts, 32)
            with dve.Fori(0, ROUNDS) as i:
                each(dve, i, [multiplied, ready], lambda k: nc.vector.scalar_tensor_tensor(
                    y[:, k, :], ps[:, k, 0:D], dinv(i, k), b[:, :], ALU.mult, ALU.add), biased)
                for k in range(SLOTS):
                    dve.wait_ge(biased, i * SLOTS + k + 1 + SLOTS)
                    if norm is None:
                        nc.vector.tensor_scalar(out(i, k), y[:, k, :], 0.0, dinv(i, k), ALU.max,
                                                ALU.mult).then_inc(ready, 1)
                    elif relu:
                        nc.vector.scalar_tensor_tensor(y[:, k, :], y[:, k, :], 0.0, x[:, k, :], ALU.max,
                                                       ALU.add).then_inc(activated, 1)
                    else:
                        nc.vector.tensor_tensor(y[:, k, :], y[:, k, :], x[:, k, :], ALU.add).then_inc(activated, 1)
                if scales is not None:
                    dve.wait_ge(ready, i * SLOTS + 2 * SLOTS)
                    nc.vector.reduce_max(peaks[:, bass.ds(i, 1)], result[:, bass.ds(i * SLOTS, SLOTS), :],
                                         axis=AX.XY).then_inc(round_peak, 1)
                if norm is not None:
                    norm.on_vector(nc, dve, i, lambda k: y[:, k, :], activated, lambda k: out(i, k), ready)

            if scales is not None:
                chain = Chain(dve, chain_sem)
                dve.wait_ge(round_peak, ROUNDS)
                chain(nc.vector.reduce_max(scale.peak[:, :], peaks[:, :], axis=AX.X))
                nc.vector.nop().then_inc(scale.peaked, 1)
                scale.on_vector(nc, dve, chain)

        @block.gpsimd
        def _(pool):
            finish_rounds(nc, pool, norm, [(dest, lambda i: result[:, bass.ds(i * SLOTS, SLOTS), :])], ready, SLOTS,
                          stored, tick)
            if scales is not None:
                scale.on_pool(nc, pool)


def gru_update(nc, io, keep):
    PS = 3
    with Scope(nc, "gru") as sc:
        w_in = sc.sb("w_in", [P, HALF, 3 * D])
        w_hid = sc.sb("w_hid", [P, HALF, 3 * D])
        b_in = sc.sb("b_in", [P, 3 * D])
        b_hid = sc.sb("b_hid", [P, 3 * D])
        gate_bias = sc.sb("gate_bias", [P, 4 * D])
        agg = sc.sb("agg", [P, SLOTS, HALF, P])
        x = sc.sb("x", [P, SLOTS, D])
        x_t = sc.sb("x_t", [P, SLOTS, HALF, P])
        gates = sc.sb("gates", [P, SLOTS, 2 * D])
        y = sc.sb("y", [P, SLOTS, D])
        turned_ps = sc.ps("turned_ps", [P, 2, 512])
        ps = sc.ps("ps", [P, PS, 2, 512])
        norm = Norm(sc)
        result = sc.sb("result", [P, NODE_TILES, D])
        agg_in, x_in = sc.sems("agg_in", SLOTS), sc.sems("x_in", SLOTS)
        (consts, turned, x_ready, multiplied, taken, new_taken, gated, reset, summed, tanned, kept, mixed, grown,
         added, ready, tick, own_sem, stored) = (sc.sem(n) for n in (
             "consts", "turned", "x_ready", "multiplied", "taken", "new_taken", "gated", "reset", "summed",
             "tanned", "kept", "mixed", "grown", "added", "ready", "tick", "own", "stored"))
        news = sc.sb("news", [P, SLOTS, 2 * D])
        block = sc.block()

        @block.sync
        def _(sp):
            for to, source in ((w_in, io["w_in"]), (w_hid, io["w_hid"])):
                sp.dma_start(to[:, :, :], source.rearrange("(h p) n -> p h n", p=P)).then_inc(consts, 16)
            sp.dma_start(b_in[:, :], io["b_in"]).then_inc(consts, 16)
            sp.dma_start(b_hid[:, :], io["b_hid"]).then_inc(consts, 16)
            for k in range(SLOTS):
                sp.dma_start(x[:, k, :], tile_rows(io["x1"])(k)).then_inc(x_in[k], 16)
                sp.dma_start(agg[:, k, :, :], agg_tiles(io)(k)).then_inc(agg_in[k], 16)
            with sp.Fori(1, ROUNDS) as i:
                for k in range(SLOTS):
                    sp.wait_ge(multiplied, (i - 1) * SLOTS + k + 1)
                    sp.dma_start(agg[:, k, :, :], agg_tiles(io)(i * SLOTS + k)).then_inc(agg_in[k], 16)
                for k in range(SLOTS):
                    sp.wait_ge(added, (i - 1) * SLOTS + k + 1)
                    sp.dma_start(x[:, k, :], tile_rows(io["x1"])(i * SLOTS + k)).then_inc(x_in[k], 16)

        @block.tensor
        def _(pe):
            pe.wait_ge(consts, 64)
            def turn(i, k):
                pe.wait_ge(x_in[k], i * 16 + 16)
                pe.sem_inc(tick, 1)
                pe.wait_ge(x_ready, i * SLOTS + k + (2 if k == 0 else 1))
                pe.sem_inc(tick, 1)
                for h in range(HALF):
                    last = nc.tensor.transpose(turned_ps[:, k % 2, h * P:(h + 1) * P], x[:, k, h * P:(h + 1) * P],
                                               keep["ident"][:, :])
                last.then_inc(turned, 1)

            with pe.Fori(0, ROUNDS) as i:
                turn(i, 0)
                for k in range(SLOTS):
                    if k + 1 < SLOTS:
                        turn(i, k + 1)
                    back = PS if k >= PS else (SLOTS if k >= SLOTS - PS else SLOTS - PS)
                    pe.wait_ge(new_taken, i * SLOTS + k + 1 + SLOTS - back)
                    pe.sem_inc(tick, 1)
                    pe.wait_ge(agg_in[k], i * 16 + 16)
                    pe.sem_inc(tick, 1)
                    for n, h in enumerate(range(HALF)):
                        nc.tensor.matmul(ps[:, k % PS, 0, 0:2 * D], agg[:, k, h, :], w_in[:, h, 0:2 * D],
                                         start=(n == 0), stop=False)
                    for h in range(HALF):
                        nc.tensor.matmul(ps[:, k % PS, 1, 0:D], agg[:, k, h, :], w_in[:, h, 2 * D:3 * D],
                                         start=(h == 0), stop=(h == 1))
                    pe.wait_ge(x_ready, i * SLOTS + k + 3)
                    pe.sem_inc(tick, 1)
                    for h in range(HALF):
                        nc.tensor.matmul(ps[:, k % PS, 0, 0:2 * D], x_t[:, k, h, :], w_hid[:, h, 0:2 * D],
                                         start=False, stop=(h == 1))
                    for h in range(HALF):
                        last = nc.tensor.matmul(ps[:, k % PS, 1, D:2 * D], x_t[:, k, h, :], w_hid[:, h, 2 * D:3 * D],
                                                start=(h == 0), stop=(h == 1))
                    last.then_inc(multiplied, 1)

        @block.scalar
        def _(act):
            act.sem_inc(x_ready, 2)
            with act.Fori(0, ROUNDS) as i:
                for k in range(SLOTS):
                    act.wait_ge(new_taken, i * SLOTS + k + 1)
                    act.sem_inc(tick, 1)
                    act.wait_ge(turned, i * SLOTS + k + 1)
                    nc.scalar.activation(x_t[:, k, :, :].rearrange("p h n -> p (h n)"), turned_ps[:, k % 2, 0:D],
                                         ACT.Copy).then_inc(x_ready, 1)
                each(act, i, [taken], lambda k: nc.scalar.activation(gates[:, k, :], gates[:, k, :], ACT.Sigmoid), gated)
                each(act, i, [summed], lambda k: nc.scalar.activation(news[:, k, 0:D], news[:, k, 0:D], ACT.Tanh), tanned)

        @block.vector
        def _(dve):
            own = Chain(dve, own_sem)
            dve.sem_inc(new_taken, SLOTS)
            dve.sem_inc(ready, SLOTS)
            dve.wait_ge(consts, 64)
            own(nc.vector.tensor_tensor(gate_bias[:, 0:2 * D], b_in[:, 0:2 * D], b_hid[:, 0:2 * D], ALU.add))
            own(nc.vector.tensor_copy(gate_bias[:, 2 * D:3 * D], b_in[:, 2 * D:3 * D]))
            own(nc.vector.tensor_copy(gate_bias[:, 3 * D:4 * D], b_hid[:, 2 * D:3 * D]))
            with dve.Fori(0, ROUNDS) as i:
                for k in range(SLOTS):
                    dve.wait_ge(ready, i * SLOTS + k + 1)
                    dve.wait_ge(multiplied, i * SLOTS + k + 1)
                    nc.vector.tensor_tensor(gates[:, k, :], ps[:, k % PS, 0, :], gate_bias[:, 0:2 * D],
                                            ALU.add).then_inc(taken, 1)
                    nc.vector.tensor_tensor(news[:, k, :], ps[:, k % PS, 1, :], gate_bias[:, 2 * D:4 * D],
                                            ALU.add).then_inc(new_taken, 1)
                dve.wait_ge(new_taken, i * SLOTS + 2 * SLOTS)
                each(dve, i, [gated], lambda k: nc.vector.tensor_tensor(
                    news[:, k, D:2 * D], news[:, k, D:2 * D], gates[:, k, 0:D], ALU.mult), reset)
                each(dve, i, [reset], lambda k: nc.vector.tensor_tensor(
                    news[:, k, 0:D], news[:, k, 0:D], news[:, k, D:2 * D], ALU.add), summed)
                each(dve, i, [tanned], lambda k: nc.vector.tensor_tensor(
                    y[:, k, :], x[:, k, :], news[:, k, 0:D], ALU.subtract), kept)
                each(dve, i, [kept], lambda k: nc.vector.tensor_tensor(
                    y[:, k, :], y[:, k, :], gates[:, k, D:2 * D], ALU.mult), mixed)
                each(dve, i, [mixed], lambda k: nc.vector.tensor_tensor(
                    y[:, k, :], y[:, k, :], news[:, k, 0:D], ALU.add), grown)
                each(dve, i, [grown], lambda k: nc.vector.tensor_tensor(
                    y[:, k, :], y[:, k, :], x[:, k, :], ALU.add), added)
                norm.on_vector(nc, dve, i, lambda k: y[:, k, :], added, lambda k: result[
                    :, bass.ds(i * SLOTS + k, 1), :].rearrange("p a f -> p (a f)"), ready)

        @block.gpsimd
        def _(pool):
            finish_rounds(nc, pool, norm, [(io["x2"], lambda i: result[:, bass.ds(i * SLOTS, SLOTS), :])], ready, SLOTS,
                          stored, tick)


def attention_inputs(nc, io, keep):
    with Scope(nc, "qkv") as sc:
        w = sc.sb("w", [P, HALF, 3 * D])
        b = sc.sb("b", [P, 3 * D])
        gain = sc.sb("gain", [P, D])
        shift = sc.sb("shift", [P, D])
        x = sc.sb("x", [P, SLOTS, D])
        x_t = sc.sb("x_t", [P, SLOTS, HALF, P])
        result = sc.sb("result", [P, NODE_TILES, 3 * D])
        turned_ps = sc.ps("turned_ps", [P, 2, 512])
        ps = sc.ps("ps", [P, 3, 2, 512])
        norm = Norm(sc)
        loaded, stored = sc.sems("loaded", SLOTS), sc.sem("stored")
        consts, normed, gained, shifted, turned, x_ready, multiplied, q_taken, ready, tick = (
            sc.sem(n) for n in ("consts", "normed", "gained", "shifted", "turned", "x_ready", "multiplied", "q_taken",
                                "ready", "tick"))
        block = sc.block()
        PS = 3

        @block.sync
        def _(sp):
            sp.dma_start(w[:, :, :], io["w_qkv"].rearrange("(h p) n -> p h n", p=P)).then_inc(consts, 16)
            sp.dma_start(b[:, :], io["b_qkv"]).then_inc(consts, 16)
            sp.dma_start(gain[:, :], io["ln_g"]).then_inc(consts, 16)
            sp.dma_start(shift[:, :], io["ln_b"]).then_inc(consts, 16)
            load_slots(sp, [(lambda k: x[:, k, :], tile_rows(io["x2"]), turned, 0)], loaded)

        @block.vector
        def _(dve):
            dve.sem_inc(ready, SLOTS)
            dve.wait_ge(consts, 64)
            with dve.Fori(0, ROUNDS) as i:
                for k in range(SLOTS):
                    dve.wait_ge(loaded[k], i * 16 + 16)
                    nc.vector.bn_stats(norm.stats[:, k, :], x[:, k, :]).then_inc(norm.stat_done, 1)
                norm.statistics(nc, dve, i)
                for k in range(SLOTS):
                    nc.vector.tensor_scalar(x[:, k, :], x[:, k, :], norm.mean_var[:, k, 0:1],
                                            norm.inverse[:, k:k + 1], ALU.subtract, ALU.mult).then_inc(normed, 1)
                each(dve, i, [normed], lambda k: nc.vector.tensor_tensor(
                    x[:, k, :], x[:, k, :], gain[:, :], ALU.mult), gained)
                each(dve, i, [gained], lambda k: nc.vector.tensor_tensor(
                    x[:, k, :], x[:, k, :], shift[:, :], ALU.add), shifted)
                for k in range(SLOTS):
                    dve.wait_ge(multiplied, i * SLOTS + k + 1)
                    out = result[:, bass.ds(i * SLOTS + k, 1), :].rearrange("p a f -> p (a f)")
                    nc.vector.tensor_tensor(out[:, 0:D], ps[:, k % PS, 0, 0:D], b[:, 0:D], ALU.add)
                    nc.vector.tensor_tensor(out[:, D:3 * D], ps[:, k % PS, 1, :], b[:, D:3 * D],
                                            ALU.add).then_inc(ready, 1)

        @block.tensor
        def _(pe):
            def turn(i, k):
                pe.wait_ge(shifted, i * SLOTS + k + 1)
                pe.sem_inc(tick, 1)
                pe.wait_ge(x_ready, i * SLOTS + k + (2 if k == 0 else 1))
                pe.sem_inc(tick, 1)
                for h in range(HALF):
                    last = nc.tensor.transpose(turned_ps[:, k % 2, h * P:(h + 1) * P], x[:, k, h * P:(h + 1) * P],
                                               keep["ident"][:, :])
                last.then_inc(turned, 1)

            with pe.Fori(0, ROUNDS) as i:
                turn(i, 0)
                for k in range(SLOTS):
                    if k + 1 < SLOTS:
                        turn(i, k + 1)
                    back = PS if k >= PS else (SLOTS if k >= SLOTS - PS else SLOTS - PS)
                    pe.wait_ge(ready, i * SLOTS + k + 1 + SLOTS - back)
                    pe.sem_inc(tick, 1)
                    pe.wait_ge(x_ready, i * SLOTS + k + 3)
                    pe.sem_inc(tick, 1)
                    for h in range(HALF):
                        nc.tensor.matmul(ps[:, k % PS, 0, 0:D], x_t[:, k, h, :], w[:, h, 0:D], start=(h == 0),
                                         stop=(h == 1))
                    for h in range(HALF):
                        last = nc.tensor.matmul(ps[:, k % PS, 1, :], x_t[:, k, h, :], w[:, h, D:3 * D],
                                                start=(h == 0), stop=(h == 1))
                    last.then_inc(multiplied, 1)

        @block.scalar
        def _(act):
            act.sem_inc(x_ready, 2)
            act.wait_ge(consts, 64)
            with act.Fori(0, ROUNDS) as i:
                for k in range(SLOTS):
                    act.wait_ge(ready, i * SLOTS + k + 1)
                    act.sem_inc(tick, 1)
                    act.wait_ge(turned, i * SLOTS + k + 1)
                    nc.scalar.activation(x_t[:, k, :, :].rearrange("p h n -> p (h n)"), turned_ps[:, k % 2, 0:D],
                                         ACT.Copy).then_inc(x_ready, 1)

        @block.gpsimd
        def _(pool):
            finish_rounds(nc, pool, norm, [(io["q"], lambda i: result[:, bass.ds(i * SLOTS, SLOTS), 0:D]),
                                           (io["kv"], lambda i: result[:, bass.ds(i * SLOTS, SLOTS), D:3 * D])],
                          ready, SLOTS, stored, tick)


def attention_edges(nc, io, keep):
    G = 4
    with Scope(nc, "edges") as outer:
        dst_place = outer.sb("dst_place", [P, EDGE_STEPS])
        cutoff = outer.sb("cutoff", [P, EDGE_STEPS])
        src_row = outer.sb("src_row", [P, EDGE_STEPS], I32)
        dst_row = outer.sb("dst_row", [P, EDGE_STEPS], I32)
        column = outer.sb("column", [1, EDGE_STEPS], I32)
        window = outer.sb("window", [1, EDGE_STEPS], I32)

        def kept(sc, dve, own, cols, step_no, width):
            src, dst, tile, weight = (c[0] for c in cols)
            under = sc.sb("under", [P, width])
            own(nc.vector.tensor_copy(src_row[:, :], src))
            own(nc.vector.tensor_scalar(dst_row[:, :], dst, float(NODES - 1), None, ALU.min))
            own(nc.vector.tensor_scalar(column[0:1, :], tile[0:1, :], float(P), None, ALU.mult))
            own(nc.vector.tensor_tensor(cutoff[:, :], step_no[:, :], tile, ALU.subtract))
            own(nc.vector.tensor_copy(window[0:1, :], cutoff[0:1, :]))
            own(nc.vector.scalar_tensor_tensor(dst_place[:, :], cutoff[:, :], -float(P), dst, ALU.mult, ALU.add))
            own(nc.vector.tensor_scalar(under[:, :], weight, 5.0, None, ALU.is_lt))
            own(nc.vector.tensor_scalar(cutoff[:, :], weight, 5.0, 0.0, ALU.min, ALU.max))
            own(nc.vector.tensor_scalar(cutoff[:, :], cutoff[:, :], -float(np.pi) / 5.0, float(np.pi) / 2.0,
                                        ALU.mult, ALU.add))
            nc.vector.nop().then_inc(angle, 1)
            dve.wait_ge(sine, 1)
            own(nc.vector.tensor_scalar(cutoff[:, :], cutoff[:, :], 0.5, 0.5, ALU.mult, ALU.add))
            own(nc.vector.tensor_tensor(cutoff[:, :], cutoff[:, :], under[:, :], ALU.mult))

        angle, sine = outer.sem("angle"), outer.sem("sine")

        def sine_on_scalar(block):
            @block.scalar
            def _(act):
                act.wait_ge(angle, 1)
                nc.scalar.activation(cutoff[:, :], cutoff[:, :], ACT.Sin).then_inc(sine, 1)

        staircase_steps(nc, "esteps", io, P, EDGE_STEPS, kept, sine_on_scalar)

        with Scope(nc, "edge") as sc:
            w = sc.sb("w", [ATTR + 1, 2 * D])
            place_no = sc.sb("place_no", [P, P])
            total = sc.sb("total", [P, NODE_TILES, D])
            attr = sc.sb("attr", [ATTR + 1, 2 * G, P])
            q = sc.sb("q", [P, 2 * G, D])
            kv = sc.sb("kv", [P, 2 * G, 2 * D])
            src_now = sc.sb("src_now", [P, 2 * G], I32)
            dst_now = sc.sb("dst_now", [P, 2 * G], I32)
            d_kv = sc.sb("d_kv", [P, 2 * G, 2 * D])
            hot = sc.sb("hot", [P, 2 * G, P])
            prod = sc.sb("prod", [P, 2 * G, D])
            message = sc.sb("message", [P, 2 * G, D])
            score = sc.sb("score", [P, 2 * G])
            attn = sc.sb("attn", [P, 2 * G])
            ps_d = sc.ps("ps_d", [P, 4, 512])
            ps_m = sc.ps("ps_m", [P, 4, 512])
            gathered, attr_in = sc.sems("gathered", 2 * G), sc.sems("attr_in", 2 * G)
            (consts, set_up, copied, multiplied, activated, hots, paired, scored, weighted, messaged, scattered, added,
             stored, tick) = (sc.sem(n) for n in (
                 "consts", "set_up", "copied", "multiplied", "activated", "hots", "paired", "scored", "weighted",
                 "messaged", "scattered", "added", "stored", "tick"))
            block = sc.block()
            U = 2 * G

            def load_attr(sp, k, at):
                t = sp.value_load(column[0:1, at], min_val=0, max_val=EDGES_P - P)
                sp.dma_start(attr[:, k, :], io["attr_t"][:, bass.ds(t, P)]).then_inc(attr_in[k], 16)

            @block.sync
            def _(sp):
                sp.dma_start(w[:, :], io["w_dkv"]).then_inc(consts, 16)
                for k in range(U):
                    load_attr(sp, k, slice(k, k + 1))
                with sp.Fori(1, EDGE_STEPS // U) as i:
                    for k in range(U):
                        sp.wait_ge(multiplied, i * U + k + 1 - U)
                        sp.sem_inc(tick, 1)
                        load_attr(sp, k, bass.ds(i * U + k, 1))
                sp.wait_ge(added, EDGE_STEPS + U)
                sp.dma_start(io["edge_sum"].rearrange("(t p) f -> p t f", p=P), total[:, :, :]).then_inc(stored, 16)
                sp.wait_ge(stored, 16)

            @block.gpsimd
            def _(pool):
                nc.gpsimd.iota(place_no[:, :], pattern=[[1, P]], base=0, channel_multiplier=0,
                               allow_small_or_imprecise_dtypes=True).then_inc(set_up, 1)
                nc.gpsimd.memset(total[:, :, :], 0.0).then_inc(set_up, 1)
                with pool.Fori(0, EDGE_STEPS // U) as i:
                    for n in range(2):
                        pool.wait_ge(messaged, i * U + n * G + G)
                        pool.sem_inc(tick, 1)
                        nc.gpsimd.tensor_copy(src_now[:, n * G:n * G + G], src_row[:, bass.ds(i * U + n * G, G)])
                        nc.gpsimd.tensor_copy(dst_now[:, n * G:n * G + G],
                                              dst_row[:, bass.ds(i * U + n * G, G)]).then_inc(copied, 1)
                        pool.wait_ge(copied, i * 2 + n + 1)
                        pool.sem_inc(tick, 1)
                        for k in range(n * G, n * G + G):
                            nc.gpsimd.indirect_dma_start(
                                q[:, k, :], None, io["q"], bass.IndirectOffsetOnAxis(ap=dst_now[:, k:k + 1], axis=0),
                                bounds_check=NODES_P - 1).then_inc(gathered[k], 16)
                            nc.gpsimd.indirect_dma_start(
                                kv[:, k, :], None, io["kv"], bass.IndirectOffsetOnAxis(ap=src_now[:, k:k + 1], axis=0),
                                bounds_check=NODES_P - 1).then_inc(gathered[k], 16)

            @block.tensor
            def _(pe):
                pe.wait_ge(consts, 16)
                with pe.Fori(0, EDGE_STEPS // U) as i:
                    for n in range(2):
                        for k in range(n * G, n * G + G):
                            pe.wait_ge(attr_in[k], i * 16 + 16)
                            pe.sem_inc(tick, 1)
                            pe.wait_ge(activated, i * U + k + 1 + U - 4)
                            pe.sem_inc(tick, 1)
                            nc.tensor.matmul(ps_d[:, k % 4, :], attr[:, k, :], w[:, :], start=True,
                                             stop=True).then_inc(multiplied, 1)
                        for k in range(n * G, n * G + G):
                            pe.wait_ge(added, i * U + k + 1 + U - 4)
                            pe.sem_inc(tick, 1)
                            pe.wait_ge(messaged, i * U + k + 1 + U)
                            pe.sem_inc(tick, 1)
                            nc.tensor.matmul(ps_m[:, k % 4, 0:D], hot[:, k, :], message[:, k, :], start=True,
                                             stop=True).then_inc(scattered, 1)

            @block.scalar
            def _(act):
                act.sem_inc(activated, U)
                with act.Fori(0, EDGE_STEPS // U) as i:
                    for n in range(2):
                        for k in range(n * G, n * G + G):
                            act.wait_ge(messaged, i * U + k + 1)
                            act.sem_inc(tick, 1)
                            act.wait_ge(multiplied, i * U + k + 1)
                            nc.scalar.activation(d_kv[:, k, :], ps_d[:, k % 4, :], ACT.Silu).then_inc(activated, 1)
                        for k in range(n * G, n * G + G):
                            act.wait_ge(scored, i * U + k + 1)
                            nc.scalar.activation(attn[:, k:k + 1], score[:, k:k + 1], ACT.Silu).then_inc(weighted, 1)

            @block.vector
            def _(dve):
                dve.sem_inc(messaged, U)
                dve.sem_inc(added, U)
                dve.wait_ge(set_up, 2)
                with dve.Fori(0, EDGE_STEPS // U) as i:
                    for n in range(2):
                        ks = range(n * G, n * G + G)
                        for k in ks:
                            dve.wait_ge(added, i * U + k + 1)
                            nc.vector.tensor_scalar(hot[:, k, :], place_no[:, :], dst_place[:, bass.ds(i * U + k, 1)],
                                                    cutoff[:, bass.ds(i * U + k, 1)], ALU.is_equal, ALU.mult)
                            dve.wait_ge(gathered[k], i * 32 + 32)
                            nc.vector.tensor_tensor(prod[:, k, :], q[:, k, :], kv[:, k, 0:D], ALU.mult).then_inc(paired, 1)
                        for k in ks:
                            dve.wait_ge(paired, i * U + k + 1)
                            dve.wait_ge(activated, i * U + k + 1 + U)
                            nc.vector.scalar_tensor_tensor(prod[:, k, :], prod[:, k, :], 1.0, d_kv[:, k, 0:D], ALU.mult,
                                                           ALU.mult, accum_out=score[:, k:k + 1]).then_inc(scored, 1)
                        for k in ks:
                            dve.wait_ge(weighted, i * U + k + 1)
                            nc.vector.scalar_tensor_tensor(message[:, k, :], kv[:, k, D:2 * D], attn[:, k:k + 1],
                                                           d_kv[:, k, D:2 * D], ALU.mult, ALU.mult).then_inc(messaged, 1)
                        for k in ks:
                            at = dve.value_load(window[0:1, bass.ds(i * U + k, 1)], min_val=0, max_val=NODE_TILES - 1)
                            acc = total[:, bass.ds(at, 1), :].rearrange("p a f -> p (a f)")
                            dve.wait_ge(scattered, i * U + k + 1)
                            dve.wait_ge(added, i * U + k + U)
                            nc.vector.tensor_tensor(acc, acc, ps_m[:, k % 4, 0:D], ALU.add).then_inc(added, 1)


def attention_update(nc, io, keep):
    with Scope(nc, "attn") as sc:
        w = sc.sb("w", [P, HALF, D])
        b = sc.sb("b", [P, D])
        s = sc.sb("s", [P, SLOTS, D])
        x = sc.sb("x", [P, SLOTS, D])
        s_t = sc.sb("s_t", [P, SLOTS, HALF, P])
        y = sc.sb("y", [P, SLOTS, D])
        turned_ps = sc.ps("turned_ps", [P, 2, 512])
        ps = sc.ps("ps", [P, SLOTS, 512])
        norm = Norm(sc)
        result = sc.sb("result", [P, NODE_TILES, D])
        s_in, x_in = sc.sems("s_in", SLOTS), sc.sems("x_in", SLOTS)
        stored, restored = sc.sem("stored"), sc.sem("restored")
        consts, turned, s_ready, multiplied, biased, added, ready, tick = (
            sc.sem(n) for n in ("consts", "turned", "s_ready", "multiplied", "biased", "added", "ready", "tick"))
        block = sc.block()

        @block.sync
        def _(sp):
            def restore(tiles):
                sp.dma_start(keep["adj"][:, tiles, :], io["adj_copy"][:, tiles, :]).then_inc(restored, 16)

            sp.dma_start(w[:, :, :], io["w_out"].rearrange("(h p) n -> p h n", p=P)).then_inc(consts, 16)
            sp.dma_start(b[:, :], io["b_out"]).then_inc(consts, 16)
            for k in range(SLOTS):
                sp.dma_start(s[:, k, :], tile_rows(io["edge_sum"])(k)).then_inc(s_in[k], 16)
                sp.dma_start(x[:, k, :], tile_rows(io["x2"])(k)).then_inc(x_in[k], 16)
            restore(slice(0, SLOTS))
            with sp.Fori(1, ROUNDS) as i:
                for k in range(SLOTS):
                    sp.wait_ge(turned, (i - 1) * SLOTS + k + 1)
                    sp.dma_start(s[:, k, :], tile_rows(io["edge_sum"])(i * SLOTS + k)).then_inc(s_in[k], 16)
                    restore(bass.ds(i * SLOTS + k, 1))
                for k in range(SLOTS):
                    sp.wait_ge(added, (i - 1) * SLOTS + k + 1)
                    sp.dma_start(x[:, k, :], tile_rows(io["x2"])(i * SLOTS + k)).then_inc(x_in[k], 16)
            sp.wait_ge(restored, 16 * (1 + NODE_TILES - SLOTS))

        @block.tensor
        def _(pe):
            pe.wait_ge(consts, 32)
            def turn(i, k):
                pe.wait_ge(s_in[k], i * 16 + 16)
                pe.sem_inc(tick, 1)
                pe.wait_ge(s_ready, i * SLOTS + k + (2 if k == 0 else 1))
                pe.sem_inc(tick, 1)
                for h in range(HALF):
                    last = nc.tensor.transpose(turned_ps[:, k % 2, h * P:(h + 1) * P], s[:, k, h * P:(h + 1) * P],
                                               keep["ident"][:, :])
                last.then_inc(turned, 1)

            with pe.Fori(0, ROUNDS) as i:
                turn(i, 0)
                for k in range(SLOTS):
                    if k + 1 < SLOTS:
                        turn(i, k + 1)
                    pe.wait_ge(biased, i * SLOTS + k + 1)
                    pe.sem_inc(tick, 1)
                    pe.wait_ge(s_ready, i * SLOTS + k + 3)
                    pe.sem_inc(tick, 1)
                    for h in range(HALF):
                        last = nc.tensor.matmul(ps[:, k, 0:D], s_t[:, k, h, :], w[:, h, :], start=(h == 0), stop=(h == 1))
                    last.then_inc(multiplied, 1)

        @block.scalar
        def _(act):
            act.sem_inc(s_ready, 2)
            with act.Fori(0, ROUNDS) as i:
                for k in range(SLOTS):
                    act.wait_ge(biased, i * SLOTS + k + 1)
                    act.sem_inc(tick, 1)
                    act.wait_ge(turned, i * SLOTS + k + 1)
                    nc.scalar.activation(s_t[:, k, :, :].rearrange("p h n -> p (h n)"), turned_ps[:, k % 2, 0:D],
                                         ACT.Copy).then_inc(s_ready, 1)

        @block.vector
        def _(dve):
            dve.sem_inc(ready, SLOTS)
            dve.sem_inc(biased, SLOTS)
            dve.wait_ge(consts, 32)
            with dve.Fori(0, ROUNDS) as i:
                each(dve, i, [multiplied, ready], lambda k: nc.vector.tensor_tensor(
                    y[:, k, :], ps[:, k, 0:D], b[:, :], ALU.add), biased)
                for k in range(SLOTS):
                    dve.wait_ge(x_in[k], i * 16 + 16)
                    dve.wait_ge(biased, i * SLOTS + k + 1 + SLOTS)
                    nc.vector.scalar_tensor_tensor(y[:, k, :], x[:, k, :], 2.0, y[:, k, :], ALU.mult,
                                                   ALU.add).then_inc(added, 1)
                norm.on_vector(nc, dve, i, lambda k: y[:, k, :], added, lambda k: result[
                    :, bass.ds(i * SLOTS + k, 1), :].rearrange("p a f -> p (a f)"), ready)

        @block.gpsimd
        def _(pool):
            finish_rounds(nc, pool, norm, [(io["x3"], lambda i: result[:, bass.ds(i * SLOTS, SLOTS), :])], ready, SLOTS,
                          stored, tick)


def program(nc, io):
    with Scope(nc, "all") as sc:
        keep = {
            "dinv": sc.sb("dinv", [P, NODE_TILES]),
            "ident": sc.sb("ident", [P, P]),
            "x_scale": sc.sb("x_scale", [P, 2]),
            "z_scale": sc.sb("z_scale", [P, 2]),
            "iota": sc.sb("iota", [P, NODE_TILES * RELS], F16),
        }
        with Scope(nc, "first") as held:
            keep["adj"] = held.sb("adj", [P, NODE_TILES, NODES_P], F16)
            with Scope(nc, "steps") as st:
                keep["cells"] = st.sb("cells", [P, BUILD_STEPS + 8, 2])
                keep["window"] = st.sb("window", [1, BUILD_STEPS], I32)
                build_steps(nc, io, keep)
                histogram(nc, io, keep)
                build_matrix(nc, io, keep)
            aggregate(nc, io, keep, "agg0", io["x"], scaled=True, save=True, scales=keep["x_scale"])
            gcn_update(nc, io, keep, "gcn0", io["w1"], io["b1"], io["z1"], scales=keep["z_scale"][:, :])
            aggregate(nc, io, keep, "agg1", io["z1"], scales=keep["z_scale"])
            gcn_update(nc, io, keep, "gcn1", io["w2"], io["b2"], io["x1"], residual=io["x"])
            aggregate(nc, io, keep, "agg2", io["x1"], relations=True)
        gru_update(nc, io, keep)
        attention_inputs(nc, io, keep)
        attention_edges(nc, io, keep)
        with Scope(nc, "second") as held:
            keep["adj"] = held.sb("adj", [P, NODE_TILES, NODES_P], F16)
            attention_update(nc, io, keep)
            aggregate(nc, io, keep, "agg3", io["x3"], scaled=True)
        gcn_update(nc, io, keep, "gcn3", io["w3"], io["b3"], io["out"], residual=io["x3"], relu=False)


def kernel(**inputs):
    import concourse.bacc as bacc
    from concourse.bass_utils import run_bass_kernel_spmd

    a = {k: np.asarray(v) for k, v in inputs.items()}
    nc = bacc.Bacc("TRN2", target_bir_lowering=False, num_devices=1)
    arrays, io = {}, {}

    def give(name, array):
        array = np.ascontiguousarray(array)
        arrays[name] = array
        io[name] = nc.dram_tensor(name, list(array.shape), mybir.dt.from_np(array.dtype), kind="ExternalInput").ap()

    def edges(v, fill):
        return np.concatenate([v, np.full(EDGES_P - EDGES, fill, v.dtype)]).reshape(EDGE_TILES, P)

    src, dst = edges(a["src"], 0), edges(a["dst"], NO_NODE)
    give("src_t", src)
    give("dst_t", dst)
    give("next_t", np.concatenate([dst[1:, 0], np.full(1, NO_NODE, dst.dtype)]))
    give("wts_t", edges(a["edge_weight"], 0))
    give("dst_p", dst.T)
    give("rel_p", edges(a["edge_type_16"], 0).T)

    def scratch(name, shape, dt=F32, kind="Internal"):
        io[name] = nc.dram_tensor(name, list(shape), dt, kind=kind).ap()

    def nodes(v):
        return np.concatenate([v, np.zeros((NODES_P - NODES, D), v.dtype)])

    def rows(v):
        return np.broadcast_to(v.reshape(1, -1), (P, v.size))

    give("x", nodes(a["x"]))
    give("attr_t", np.concatenate([np.concatenate([a["edge_attr_64"].T, np.zeros((ATTR, EDGES_P - EDGES), np.float32)], 1),
                                   np.ones((1, EDGES_P), np.float32)]))
    give("w_dkv", np.concatenate([
        np.concatenate([a["L2_gnn_Wdk"].T, a["L2_gnn_Wdv"].T], 1),
        np.concatenate([a["L2_gnn_bdk"], a["L2_gnn_bdv"]])[None]]))
    give("relvectors", a["L1_gnn_relvectors"])
    give("w1", a["L0_gnn_W1"])
    give("b1", rows(a["L0_gnn_b1"]))
    give("w2", a["L0_gnn_W2"])
    give("b2", rows(a["L0_gnn_b2"]))
    give("w3", a["L3_gnn_W"].T)
    give("b3", rows(a["L3_gnn_b"]))
    give("w_in", a["L1_gnn_w_ih"].T)
    give("b_in", rows(a["L1_gnn_b_ih"]))
    give("w_hid", a["L1_gnn_w_hh"].T)
    give("b_hid", rows(a["L1_gnn_b_hh"]))
    give("w_qkv", np.concatenate([a["L2_gnn_Wq"].T, a["L2_gnn_Wk"].T, a["L2_gnn_Wv"].T], 1))
    give("b_qkv", rows(np.concatenate([a["L2_gnn_bq"], a["L2_gnn_bk"], a["L2_gnn_bv"]])))
    give("w_out", a["L2_gnn_Wo"].T)
    give("b_out", rows(a["L2_gnn_bo"]))
    give("ln_g", rows(a["L2_gnn_ln_g"]))
    give("ln_b", rows(a["L2_gnn_ln_b"]))

    scratch("rel_counts", [RELS, NODES_P])
    scratch("adj_copy", [P, NODE_TILES, NODES_P], F16)
    scratch("agg_t", [HALF, P, NODES_P])
    for name in ("z1", "x1", "x2", "x3", "q", "edge_sum"):
        scratch(name, [NODES_P, D])
    scratch("kv", [NODES_P, 2 * D])
    scratch("out", [NODES_P, D], kind="ExternalOutput")
    program(nc, io)
    r = run_bass_kernel_spmd(nc, [arrays], core_ids=[0])
    return r.results[0]["out"][0:NODES]
```

```python
from contextlib import ExitStack

import numpy as np

import concourse.bass as bass
import concourse.mybir as mybir

F32 = mybir.dt.float32
F16 = mybir.dt.float16
BF16 = mybir.dt.bfloat16
I32 = mybir.dt.int32
ALU = mybir.AluOpType
ACT = mybir.ActivationFunctionType
AX = mybir.AxisListType

P = 128
NODES = 3125
EDGES = 53125
D = 256
HALF = D // P
ATTR = 64
RELS = 16
NODE_TILES = -(-NODES // P)
NODES_P = NODE_TILES * P
EDGE_TILES = -(-EDGES // P)
EDGES_P = EDGE_TILES * P
NO_NODE = 4095
SEL_J = 4
SEL_P = EDGE_TILES // SEL_J
BUILD_W = 8
BUILD_WINDOWS = NODES_P // BUILD_W
BUILD_STEPS = EDGE_TILES + BUILD_WINDOWS
EDGE_STEPS = EDGE_TILES + NODE_TILES - 1
CHUNK = 400
CHUNKS = NODES_P // CHUNK
RESTORED = 2
LN_EPS = 1e-5
NORMED_SCALE = 1024.0


class Chain:

    def __init__(self, engine, sem):
        self.engine, self.sem, self.n = engine, sem, 0

    def __call__(self, instruction):
        self.n += 1
        instruction.then_inc(self.sem, 1)
        self.engine.wait_ge(self.sem, self.n)


class Scope:

    def __init__(self, nc, name):
        self.nc, self.name, self.stack, self.semaphores = nc, name, ExitStack(), []

    def __enter__(self):
        self.stack.__enter__()
        return self

    def __exit__(self, *a):
        self.stack.__exit__(*a)
        if self.semaphores:
            self.nc.clear_and_free_semaphores(self.semaphores)
            self.nc.all_engine_barrier()

    def sb(self, name, shape, dt=F32):
        return self.stack.enter_context(self.nc.sbuf_tensor(f"{self.name}_{name}", list(shape), dt))

    def ps(self, name, shape, dt=F32):
        return self.stack.enter_context(self.nc.psum_tensor(f"{self.name}_{name}", list(shape), dt))

    def sem(self, name):
        self.semaphores.append(self.nc.alloc_semaphore(name=f"{self.name}_{name}"))
        return self.semaphores[-1]

    def sems(self, name, n):
        return [self.sem(f"{name}{k}") for k in range(n)]

    def block(self):
        return self.stack.enter_context(self.nc.Block())


def staircase_steps(nc, name, io, window, steps, kept, beside=None, on_pool=None, places=None):
    shift = window.bit_length() - 1
    parts = -(-steps // 512)
    width = -(-steps // parts)
    with Scope(nc, name) as sc:
        src_i = sc.sb("src_i", [SEL_P, SEL_J, P], I32)
        dst_i = sc.sb("dst_i", [SEL_P, SEL_J, P], I32)
        next_i = sc.sb("next_i", [SEL_P, SEL_J], I32)
        first_i = sc.sb("first_i", [SEL_P, SEL_J], I32)
        wts = sc.sb("wts", [SEL_P, SEL_J, P])
        src_f = sc.sb("src_f", [SEL_P, SEL_J, P])
        dst_f = sc.sb("dst_f", [SEL_P, SEL_J, P])
        tile_f = sc.sb("tile_f", [SEL_P, SEL_J, P])
        starts = sc.sb("starts", [SEL_P, 2, SEL_J])
        step_no = sc.sb("step_no", [P, steps])
        after = sc.sb("after", [SEL_P, steps])
        select = sc.sb("select", [SEL_P, SEL_J, steps])
        sums = [sc.ps(f"sums{v}", [P, parts, 512]) for v in range(3 if parts > 1 else 4)]
        loaded, iotas, selected, picked, dve_own = (
            sc.sem(n) for n in ("loaded", "iotas", "selected", "picked", "dve_own"))
        values = [src_f, dst_f, tile_f, wts][:len(sums)]
        if places is not None:
            block_rows = steps // SEL_J
            place = sc.sb("place", [SEL_P, SEL_J, P])
            rows = sc.sb("rows", [block_rows, SEL_J, P], F16)
            rows_ps = sc.ps("rows_ps", [block_rows, SEL_J, P])
            placed, rows_made, rows_moved, stored = (sc.sem(n) for n in ("placed", "rows_made", "rows_moved", "stored"))
        block = sc.block()
        if beside is not None:
            def move_rows(act):
                act.wait_ge(rows_made, 1)
                nc.scalar.activation(rows[:, :, :], rows_ps[:, :, :], ACT.Copy).then_inc(rows_moved, 1)

            beside(block, move_rows)

        @block.sync
        def _(sp):
            by_tile = lambda a: a.rearrange("(p j) e -> p j e", j=SEL_J)
            sp.dma_start(src_i[:, :, :], by_tile(io["src_t"][0:EDGE_TILES])).then_inc(loaded, 16)
            sp.dma_start(dst_i[:, :, :], by_tile(io["dst_t"][0:EDGE_TILES])).then_inc(loaded, 16)
            sp.dma_start(next_i[:, :], io["next_t"].rearrange("(p j) -> p j", j=SEL_J)).then_inc(loaded, 16)
            sp.dma_start(wts[:, :, :], by_tile(io["wts_t"][0:EDGE_TILES])).then_inc(loaded, 16)
            if places is not None:
                sp.wait_ge(rows_moved, 1)
                sp.dma_start(places.rearrange("(b s) e -> s b e", b=SEL_J), rows[:, :, :]).then_inc(stored, 16)
                sp.wait_ge(stored, 16)

        @block.gpsimd
        def _(pool):
            nc.gpsimd.iota(step_no[:, :], pattern=[[1, steps]], base=0, channel_multiplier=0,
                           allow_small_or_imprecise_dtypes=True).then_inc(iotas, 1)
            nc.gpsimd.iota(tile_f[:, :, :], pattern=[[1, SEL_J], [0, P]], base=0, channel_multiplier=SEL_J,
                           allow_small_or_imprecise_dtypes=True).then_inc(iotas, 1)
            if on_pool is not None:
                on_pool(pool)

        @block.vector
        def _(dve):
            own = Chain(dve, dve_own)
            dve.wait_ge(loaded, 64)
            dve.wait_ge(iotas, 2)
            own(nc.vector.tensor_copy(first_i[:, :], dst_i[:, :, 0]))
            own(nc.vector.memset(first_i[0:1, 0:1], 0))
            own(nc.vector.tensor_scalar(first_i[:, :], first_i[:, :], shift, None, ALU.logical_shift_right))
            own(nc.vector.tensor_scalar(next_i[:, :], next_i[:, :], shift, None, ALU.logical_shift_right))
            own(nc.vector.tensor_tensor(starts[:, 0, :], first_i[:, :], tile_f[:, :, 0], ALU.add))
            own(nc.vector.scalar_tensor_tensor(starts[:, 1, :], next_i[:, :], 1.0, tile_f[:, :, 0],
                                               ALU.add, ALU.add))
            own(nc.vector.tensor_copy(src_f[:, :, :], src_i[:, :, :]))
            own(nc.vector.tensor_copy(dst_f[:, :, :], dst_i[:, :, :]))
            for j in range(SEL_J):
                own(nc.vector.tensor_scalar(after[:, :], step_no[0:SEL_P, :], starts[:, 1, j:j + 1], None,
                                            ALU.is_ge))
                last = nc.vector.scalar_tensor_tensor(select[:, j, :], step_no[0:SEL_P, :], starts[:, 0, j:j + 1],
                                                      after[:, :], ALU.is_ge, ALU.subtract)
                own(last)
            nc.vector.nop().then_inc(selected, 1)
            if places is not None:
                own(nc.vector.tensor_scalar(dst_i[:, :, :], dst_i[:, :, :], P - 1, None, ALU.bitwise_and))
                nc.vector.tensor_copy(place[:, :, :], dst_i[:, :, :]).then_inc(placed, 1)
            dve.wait_ge(picked, 1)
            kept(sc, dve, own, [[s[:, h, 0:width] for h in range(parts)] for s in sums], step_no, width)

        @block.tensor
        def _(pe):
            pe.wait_ge(selected, 1)
            for v, value in enumerate(values):
                for h in range(parts):
                    for j in range(SEL_J):
                        last = nc.tensor.matmul(sums[v][:, h, 0:width], value[:, j, :],
                                                select[:, j, h * width:(h + 1) * width],
                                                start=(j == 0), stop=(j == SEL_J - 1))
            last.then_inc(picked, 1)
            if places is not None:
                pe.wait_ge(placed, 1)
                for b in range(SEL_J):
                    for j in range(SEL_J):
                        last = nc.tensor.matmul(rows_ps[:, b, :], select[:, j, b * block_rows:(b + 1) * block_rows],
                                                place[:, j, :], start=(j == 0), stop=(j == SEL_J - 1))
                last.then_inc(rows_made, 1)


def build_steps(nc, io, keep):

    def kept(sc, dve, own, cols, step_no, width):
        own(nc.vector.memset(keep["cells"][:, BUILD_STEPS:, :], -1.0))
        raw = sc.sb("raw", [P, width], I32)
        win = sc.sb("win", [P, width])
        col = sc.sb("col", [P, width])
        ok = sc.sb("ok", [P, width])
        ok2 = sc.sb("ok2", [P, width])
        for h, (src, dst, tile) in enumerate(zip(*cols)):
            at = slice(h * width, (h + 1) * width)
            own(nc.vector.tensor_copy(raw[:, :], src))
            own(nc.vector.tensor_scalar(raw[:, :], raw[:, :], P - 1, None, ALU.bitwise_and))
            own(nc.vector.tensor_copy(keep["cells"][:, at, 0], raw[:, :]))
            own(nc.vector.tensor_tensor(col[:, :], src, keep["cells"][:, at, 0], ALU.subtract))
            own(nc.vector.tensor_tensor(win[:, :], step_no[:, at], tile, ALU.subtract))
            own(nc.vector.tensor_scalar(keep["window"][0:1, at], win[0:1, :], float(BUILD_WINDOWS - 1),
                                        float(BUILD_W), ALU.min, ALU.mult))
            own(nc.vector.scalar_tensor_tensor(win[:, :], win[:, :], -float(BUILD_W), dst, ALU.mult, ALU.add))
            own(nc.vector.tensor_scalar(ok[:, :], win[:, :], 0.0, None, ALU.is_ge))
            own(nc.vector.scalar_tensor_tensor(ok2[:, :], win[:, :], float(BUILD_W), ok[:, :], ALU.is_lt,
                                               ALU.mult))
            own(nc.vector.scalar_tensor_tensor(col[:, :], col[:, :], BUILD_W / P, win[:, :], ALU.mult, ALU.add))
            own(nc.vector.scalar_tensor_tensor(col[:, :], col[:, :], 1.0, ok2[:, :], ALU.add, ALU.mult))
            own(nc.vector.tensor_scalar(keep["cells"][:, at, 1], col[:, :], 1.0, None, ALU.subtract))

    staircase_steps(nc, "bsteps", io, BUILD_W, BUILD_STEPS, kept)


class RowHots:

    def __init__(self, sc):
        self.hot = sc.sb("row_hot", [P, 16, P], F16)
        self.now = sc.sb("row_now", [P, 2, 8])
        self.distance = sc.sb("distance", [P, 2, 8, P], F16)
        self.copied, self.apart, self.ready, self.tick = (
            sc.sem(n) for n in ("row_copied", "row_apart", "row_ready", "row_tick"))

    def on_scalar(self, nc, act, keep, cells, steps, used, halves=2):
        act.sem_inc(self.ready, halves)
        with act.Fori(0, steps // 16) as i:
            for n in range(halves):
                act.wait_ge(self.ready, i * halves + n + 1)
                act.sem_inc(self.tick, 1)
                nc.scalar.activation(self.now[:, n, :], cells[:, bass.ds(i * 16 + n * 8, 8), 0],
                                     ACT.Copy).then_inc(self.copied, 1)
                act.wait_ge(self.copied, i * halves + n + 1)
                for k in range(8):
                    nc.scalar.activation(self.distance[:, n, k, :], keep["iota"][:, 0:P], ACT.Abs,
                                         bias=self.now[:, n, k:k + 1], scale=-1.0).then_inc(self.apart, 1)
                act.wait_ge(self.apart, i * (8 * halves) + n * 8 + 8)
                act.sem_inc(self.tick, 1)
                act.wait_ge(used, i * 16 + n * 8 + 8)
                nc.scalar.activation(self.hot[:, n * 8:n * 8 + 8, :].rearrange("p k e -> p (k e)"),
                                     self.distance[:, n, :, :].rearrange("p k e -> p (k e)"), ACT.Relu, bias=1.0,
                                     scale=-1.0).then_inc(self.ready, 1)


def histogram(nc, io, keep):
    GROUP = 8
    with Scope(nc, "hist") as sc:
        dst_i = sc.sb("dst_i", [P, EDGE_TILES], I32)
        rel_i = sc.sb("rel_i", [P, EDGE_TILES], I32)
        high = sc.sb("high", [P, EDGE_TILES])
        cells = sc.sb("cells", [P, EDGE_TILES + 16, 2])
        now = sc.sb("now", [P, 16, 2])
        root = sc.sb("root", [P, NODE_TILES])
        copied_low, copied_high, celled = sc.sem("copied_low"), sc.sem("copied_high"), sc.sem("celled")
        rows = RowHots(sc)
        key_hot = sc.sb("key_hot", [P, GROUP, NODE_TILES * RELS], F16)
        counts = sc.sb("counts", [P, NODE_TILES * RELS])
        deg = sc.sb("deg", [P, NODE_TILES])
        rel_rows = sc.sb("rel_rows", [RELS, NODES_P])
        zero = sc.sb("zero", [P, NODE_TILES * RELS], F16)
        ps = sc.ps("counts_ps", [P, NODE_TILES * RELS])
        tr = sc.ps("rel_ps", [P, 2, 512])
        loaded, ready, used, dve_own, iotas, summed, counted, rooted, turned, moved, stored, zeroed, tick = (
            sc.sem(n) for n in ("loaded", "ready", "used", "dve_own", "iotas", "summed", "counted", "rooted",
                                "turned", "moved", "stored", "zeroed", "tick"))
        block = sc.block()
        groups = -(-NODE_TILES // 4)

        @block.sync
        def _(sp):
            sp.dma_start(dst_i[:, :], io["dst_p"]).then_inc(loaded, 16)
            sp.dma_start(rel_i[:, :], io["rel_p"]).then_inc(loaded, 16)
            sp.wait_ge(moved, groups)
            sp.dma_start(io["rel_counts"], rel_rows[:, :]).then_inc(stored, 16)
            sp.wait_ge(stored, 16)

        @block.gpsimd
        def _(pool):
            nc.gpsimd.iota(keep["iota"][:, :], pattern=[[1, NODE_TILES * RELS]], base=0, channel_multiplier=0,
                           allow_small_or_imprecise_dtypes=True).then_inc(iotas, 1)
            nc.gpsimd.memset(zero[:, :], 0.0).then_inc(zeroed, 1)
            nc.gpsimd.memset(keep["ident"][:, :], 0.0).then_inc(iotas, 1)
            pool.wait_ge(iotas, 2)
            nc.gpsimd.affine_select(out=keep["ident"][:, :], in_=keep["ident"][:, :], compare_op=ALU.not_equal,
                                    fill=1.0, base=0, pattern=[[-1, P]], channel_multiplier=1).then_inc(iotas, 1)
            for part in range(0, NODE_TILES, 5):
                nc.gpsimd.memset(keep["adj"][:, part:part + 5, :], 0.0).then_inc(zeroed, 1)

        @block.vector
        def _(dve):
            own = Chain(dve, dve_own)
            dve.wait_ge(loaded, 32)
            dve.wait_ge(iotas, 3)
            raw = high[:, :].bitcast(I32)
            low, key = cells[:, 0:EDGE_TILES, 0], cells[:, 0:EDGE_TILES, 1]
            own(nc.vector.memset(cells[:, EDGE_TILES:, :], -1.0))
            own(nc.vector.tensor_scalar(raw, dst_i[:, :], P - 1, None, ALU.bitwise_and))
            own(nc.vector.tensor_copy(low, raw))
            own(nc.vector.tensor_copy(key, dst_i[:, :]))
            own(nc.vector.tensor_tensor(high[:, :], key, low, ALU.subtract))
            own(nc.vector.scalar_tensor_tensor(key, high[:, :], RELS / P, rel_i[:, :], ALU.mult, ALU.add))
            nc.vector.tensor_copy(now[:, 0:8, :], cells[:, 0:8, :]).then_inc(copied_low, 1)
            dve.sem_inc(ready, 8)
            nc.vector.nop().then_inc(celled, 1)
            with dve.Fori(0, EDGE_TILES // 16) as i:
                dve.wait_ge(copied_low, i + 1)
                for k in range(16):
                    if k == 2:
                        dve.wait_ge(ready, i * 16 + 8)
                        nc.vector.tensor_copy(now[:, 8:16, :], cells[:, bass.ds(i * 16 + 8, 8), :]).then_inc(
                            copied_high, 1)
                    if k == 8:
                        dve.wait_ge(copied_high, i + 1)
                    if k == 10:
                        dve.wait_ge(ready, i * 16 + 16)
                        nc.vector.tensor_copy(now[:, 0:8, :], cells[:, bass.ds(i * 16 + 16, 8), :]).then_inc(
                            copied_low, 1)
                    if k % 4 == 0:
                        dve.wait_ge(used, i * 16 + k + 12)
                    if k >= 8:
                        nc.vector.tensor_scalar(rows.hot[:, k, :], keep["iota"][:, 0:P], now[:, k, 0:1], None,
                                                ALU.is_equal)
                    nc.vector.tensor_scalar(key_hot[:, k % GROUP, :], keep["iota"][:, :], now[:, k, 1:2], None,
                                            ALU.is_equal).then_inc(ready, 1)
            dve.wait_ge(summed, 1)
            own(nc.vector.tensor_copy(counts[:, :], ps[:, :]))
            nc.vector.nop().then_inc(counted, 1)
            own(nc.vector.reduce_sum(deg[:, :], counts[:, :].rearrange("p (w r) -> p w r", r=RELS), axis=AX.X))
            own(nc.vector.tensor_scalar(deg[:, :], deg[:, :], 1.0, None, ALU.add))
            nc.vector.nop().then_inc(counted, 1)
            dve.wait_ge(rooted, 1)
            own(nc.vector.reciprocal(keep["dinv"][:, :], root[:, :]))
            for g in range(groups):
                n = min(4, NODE_TILES - 4 * g) * P
                dve.wait_ge(turned, g + 1)
                nc.vector.tensor_copy(rel_rows[:, g * 512:g * 512 + n], tr[0:RELS, g % 2, 0:n]).then_inc(moved, 1)

        @block.scalar
        def _(act):
            act.wait_ge(celled, 1)
            rows.on_scalar(nc, act, keep, cells, EDGE_TILES, used, halves=1)
            act.wait_ge(counted, 2)
            nc.scalar.activation(root[:, :], deg[:, :], ACT.Sqrt).then_inc(rooted, 1)

        @block.tensor
        def _(pe):
            pe.wait_ge(zeroed, 1)
            nc.tensor.matmul(ps[:, :], zero[:, 0:P], zero[:, :], start=True, stop=False).then_inc(used, 16)
            with pe.Fori(0, EDGE_TILES // 16) as i:
                for k in range(16):
                    if k == 0:
                        pe.wait_ge(rows.ready, i + 2)
                        pe.sem_inc(tick, 1)
                    pe.wait_ge(ready, i * 16 + k + 9)
                    nc.tensor.matmul(ps[:, :], rows.hot[:, k, :], key_hot[:, k % GROUP, :], start=False,
                                     stop=False).then_inc(used, 1)
            nc.tensor.matmul(ps[:, :], zero[:, 0:P], zero[:, :], start=False, stop=True).then_inc(summed, 1)
            pe.wait_ge(counted, 1)
            pe.wait_ge(iotas, 3)
            for g in range(groups):
                if g >= 2:
                    pe.wait_ge(moved, g - 1)
                for b in range(min(4, NODE_TILES - 4 * g)):
                    t = 4 * g + b
                    last = nc.tensor.transpose(tr[0:RELS, g % 2, b * P:(b + 1) * P],
                                               counts[:, t * RELS:(t + 1) * RELS], keep["ident"][:, :])
                last.then_inc(turned, 1)


def change_loops(nc, keep, how, looped):
    flat = keep["adj"][:, :, :].rearrange("p t d -> p (t d)")
    most = (NODE_TILES - 1) * (NODES_P + P)
    blocks = flat[:, 0:most].rearrange("p (t d) -> p t d", d=NODES_P + P)[:, :, 0:P]
    ones = keep["ident"][:, :].unsqueeze(1).broadcast_to([P, NODE_TILES - 1, P])
    nc.vector.tensor_tensor(blocks, blocks, ones, how).then_inc(looped, 1)
    nc.vector.tensor_tensor(flat[:, most:most + P], flat[:, most:most + P], keep["ident"][:, :], how).then_inc(looped, 1)


class PowerScale:

    def __init__(self, sc, scales):
        self.scales = scales
        self.peak = sc.sb("peak", [P, 1])
        self.top = sc.sb("top", [P, 1])
        self.bits = sc.sb("bits", [P, 1], I32)
        self.exponent = sc.sb("exponent", [P, 2], I32)
        self.peaked, self.topped = sc.sem("peaked"), sc.sem("topped")

    def on_pool(self, nc, pool):
        pool.wait_ge(self.peaked, 1)
        nc.gpsimd.partition_all_reduce(self.top[:, :], self.peak[:, :], P, bass.bass_isa.ReduceOp.max).then_inc(
            self.topped, 1)

    def on_vector(self, nc, dve, own):
        dve.wait_ge(self.topped, 1)
        own(nc.vector.tensor_scalar(self.top[:, :], self.top[:, :], 2.0 ** -100, None, ALU.max))
        own(nc.vector.tensor_scalar(self.bits[:, :], self.top[:, :].bitcast(I32), 23, None, ALU.logical_shift_right))
        own(nc.vector.tensor_scalar(self.exponent[:, 0:1], self.bits[:, :], -1.0, 268.0, ALU.mult, ALU.add))
        own(nc.vector.tensor_scalar(self.exponent[:, 1:2], self.bits[:, :], 14.0, None, ALU.subtract))
        own(nc.vector.tensor_scalar(self.scales.bitcast(I32), self.exponent[:, :], 23, None, ALU.logical_shift_left))


def build_matrix(nc, io, keep):
    GROUP = 8
    ROUND = 24
    with Scope(nc, "build") as sc:
        rows = RowHots(sc)
        col_hot = sc.sb("col_hot", [P, GROUP, NODE_TILES * BUILD_W], F16)
        part = sc.ps("part", [P, GROUP, 512])
        now = sc.sb("now", [P, ROUND, 2])
        first, second = sc.sem("first_half"), sc.sem("second_half")
        hots_ready, multiplied, looped, tick = (sc.sem(n) for n in ("hots_ready", "multiplied", "looped", "tick"))
        x_all = sc.sb("x_all", [P, NODE_TILES, D])
        x_loaded, chain_sem = sc.sem("x_loaded"), sc.sem("chain")
        scale = PowerScale(sc, keep["x_scale"][:, :])
        block = sc.block()

        @block.sync
        def _(sp):
            sp.dma_start(x_all[:, :, :], io["x"].rearrange("(t p) f -> p t f", p=P)).then_inc(x_loaded, 16)

        @block.gpsimd
        def _(pool):
            scale.on_pool(nc, pool)

        @block.vector
        def _(dve):
            adj = keep["adj"]
            chain = Chain(dve, chain_sem)
            def one_hots(k):
                nc.vector.tensor_scalar(col_hot[:, k % GROUP, :], keep["iota"][:, 0:NODE_TILES * BUILD_W], now[:, k, 1:2],
                                        None, ALU.is_equal).then_inc(hots_ready, 1)

            nc.vector.tensor_copy(now[:, 0:GROUP, :], keep["cells"][:, 0:GROUP, :]).then_inc(second, ROUND // 2)
            dve.wait_ge(second, ROUND // 2)
            for k in range(GROUP):
                one_hots(k)
            with dve.Fori(0, BUILD_STEPS // ROUND) as i:
                _, columns = nc.values_load_multi_w_load_instructions(
                    keep["window"][0:1, bass.ds(i * ROUND, ROUND)], engines=[mybir.EngineType.DVE], min_val=0,
                    max_val=NODES_P - BUILD_W,
                    skip_runtime_bounds_check_because="the columns are the chip's own, held to the last window")
                dve.wait_ge(hots_ready, i * ROUND + GROUP)
                nc.vector.tensor_copy(now[:, :, :], keep["cells"][:, bass.ds(i * ROUND + GROUP, ROUND), :]).wait_op(
                    second, ROUND // 2, "sem-ge").then_inc(first, 1)
                for k in range(ROUND):
                    at = adj[:, :, bass.ds(columns[k], BUILD_W)]
                    if k % 4 == 0:
                        dve.wait_ge(multiplied, i * ROUND + k + 4 + 16)
                    if k == 5:
                        dve.wait_ge(first, 1)
                        dve.sem_clear(second)
                    if k == ROUND // 2 + 5:
                        dve.wait_ge(second, 1)
                        dve.sem_clear(first)
                    before, count = (first, k + 1) if k <= ROUND // 2 else (second, k - ROUND // 2)
                    nc.vector.tensor_tensor(at, at, part[:, k % GROUP, 0:NODE_TILES * BUILD_W].rearrange(
                        "p (s w) -> p s w", w=BUILD_W), ALU.add).wait_op(
                            before, count, "sem-ge").then_inc(first if k < ROUND // 2 else second, 1)
                    one_hots(k)
            dve.wait_ge(second, ROUND // 2)
            dve.wait_ge(x_loaded, 16)
            chain(nc.vector.tensor_reduce(scale.peak[:, :], x_all[:, :, :], AX.XY, ALU.max, apply_absolute_value=True))
            nc.vector.nop().then_inc(scale.peaked, 1)
            change_loops(nc, keep, ALU.add, looped)
            scale.on_vector(nc, dve, chain)

        @block.scalar
        def _(act):
            rows.on_scalar(nc, act, keep, keep["cells"], BUILD_STEPS, multiplied)

        @block.tensor
        def _(pe):
            pe.sem_inc(multiplied, 16)
            with pe.Fori(0, BUILD_STEPS // 16) as i:
                for k in range(16):
                    if k % 8 == 0:
                        pe.wait_ge(rows.ready, i * 2 + k // 8 + 3)
                        pe.sem_inc(tick, 1)
                    pe.wait_ge(hots_ready, i * 16 + k + 1)
                    nc.tensor.matmul(part[:, k % GROUP, 0:NODE_TILES * BUILD_W], rows.hot[:, k, :],
                                     col_hot[:, k % GROUP, :], start=True, stop=True).then_inc(multiplied, 1)


def aggregate(nc, io, keep, name, source, scaled=False, relations=False, save=False, restore=False, scales=None):
    SLOTS = 5
    with Scope(nc, name) as sc:
        grow, shrink = (NORMED_SCALE, 1.0 / NORMED_SCALE) if scales is None else (scales[:, 0:1], scales[:, 1:2])
        parts = sc.sb("parts", [P, NODE_TILES, 2, D], F16)
        raw = sc.sb("raw", [P, SLOTS, D])
        staged = sc.sb("staged", [P, HALF, CHUNK])
        ps = sc.ps("sums", [P, 2, HALF, 512])
        if relations:
            counts = sc.sb("counts", [RELS, CHUNK])
            vectors = sc.sb("vectors", [RELS, D])
            rel_loaded, vec_loaded, looped = sc.sem("rel_loaded"), sc.sem("vec_loaded"), sc.sem("looped")
        loaded = sc.sems("loaded", SLOTS)
        prepared, high_done, low_done, summed, out0, out1, free, tick = (
            sc.sem(n) for n in ("prepared", "high_done", "low_done", "summed", "out0",
                                "out1", "free", "tick"))
        stored = sc.sems("stored", HALF)
        saved, restored = sc.sem("saved"), sc.sem("restored")
        block = sc.block()
        adj = keep["adj"]
        rows = source.rearrange("(t p) f -> t p f", p=P)

        @block.sync
        def _(sp):
            for k in range(SLOTS):
                sp.dma_start(raw[:, k, :], rows[k]).then_inc(loaded[k], 16)
            if relations:
                sp.dma_start(vectors[:, :], io["relvectors"]).then_inc(vec_loaded, 16)
            with sp.Fori(1, NODE_TILES // SLOTS) as i:
                for k in range(SLOTS):
                    sp.wait_ge(low_done, (i - 1) * SLOTS + k + 1)
                    sp.dma_start(raw[:, k, :], source[bass.ds((i * SLOTS + k) * P, P), :]).then_inc(loaded[k], 16)
            def move_chunk(c):
                if relations:
                    sp.wait_ge(summed, c + 1)
                    sp.dma_start(counts[:, :], io["rel_counts"][:, bass.ds(c * CHUNK, CHUNK)]).then_inc(rel_loaded, 16)
                for h, out in enumerate((out0, out1)):
                    sp.wait_ge(out, c + 3)
                    sp.dma_start(io["agg_t"][h, :, bass.ds(c * CHUNK, CHUNK)], staged[:, h, :]).then_inc(stored[h], 16)
                if save:
                    columns = bass.ds(c * CHUNK, CHUNK)
                    sp.dma_start(io["adj_copy"][:, :, columns], adj[:, :, columns]).then_inc(saved, 16)
                for h in range(HALF):
                    sp.wait_ge(stored[h], (c + 1) * 16)
                sp.sem_inc(free, 1)

            if restore:
                def bring_back(chunk):
                    columns = bass.ds(chunk * CHUNK, CHUNK)
                    sp.dma_start(adj[:, :, columns], io["adj_copy"][:, :, columns]).then_inc(restored, 16)

                bring_back(RESTORED)
                with sp.Fori(0, CHUNKS - RESTORED - 1) as c:
                    sp.wait_ge(restored, (c + 2) * 16)
                    sp.sem_inc(tick, 1)
                    bring_back(c + RESTORED + 1)
                    move_chunk(c)
                with sp.Fori(CHUNKS - RESTORED - 1, CHUNKS) as c:
                    move_chunk(c)
            else:
                with sp.Fori(0, CHUNKS) as c:
                    move_chunk(c)
            if save:
                sp.wait_ge(saved, 16 * CHUNKS)

        @block.vector
        def _(dve):
            if relations:
                change_loops(nc, keep, ALU.subtract, looped)
                dve.wait_ge(vec_loaded, 16)
                nc.vector.tensor_scalar(vectors[:, :], vectors[:, :], NORMED_SCALE, None, ALU.mult).then_inc(looped, 1)
            with dve.Fori(0, NODE_TILES // SLOTS) as i:
                for k in range(SLOTS):
                    dve.wait_ge(loaded[k], i * 16 + 16)
                    if scaled:
                        nc.vector.tensor_scalar(raw[:, k, :], raw[:, k, :],
                                                keep["dinv"][:, bass.ds(i * SLOTS + k, 1)], grow,
                                                ALU.mult, ALU.mult).then_inc(prepared, 1)
                    else:
                        nc.vector.tensor_scalar(raw[:, k, :], raw[:, k, :], grow, None, ALU.mult).then_inc(prepared, 1)
                for k in range(SLOTS):
                    dve.wait_ge(high_done, i * SLOTS + k + 1)
                    both = parts[:, bass.ds(i * SLOTS + k, 1), :, :].rearrange("p a b f -> p (a b) f")
                    nc.vector.tensor_tensor(both[:, 1, :], raw[:, k, :], both[:, 0, :], ALU.subtract).then_inc(low_done, 1)
            with dve.Fori(0, CHUNKS // 2) as j:
                for par in range(2):
                    dve.wait_ge(free, j * 2 + par + 1)
                    dve.wait_ge(summed, j * 2 + par + 2)
                    nc.vector.tensor_scalar(staged[:, 1, :], ps[:, par, 1, 0:CHUNK], shrink, None,
                                            ALU.mult).then_inc(out1, 1)

        @block.scalar
        def _(act):
            act.sem_inc(out0, 2)
            act.sem_inc(out1, 2)
            act.sem_inc(free, 1)
            act.sem_inc(summed, 1)
            with act.Fori(0, NODE_TILES // SLOTS) as i:
                for k in range(SLOTS):
                    act.wait_ge(prepared, i * SLOTS + k + 1)
                    act.sem_inc(tick, 1)
                    nc.scalar.activation(parts[:, bass.ds(i * SLOTS + k, 1), 0, :].rearrange("p a f -> p (a f)"),
                                         raw[:, k, :], ACT.Copy).then_inc(high_done, 1)
            with act.Fori(0, CHUNKS // 2) as j:
                for par in range(2):
                    act.wait_ge(free, j * 2 + par + 1)
                    act.sem_inc(tick, 1)
                    act.wait_ge(summed, j * 2 + par + 2)
                    nc.scalar.activation(staged[:, 0, :], ps[:, par, 0, 0:CHUNK], ACT.Identity,
                                         scale=shrink).then_inc(out0, 1)

        @block.tensor
        def _(pe):
            if relations:
                pe.wait_ge(looped, 3)

            def sum_chunk_pair(j):
                for par in range(2):
                    pe.wait_ge(out0, j * 2 + par + 1)
                    pe.sem_inc(tick, 1)
                    pe.wait_ge(out1, j * 2 + par + 1)
                    pe.sem_inc(tick, 1)
                    for s in range(NODE_TILES):
                        pe.wait_ge(low_done, s + 1)
                        for h in range(HALF):
                            for part in range(2):
                                last = nc.tensor.matmul(ps[:, par, h, 0:CHUNK], parts[:, s, part, h * P:(h + 1) * P],
                                                        adj[:, s, bass.ds((j * 2 + par) * CHUNK, CHUNK)],
                                                        start=(s == 0 and part == 0),
                                                        stop=(s == NODE_TILES - 1 and part == 1 and not relations))
                    if relations:
                        pe.wait_ge(rel_loaded, (j * 2 + par + 1) * 16)
                        pe.sem_inc(tick, 1)
                        for h in range(HALF):
                            last = nc.tensor.matmul(ps[:, par, h, 0:CHUNK], vectors[:, h * P:(h + 1) * P],
                                                    counts[:, :], start=False, stop=True)
                    last.then_inc(summed, 1)

            if restore:
                pe.sem_inc(restored, 16)
            with pe.Fori(0, CHUNKS // 2) as j:
                if restore:
                    pe.wait_ge(restored, j * 32 + 16)
                    pe.sem_inc(tick, 1)
                sum_chunk_pair(j)


SLOTS = 5
ROUNDS = NODE_TILES // SLOTS


def each(engine, i, waits, emit, done, tick=None):
    for k in range(SLOTS):
        for w in waits:
            engine.wait_ge(w, i * SLOTS + k + 1)
            if tick is not None:
                engine.sem_inc(tick, 1)
        emit(k).then_inc(done, 1)


def load_slots(sp, loads, loaded):
    for k in range(SLOTS):
        for to, source, _, _ in loads:
            sp.dma_start(to(k), source(k)).then_inc(loaded[k], 16)
    with sp.Fori(1, ROUNDS) as i:
        for to, source, free, ahead in loads:
            for k in range(SLOTS):
                sp.wait_ge(free, (i - 1) * SLOTS + k + 1 + ahead)
                sp.dma_start(to(k), source(i * SLOTS + k)).then_inc(loaded[k], 16)


def tile_rows(a):
    return lambda t: a[bass.ds(t * P, P), :]


class Norm:

    def __init__(self, sc):
        self.stats = sc.sb("stats", [P, SLOTS, 6])
        self.mean_var = sc.sb("mean_var", [P, SLOTS, 2])
        self.spread = sc.sb("spread", [P, SLOTS])
        self.inverse = sc.sb("inverse", [P, SLOTS])
        self.power = sc.sb("power", [P, SLOTS])
        (self.stat_done, self.mean_done, self.spread_done, self.inverse_done, self.power_set,
         self.tick) = (sc.sem(n) for n in ("stat_done", "mean_done", "spread_done", "inverse_done", "power_set",
                                           "norm_tick"))

    def statistics(self, nc, dve, i, between=None):
        each(dve, i, [self.stat_done], lambda k: nc.vector.bn_aggr(self.mean_var[:, k, :], self.stats[:, k, :]),
             self.mean_done, self.tick)
        dve.wait_ge(self.mean_done, i * SLOTS + SLOTS)
        nc.vector.tensor_scalar(self.spread[:, :], self.mean_var[:, :, 1], LN_EPS, None,
                                ALU.add).then_inc(self.spread_done, 1)
        if between is not None:
            between()
        dve.wait_ge(self.inverse_done, i + 1)

    def on_vector(self, nc, dve, i, y, before, out, done, between=None):
        each(dve, i, [before], lambda k: nc.vector.bn_stats(self.stats[:, k, :], y(k)), self.stat_done)
        self.statistics(nc, dve, i, between)
        for k in range(SLOTS):
            nc.vector.tensor_scalar(out(k), y(k), self.mean_var[:, k, 0:1], self.inverse[:, k:k + 1], ALU.subtract,
                                    ALU.mult).then_inc(done, 1)

    def set_power(self, nc, pool):
        nc.gpsimd.memset(self.power[:, :], -0.5).then_inc(self.power_set, 1)
        pool.wait_ge(self.power_set, 1)

    def on_pool(self, nc, pool, i):
        pool.wait_ge(self.spread_done, i + 1)
        nc.gpsimd.tensor_tensor(self.inverse[:, :], self.spread[:, :], self.power[:, :],
                                ALU.pow).then_inc(self.inverse_done, 1)


def round_rows(a, i):
    return a[bass.ds(i * (SLOTS * P), SLOTS * P), :].rearrange("(k p) f -> p k f", p=P)


def finish_rounds(nc, pool, norm, stores, ready, ahead, stored, tick, norm_ahead=False):
    if norm:
        norm.set_power(nc, pool)
    if norm_ahead:
        norm.on_pool(nc, pool, 0)
    with pool.Fori(0, ROUNDS - 1 if norm_ahead else ROUNDS) as i:
        if norm:
            norm.on_pool(nc, pool, i + 1 if norm_ahead else i)
        pool.wait_ge(ready, i * SLOTS + SLOTS + ahead)
        pool.sem_inc(tick, 1)
        for dest, what in stores:
            pool.dma_start(round_rows(dest, i), what(i)).then_inc(stored, 16)
    if norm_ahead:
        pool.wait_ge(ready, ROUNDS * SLOTS + ahead)
        for dest, what in stores:
            pool.dma_start(round_rows(dest, ROUNDS - 1), what(ROUNDS - 1)).then_inc(stored, 16)
    pool.wait_ge(stored, 16 * len(stores) * ROUNDS)


def agg_tiles(io):
    return lambda t: io["agg_t"][:, :, bass.ds(t * P, P)].rearrange("h p n -> p h n")


def gcn_update(nc, io, keep, name, weight, bias, dest, residual=None, relu=True, scales=None):
    with Scope(nc, name) as sc:
        w = sc.sb("w", [P, HALF, D])
        b = sc.sb("b", [P, D])
        agg = sc.sb("agg", [P, SLOTS, HALF, P])
        y = sc.sb("y", [P, SLOTS, D])
        result = sc.sb("result", [P, NODE_TILES, D])
        ps = sc.ps("ps", [P, SLOTS, 512])
        norm = Norm(sc) if residual is not None else None
        x = sc.sb("x", [P, SLOTS, D]) if norm else None
        loaded = sc.sems("loaded", SLOTS)
        consts, multiplied, biased, activated, ready, stored, tick = (
            sc.sem(n) for n in ("consts", "multiplied", "biased", "activated", "ready", "stored", "tick"))
        if scales is not None:
            scale = PowerScale(sc, scales)
            peaks = sc.sb("peaks", [P, ROUNDS])
            chain_sem, round_peak = sc.sem("chain"), sc.sem("round_peak")
        block = sc.block()
        dinv = lambda i, k: keep["dinv"][:, bass.ds(i * SLOTS + k, 1)]
        out = lambda i, k: result[:, bass.ds(i * SLOTS + k, 1), :].rearrange("p a f -> p (a f)")
        loads = [(lambda k: agg[:, k, :, :], agg_tiles(io), multiplied, 0)]
        if norm:
            loads.append((lambda k: x[:, k, :], tile_rows(residual), activated, 0))

        @block.sync
        def _(sp):
            sp.dma_start(w[:, :, :], weight.rearrange("(h p) n -> p h n", p=P)).then_inc(consts, 16)
            sp.dma_start(b[:, :], bias).then_inc(consts, 16)
            load_slots(sp, loads, loaded)

        @block.tensor
        def _(pe):
            pe.wait_ge(consts, 32)
            with pe.Fori(0, ROUNDS) as i:
                for k in range(SLOTS):
                    pe.wait_ge(loaded[k], i * (16 * len(loads)) + 16 * len(loads))
                    pe.sem_inc(tick, 1)
                    pe.wait_ge(biased, i * SLOTS + k + 1)
                    pe.sem_inc(tick, 1)
                    for h in range(HALF):
                        last = nc.tensor.matmul(ps[:, k, 0:D], agg[:, k, h, :], w[:, h, :], start=(h == 0),
                                                stop=(h == HALF - 1))
                    last.then_inc(multiplied, 1)

        @block.vector
        def _(dve):
            dve.sem_inc(ready, SLOTS)
            dve.sem_inc(biased, SLOTS)
            dve.wait_ge(consts, 32)
            with dve.Fori(0, ROUNDS) as i:
                each(dve, i, [multiplied, ready], lambda k: nc.vector.scalar_tensor_tensor(
                    y[:, k, :], ps[:, k, 0:D], dinv(i, k), b[:, :], ALU.mult, ALU.add), biased)
                for k in range(SLOTS):
                    dve.wait_ge(biased, i * SLOTS + k + 1 + SLOTS)
                    if norm is None:
                        nc.vector.tensor_scalar(out(i, k), y[:, k, :], 0.0, dinv(i, k), ALU.max,
                                                ALU.mult).then_inc(ready, 1)
                    elif relu:
                        nc.vector.scalar_tensor_tensor(y[:, k, :], y[:, k, :], 0.0, x[:, k, :], ALU.max,
                                                       ALU.add).then_inc(activated, 1)
                    else:
                        nc.vector.tensor_tensor(y[:, k, :], y[:, k, :], x[:, k, :], ALU.add).then_inc(activated, 1)
                if scales is not None:
                    dve.wait_ge(ready, i * SLOTS + 2 * SLOTS)
                    nc.vector.reduce_max(peaks[:, bass.ds(i, 1)], result[:, bass.ds(i * SLOTS, SLOTS), :],
                                         axis=AX.XY).then_inc(round_peak, 1)
                if norm is not None:
                    norm.on_vector(nc, dve, i, lambda k: y[:, k, :], activated, lambda k: out(i, k), ready)

            if scales is not None:
                chain = Chain(dve, chain_sem)
                dve.wait_ge(round_peak, ROUNDS)
                chain(nc.vector.reduce_max(scale.peak[:, :], peaks[:, :], axis=AX.X))
                nc.vector.nop().then_inc(scale.peaked, 1)
                scale.on_vector(nc, dve, chain)

        @block.gpsimd
        def _(pool):
            finish_rounds(nc, pool, norm, [(dest, lambda i: result[:, bass.ds(i * SLOTS, SLOTS), :])], ready, SLOTS,
                          stored, tick)
            if scales is not None:
                scale.on_pool(nc, pool)


def gru_update(nc, io, keep):
    PS = 3
    with Scope(nc, "gru") as sc:
        w_in = sc.sb("w_in", [P, HALF, 3 * D])
        w_hid = sc.sb("w_hid", [P, HALF, 3 * D])
        b_in = sc.sb("b_in", [P, 3 * D])
        b_hid = sc.sb("b_hid", [P, 3 * D])
        gate_bias = sc.sb("gate_bias", [P, 4 * D])
        agg = sc.sb("agg", [P, SLOTS, HALF, P])
        x_in_rows = sc.sb("x_in_rows", [P, SLOTS, D])
        x = sc.sb("x", [P, SLOTS, D])
        x_t = sc.sb("x_t", [P, SLOTS, HALF, P])
        gates = sc.sb("gates", [P, SLOTS, 2 * D])
        y = sc.sb("y", [P, SLOTS, D])
        turned_ps = sc.ps("turned_ps", [P, 2, 512])
        ps = sc.ps("ps", [P, PS, 2, 512])
        norm = Norm(sc)
        result = sc.sb("result", [P, NODE_TILES, D])
        agg_in, rows_in, x_in = sc.sems("agg_in", SLOTS), sc.sems("rows_in", SLOTS), sc.sems("x_in", SLOTS)
        (consts, turned, x_ready, multiplied, taken, new_taken, gated, reset, summed, tanned, kept, mixed, grown,
         added, ready, tick, own_sem, stored) = (sc.sem(n) for n in (
             "consts", "turned", "x_ready", "multiplied", "taken", "new_taken", "gated", "reset", "summed",
             "tanned", "kept", "mixed", "grown", "added", "ready", "tick", "own", "stored"))
        news = sc.sb("news", [P, SLOTS, 2 * D])
        block = sc.block()

        @block.sync
        def _(sp):
            for to, source in ((w_in, io["w_in"]), (w_hid, io["w_hid"])):
                sp.dma_start(to[:, :, :], source.rearrange("(h p) n -> p h n", p=P)).then_inc(consts, 16)
            sp.dma_start(b_in[:, :], io["b_in"]).then_inc(consts, 16)
            sp.dma_start(b_hid[:, :], io["b_hid"]).then_inc(consts, 16)
            for k in range(SLOTS):
                sp.dma_start(x_in_rows[:, k, :], tile_rows(io["x1"])(k)).then_inc(rows_in[k], 16)
                sp.dma_start(agg[:, k, :, :], agg_tiles(io)(k)).then_inc(agg_in[k], 16)
            for k in range(SLOTS):
                sp.dma_start(x[:, k, :], tile_rows(io["x1"])(k)).then_inc(x_in[k], 16)
            with sp.Fori(1, ROUNDS) as i:
                for k in range(SLOTS):
                    sp.wait_ge(turned, (i - 1) * SLOTS + k + 1)
                    sp.sem_inc(tick, 1)
                    sp.dma_start(x_in_rows[:, k, :],
                                 tile_rows(io["x1"])(i * SLOTS + k)).then_inc(rows_in[k], 16)
                    sp.wait_ge(multiplied, (i - 1) * SLOTS + k + 1)
                    sp.sem_inc(tick, 1)
                    sp.dma_start(agg[:, k, :, :], agg_tiles(io)(i * SLOTS + k)).then_inc(agg_in[k], 16)
                for k in range(SLOTS):
                    sp.wait_ge(added, (i - 1) * SLOTS + k + 1)
                    sp.sem_inc(tick, 1)
                    sp.dma_start(x[:, k, :], tile_rows(io["x1"])(i * SLOTS + k)).then_inc(x_in[k], 16)

        @block.tensor
        def _(pe):
            pe.wait_ge(consts, 64)
            def turn(i, k):
                pe.wait_ge(rows_in[k], i * 16 + 16)
                pe.sem_inc(tick, 1)
                pe.wait_ge(x_ready, i * SLOTS + k + (2 if k == 0 else 1))
                pe.sem_inc(tick, 1)
                for h in range(HALF):
                    last = nc.tensor.transpose(turned_ps[:, k % 2, h * P:(h + 1) * P], x_in_rows[:, k, h * P:(h + 1) * P],
                                               keep["ident"][:, :])
                last.then_inc(turned, 1)

            with pe.Fori(0, ROUNDS) as i:
                turn(i, 0)
                for k in range(SLOTS):
                    if k + 1 < SLOTS:
                        turn(i, k + 1)
                    back = PS if k >= PS else (SLOTS if k >= SLOTS - PS else SLOTS - PS)
                    pe.wait_ge(new_taken, i * SLOTS + k + 1 + SLOTS - back)
                    pe.sem_inc(tick, 1)
                    pe.wait_ge(agg_in[k], i * 16 + 16)
                    pe.sem_inc(tick, 1)
                    for n, h in enumerate(range(HALF)):
                        nc.tensor.matmul(ps[:, k % PS, 0, 0:2 * D], agg[:, k, h, :], w_in[:, h, 0:2 * D],
                                         start=(n == 0), stop=False)
                    for h in range(HALF):
                        nc.tensor.matmul(ps[:, k % PS, 1, 0:D], agg[:, k, h, :], w_in[:, h, 2 * D:3 * D],
                                         start=(h == 0), stop=(h == 1))
                    pe.wait_ge(x_ready, i * SLOTS + k + 3)
                    pe.sem_inc(tick, 1)
                    for h in range(HALF):
                        nc.tensor.matmul(ps[:, k % PS, 0, 0:2 * D], x_t[:, k, h, :], w_hid[:, h, 0:2 * D],
                                         start=False, stop=(h == 1))
                    for h in range(HALF):
                        last = nc.tensor.matmul(ps[:, k % PS, 1, D:2 * D], x_t[:, k, h, :], w_hid[:, h, 2 * D:3 * D],
                                                start=(h == 0), stop=(h == 1))
                    last.then_inc(multiplied, 1)

        @block.scalar
        def _(act):
            act.sem_inc(x_ready, 2)

            def copy_turned(i, k):
                act.wait_ge(new_taken, i * SLOTS + k + 1)
                act.sem_inc(tick, 1)
                act.wait_ge(turned, i * SLOTS + k + 1)
                nc.scalar.activation(x_t[:, k, :, :].rearrange("p h n -> p (h n)"), turned_ps[:, k % 2, 0:D],
                                     ACT.Copy).then_inc(x_ready, 1)

            def sigmoids(i):
                each(act, i, [taken], lambda k: nc.scalar.activation(gates[:, k, :], gates[:, k, :], ACT.Sigmoid), gated)

            def tanhs(i):
                each(act, i, [summed], lambda k: nc.scalar.activation(news[:, k, 0:D], news[:, k, 0:D], ACT.Tanh), tanned)

            for k in range(SLOTS):
                copy_turned(0, k)
            with act.Fori(0, ROUNDS - 1) as i:
                copy_turned(i + 1, 0)
                sigmoids(i)
                copy_turned(i + 1, 1)
                tanhs(i)
                for k in range(2, SLOTS):
                    copy_turned(i + 1, k)
            sigmoids(ROUNDS - 1)
            tanhs(ROUNDS - 1)

        @block.vector
        def _(dve):
            own = Chain(dve, own_sem)
            dve.sem_inc(new_taken, SLOTS)
            dve.sem_inc(ready, SLOTS)
            dve.wait_ge(consts, 64)
            own(nc.vector.tensor_tensor(gate_bias[:, 0:2 * D], b_in[:, 0:2 * D], b_hid[:, 0:2 * D], ALU.add))
            own(nc.vector.tensor_copy(gate_bias[:, 2 * D:3 * D], b_in[:, 2 * D:3 * D]))
            own(nc.vector.tensor_copy(gate_bias[:, 3 * D:4 * D], b_hid[:, 2 * D:3 * D]))

            def take(i, tiles):
                for k in tiles:
                    dve.wait_ge(multiplied, i * SLOTS + k + 1)
                    nc.vector.tensor_tensor(gates[:, k, :], ps[:, k % PS, 0, :], gate_bias[:, 0:2 * D],
                                            ALU.add).then_inc(taken, 1)
                    nc.vector.tensor_tensor(news[:, k, :], ps[:, k % PS, 1, :], gate_bias[:, 2 * D:4 * D],
                                            ALU.add).then_inc(new_taken, 1)

            def update(i, between=None):
                take(i, range(2, SLOTS))
                dve.wait_ge(new_taken, i * SLOTS + 2 * SLOTS)
                each(dve, i, [gated], lambda k: nc.vector.tensor_tensor(
                    news[:, k, D:2 * D], news[:, k, D:2 * D], gates[:, k, 0:D], ALU.mult), reset)
                each(dve, i, [reset], lambda k: nc.vector.tensor_tensor(
                    news[:, k, 0:D], news[:, k, 0:D], news[:, k, D:2 * D], ALU.add), summed)
                for k in range(SLOTS):
                    dve.wait_ge(x_in[k], i * 16 + 16)
                dve.wait_ge(ready, i * SLOTS + SLOTS)
                each(dve, i, [tanned], lambda k: nc.vector.tensor_tensor(
                    y[:, k, :], x[:, k, :], news[:, k, 0:D], ALU.subtract), kept)
                each(dve, i, [kept], lambda k: nc.vector.tensor_tensor(
                    y[:, k, :], y[:, k, :], gates[:, k, D:2 * D], ALU.mult), mixed)
                each(dve, i, [mixed], lambda k: nc.vector.tensor_tensor(
                    y[:, k, :], y[:, k, :], news[:, k, 0:D], ALU.add), grown)
                each(dve, i, [grown], lambda k: nc.vector.tensor_tensor(
                    y[:, k, :], y[:, k, :], x[:, k, :], ALU.add), added)
                norm.on_vector(nc, dve, i, lambda k: y[:, k, :], added, lambda k: result[
                    :, bass.ds(i * SLOTS + k, 1), :].rearrange("p a f -> p (a f)"), ready, between)

            take(0, range(0, 2))
            with dve.Fori(0, ROUNDS - 1) as i:
                update(i, lambda: take(i + 1, range(0, 2)))
            update(ROUNDS - 1)

        @block.gpsimd
        def _(pool):
            finish_rounds(nc, pool, norm, [(io["x2"], lambda i: result[:, bass.ds(i * SLOTS, SLOTS), :])], ready, SLOTS,
                          stored, tick)


def attention_inputs(nc, io, keep):
    with Scope(nc, "qkv") as sc:
        w = sc.sb("w", [P, HALF, 3 * D])
        b = sc.sb("b", [P, 3 * D])
        gain = sc.sb("gain", [P, D])
        shift = sc.sb("shift", [P, D])
        x = sc.sb("x", [P, SLOTS, D])
        y = sc.sb("y", [P, SLOTS, D])
        x_t = sc.sb("x_t", [P, SLOTS, HALF, P])
        result = sc.sb("result", [P, NODE_TILES, 2 * D])
        q = keep["q"]
        scale = PowerScale(sc, keep["q_scale"][:, :])
        peaks = sc.sb("peaks", [P, ROUNDS])
        chain_sem, round_peak = sc.sem("chain"), sc.sem("round_peak")
        turned_ps = sc.ps("turned_ps", [P, 2, 512])
        ps = sc.ps("ps", [P, 3, 2, 512])
        norm = Norm(sc)
        loaded, stored = sc.sems("loaded", SLOTS), sc.sem("stored")
        consts, normed, gained, shifted, turned, x_ready, multiplied, ready, tick = (
            sc.sem(n) for n in ("consts", "normed", "gained", "shifted", "turned", "x_ready", "multiplied", "ready",
                                "tick"))
        block = sc.block()
        PS = 3

        @block.sync
        def _(sp):
            sp.dma_start(w[:, :, :], io["w_qkv"].rearrange("(h p) n -> p h n", p=P)).then_inc(consts, 16)
            sp.dma_start(b[:, :], io["b_qkv"]).then_inc(consts, 16)
            sp.dma_start(gain[:, :], io["ln_g"]).then_inc(consts, 16)
            sp.dma_start(shift[:, :], io["ln_b"]).then_inc(consts, 16)
            load_slots(sp, [(lambda k: x[:, k, :], tile_rows(io["x2"]), normed, 0)], loaded)

        @block.vector
        def _(dve):
            dve.sem_inc(ready, SLOTS)
            dve.wait_ge(consts, 64)

            def statistics(i):
                for k in range(SLOTS):
                    dve.wait_ge(loaded[k], i * 16 + 16)
                    nc.vector.bn_stats(norm.stats[:, k, :], x[:, k, :]).then_inc(norm.stat_done, 1)
                norm.statistics(nc, dve, i)

            def normalise(i, k):
                nc.vector.tensor_scalar(y[:, k, :], x[:, k, :], norm.mean_var[:, k, 0:1],
                                        norm.inverse[:, k:k + 1], ALU.subtract, ALU.mult).then_inc(normed, 1)
                dve.wait_ge(normed, i * SLOTS + k + 1)
                nc.vector.tensor_tensor(y[:, k, :], y[:, k, :], gain[:, :], ALU.mult).then_inc(gained, 1)
                dve.wait_ge(gained, i * SLOTS + k + 1)
                nc.vector.tensor_tensor(y[:, k, :], y[:, k, :], shift[:, :], ALU.add).then_inc(shifted, 1)

            def take(i, k):
                dve.wait_ge(multiplied, i * SLOTS + k + 1)
                tile = bass.ds(i * SLOTS + k, 1)
                nc.vector.tensor_tensor(q[:, tile, :].rearrange("p a f -> p (a f)"), ps[:, k % PS, 0, 0:D],
                                        b[:, 0:D], ALU.add)
                nc.vector.tensor_tensor(result[:, tile, :].rearrange("p a f -> p (a f)"), ps[:, k % PS, 1, :],
                                        b[:, D:3 * D], ALU.add).then_inc(ready, 1)

            def peak_of_round(i):
                dve.wait_ge(ready, i * SLOTS + 2 * SLOTS)
                nc.vector.tensor_reduce(peaks[:, bass.ds(i, 1)], q[:, bass.ds(i * SLOTS, SLOTS), :], AX.XY, ALU.max,
                                        apply_absolute_value=True).then_inc(round_peak, 1)

            statistics(0)
            for k in range(SLOTS):
                normalise(0, k)
            with dve.Fori(0, ROUNDS - 1) as i:
                statistics(i + 1)
                for k in range(SLOTS):
                    take(i, k)
                    dve.wait_ge(turned, i * SLOTS + k + 1)
                    normalise(i + 1, k)
                peak_of_round(i)
            for k in range(SLOTS):
                take(ROUNDS - 1, k)
            peak_of_round(ROUNDS - 1)
            chain = Chain(dve, chain_sem)
            dve.wait_ge(round_peak, ROUNDS)
            chain(nc.vector.reduce_max(scale.peak[:, :], peaks[:, :], axis=AX.X))
            nc.vector.nop().then_inc(scale.peaked, 1)
            scale.on_vector(nc, dve, chain)

        @block.tensor
        def _(pe):
            def turn(i, k):
                pe.wait_ge(shifted, i * SLOTS + k + 1)
                pe.sem_inc(tick, 1)
                pe.wait_ge(x_ready, i * SLOTS + k + (2 if k == 0 else 1))
                pe.sem_inc(tick, 1)
                for h in range(HALF):
                    last = nc.tensor.transpose(turned_ps[:, k % 2, h * P:(h + 1) * P], y[:, k, h * P:(h + 1) * P],
                                               keep["ident"][:, :])
                last.then_inc(turned, 1)

            with pe.Fori(0, ROUNDS) as i:
                turn(i, 0)
                for k in range(SLOTS):
                    if k + 1 < SLOTS:
                        turn(i, k + 1)
                    back = PS if k >= PS else (SLOTS if k >= SLOTS - PS else SLOTS - PS)
                    pe.wait_ge(ready, i * SLOTS + k + 1 + SLOTS - back)
                    pe.sem_inc(tick, 1)
                    pe.wait_ge(x_ready, i * SLOTS + k + 3)
                    pe.sem_inc(tick, 1)
                    for h in range(HALF):
                        nc.tensor.matmul(ps[:, k % PS, 0, 0:D], x_t[:, k, h, :], w[:, h, 0:D], start=(h == 0),
                                         stop=(h == 1))
                    for h in range(HALF):
                        last = nc.tensor.matmul(ps[:, k % PS, 1, :], x_t[:, k, h, :], w[:, h, D:3 * D],
                                                start=(h == 0), stop=(h == 1))
                    last.then_inc(multiplied, 1)

        @block.scalar
        def _(act):
            act.sem_inc(x_ready, 2)
            act.wait_ge(consts, 64)
            with act.Fori(0, ROUNDS) as i:
                for k in range(SLOTS):
                    act.wait_ge(ready, i * SLOTS + k + 1)
                    act.sem_inc(tick, 1)
                    act.wait_ge(turned, i * SLOTS + k + 1)
                    nc.scalar.activation(x_t[:, k, :, :].rearrange("p h n -> p (h n)"), turned_ps[:, k % 2, 0:D],
                                         ACT.Copy).then_inc(x_ready, 1)

        @block.gpsimd
        def _(pool):
            finish_rounds(nc, pool, norm, [(io["kv"], lambda i: result[:, bass.ds(i * SLOTS, SLOTS), :])],
                          ready, SLOTS, stored, tick, norm_ahead=True)
            scale.on_pool(nc, pool)


def attention_edges(nc, io, keep):
    G = 4
    U = 2 * G
    with Scope(nc, "edges") as outer:
        spots = outer.sb("spots", [P, EDGE_STEPS, 3])
        cutoff = outer.sb("cutoff", [P, EDGE_STEPS])
        src_row = outer.sb("src_row", [P, EDGE_STEPS], I32)
        column = outer.sb("column", [1, EDGE_STEPS], I32)
        window = outer.sb("window", [1, EDGE_STEPS], I32)
        q_parts = outer.sb("q_parts", [P, NODE_TILES, 2, D], F16)
        partition = outer.sb("partition", [P, 1])
        angle, sine, high_done, numbered = (outer.sem(n) for n in ("angle", "sine", "high_done", "numbered"))

        def kept(sc, dve, own, cols, step_no, width):
            src, dst, tile, weight = (c[0] for c in cols)
            under = sc.sb("under", [P, width])
            own(nc.vector.tensor_copy(src_row[:, :], src))
            own(nc.vector.tensor_scalar(column[0:1, :], tile[0:1, :], float(P), None, ALU.mult))
            own(nc.vector.tensor_tensor(cutoff[:, :], step_no[:, :], tile, ALU.subtract))
            own(nc.vector.tensor_copy(window[0:1, :], cutoff[0:1, :]))
            own(nc.vector.scalar_tensor_tensor(spots[:, :, 0], cutoff[:, :], -float(P), dst, ALU.mult, ALU.add))
            own(nc.vector.tensor_scalar(under[:, :], weight, 5.0, None, ALU.is_lt))
            own(nc.vector.tensor_scalar(cutoff[:, :], weight, 5.0, 0.0, ALU.min, ALU.max))
            own(nc.vector.tensor_scalar(cutoff[:, :], cutoff[:, :], -float(np.pi) / 5.0, float(np.pi) / 2.0,
                                        ALU.mult, ALU.add))
            nc.vector.nop().then_inc(angle, 1)
            dve.wait_ge(sine, 1)
            own(nc.vector.tensor_scalar(cutoff[:, :], cutoff[:, :], 0.5, 0.5, ALU.mult, ALU.add))
            own(nc.vector.tensor_tensor(spots[:, :, 1], cutoff[:, :], under[:, :], ALU.mult))
            own(nc.vector.tensor_scalar(spots[:, :, 2], spots[:, :, 1], -1.0, None, ALU.mult))
            dve.wait_ge(high_done, 1)
            own(nc.vector.scalar_tensor_tensor(q_parts[:, :, 1, :], keep["q"][:, :, :], keep["q_scale"][:, 0:1],
                                               q_parts[:, :, 0, :], ALU.mult, ALU.subtract))

        def beside(block, move_rows):
            @block.scalar
            def _(act):
                nc.scalar.activation(q_parts[:, :, 0, :], keep["q"][:, :, :], ACT.Identity,
                                     scale=keep["q_scale"][:, 0:1]).then_inc(high_done, 1)
                move_rows(act)
                act.wait_ge(angle, 1)
                nc.scalar.activation(cutoff[:, :], cutoff[:, :], ACT.Sin).then_inc(sine, 1)

        def partitions(pool):
            nc.gpsimd.iota(partition[:, :], pattern=[[0, 1]], base=0, channel_multiplier=1,
                           allow_small_or_imprecise_dtypes=True).then_inc(numbered, 1)

        staircase_steps(nc, "esteps", io, P, EDGE_STEPS, kept, beside, partitions, places=io["dst_place"])

        with Scope(nc, "edge") as sc:
            w = sc.sb("w", [ATTR + 1, 2 * D])
            total = sc.sb("total", [P, NODE_TILES, D])
            attr = sc.sb("attr", [ATTR + 1, U, P])
            dst_all = sc.sb("dst_all", [P, U, P], F16)
            pick = sc.sb("pick", [P, U, P], F16)
            kv = sc.sb("kv", [P, U, 2 * D])
            src_now = sc.sb("src_now", [P, U], I32)
            spot_now = sc.sb("spot_now", [P, U, 3])
            apart = sc.sb("apart", [P, U, P], F16)
            d_kv = sc.sb("d_kv", [P, U, 2 * D])
            hot = sc.sb("hot", [P, U, P])
            prod = sc.sb("prod", [P, U, D])
            message = sc.sb("message", [P, U, D])
            score = sc.sb("score", [P, U])
            attn = sc.sb("attn", [P, U])
            ps_d = sc.ps("ps_d", [P, G, 512])
            ps_q = sc.ps("ps_q", [P, G // 2, 2, D])
            ps_m = sc.ps("ps_m", [P, G // 2, 2, D])
            gathered, attr_in, dst_in = sc.sems("gathered", U), sc.sems("attr_in", U // 2), sc.sems("dst_in", 2)
            (consts, set_up, sources, spotted, distanced, hots, multiplied, q_picked, picks, activated, paired, scored,
             weighted, messaged, scattered, added, stored, tick) = (sc.sem(n) for n in (
                 "consts", "set_up", "sources", "spotted", "distanced", "hots", "multiplied", "q_picked", "picks",
                 "activated", "paired", "scored", "weighted", "messaged", "scattered", "added", "stored", "tick"))
            block = sc.block()
            dst_flat = io["dst_place"].rearrange("t e -> (t e)")

            def halves(n):
                return range(n * G, n * G + G)

            @block.sync
            def _(sp):
                def columns(i, n):
                    return nc.values_load_multi_w_load_instructions(
                        column[0:1, bass.ds(i * U + n * G, G)], engines=[mybir.EngineType.SP], min_val=0,
                        max_val=EDGES_P - P,
                        skip_runtime_bounds_check_because="the chip counted these tiles itself")[1]

                def load_attr(i, n, used=None):
                    for k, t in zip(halves(n), columns(i, n)):
                        if used is not None and k % 2 == 0:
                            sp.wait_ge(multiplied, used * U + k + 2)
                            sp.sem_inc(tick, 1)
                        sp.dma_start(attr[:, k, :], io["attr_t"][:, bass.ds(t, P)]).then_inc(attr_in[k // 2], 16)

                def load_dst(i, n):
                    row = dst_flat[bass.ds((i * U + n * G) * P, G * P)]
                    sp.dma_start(dst_all[:, n * G:n * G + G, :].rearrange("p k e -> p (k e)"),
                                 row.partition_broadcast(P)).then_inc(dst_in[n], 16)

                rounds = EDGE_STEPS // U
                for n in range(2):
                    load_dst(0, n)
                sp.dma_start(w[:, :], io["w_dkv"]).then_inc(consts, 16)
                for n in range(2):
                    load_attr(0, n)
                for n in range(2):
                    sp.wait_ge(picks, n + 1)
                    load_dst(1, n)
                with sp.Fori(1, rounds - 1) as i:
                    for n in range(2):
                        load_attr(i, n, used=i - 1)
                        sp.wait_ge(picks, i * 2 + n + 1)
                        sp.sem_inc(tick, 1)
                        load_dst(i + 1, n)
                for n in range(2):
                    load_attr(rounds - 1, n, used=rounds - 2)
                sp.wait_ge(added, EDGE_STEPS + G)
                sp.dma_start(io["edge_sum"].rearrange("(t p) f -> p t f", p=P), total[:, :, :]).then_inc(stored, 16)
                sp.wait_ge(stored, 16)

            @block.gpsimd
            def _(pool):
                nc.gpsimd.memset(total[:, :, :], 0.0).then_inc(set_up, 1)
                with pool.Fori(0, EDGE_STEPS // U) as i:
                    for n in range(2):
                        half = slice(n * G, n * G + G)
                        pool.wait_ge(messaged, i * U + n * G + G)
                        pool.sem_inc(tick, 1)
                        nc.gpsimd.tensor_copy(src_now[:, half], src_row[:, bass.ds(i * U + n * G, G)]).then_inc(sources, 1)
                        pool.wait_ge(sources, i * 2 + n + 1)
                        pool.sem_inc(tick, 1)
                        for k in halves(n):
                            nc.gpsimd.indirect_dma_start(
                                kv[:, k, :], None, io["kv"], bass.IndirectOffsetOnAxis(ap=src_now[:, k:k + 1], axis=0),
                                bounds_check=NODES_P - 1).then_inc(gathered[k], 16)

            @block.tensor
            def _(pe):
                def make(i, n):
                    _, windows = nc.values_load_multi_w_load_instructions(
                        window[0:1, bass.ds(i * U + n * G, G)], engines=[mybir.EngineType.PE], min_val=0,
                        max_val=NODE_TILES - 1,
                        skip_runtime_bounds_check_because="the chip counted these windows itself")
                    pe.wait_ge(activated, i * U + n * G + G)
                    pe.sem_inc(tick, 1)
                    for k in halves(n):
                        if k % G == G // 2:
                            pick_q(i, n, windows)
                        if k % 2 == 0:
                            pe.wait_ge(attr_in[k // 2], i * 32 + 32)
                            pe.sem_inc(tick, 1)
                        nc.tensor.matmul(ps_d[:, k % G, :], attr[:, k, :], w[:, :], start=True,
                                         stop=True).then_inc(multiplied, 1)

                def pick_q(i, n, windows):
                    pe.wait_ge(paired, i * U + n * G + G)
                    pe.sem_inc(tick, 1)
                    pe.wait_ge(picks, i * 2 + n + 1)
                    pe.sem_inc(tick, 1)
                    for k in halves(n):
                        for part in range(2):
                            last = nc.tensor.matmul(ps_q[:, k % G // 2, k % 2, :], pick[:, k, :], q_parts[
                                :, bass.ds(windows[k % G], 1), part, :].rearrange("p a f -> p (a f)"),
                                start=(part == 0), stop=(part == 1))
                        last.then_inc(q_picked, 1)

                def scatter(i, n):
                    pe.wait_ge(hots, i * U + n * G + G)
                    pe.sem_inc(tick, 1)
                    pe.wait_ge(added, i * U + n * G + G)
                    pe.sem_inc(tick, 1)
                    for k in halves(n):
                        pe.wait_ge(messaged, i * U + k + 1 + U)
                        pe.sem_inc(tick, 1)
                        nc.tensor.matmul(ps_m[:, k % G // 2, k % 2, :], hot[:, k, :], message[:, k, :], start=True,
                                         stop=True).then_inc(scattered, 1)

                pe.sem_inc(q_picked, U)
                pe.sem_inc(scattered, U)
                pe.wait_ge(consts, 16)
                make(0, 0)
                with pe.Fori(0, EDGE_STEPS // U - 1) as i:
                    make(i, 1)
                    scatter(i, 0)
                    make(i + 1, 0)
                    scatter(i, 1)
                last = EDGE_STEPS // U - 1
                make(last, 1)
                scatter(last, 0)
                scatter(last, 1)

            @block.scalar
            def _(act):
                def activate(i, n):
                    for k in halves(n):
                        act.wait_ge(messaged, i * U + k + 1)
                        act.sem_inc(tick, 1)
                        act.wait_ge(multiplied, i * U + k + 1)
                        nc.scalar.activation(d_kv[:, k, :], ps_d[:, k % G, :], ACT.Silu).then_inc(activated, 1)

                def weigh(i, n):
                    for k in halves(n):
                        act.wait_ge(scored, i * U + k + 1)
                        nc.scalar.activation(attn[:, k:k + 1], score[:, k:k + 1], ACT.Silu).then_inc(weighted, 1)

                def mark(i, n):
                    act.wait_ge(hots, i * U + n * G)
                    act.sem_inc(tick, 1)
                    act.wait_ge(scattered, i * U + n * G + G)
                    act.sem_inc(tick, 1)
                    nc.scalar.activation(spot_now[:, n * G:n * G + G, :], spots[:, bass.ds(i * U + n * G, G), :],
                                         ACT.Copy).then_inc(spotted, 1)
                    act.wait_ge(spotted, i * 2 + n + 1)
                    act.sem_inc(tick, 1)
                    for k in halves(n):
                        nc.scalar.activation(apart[:, k, :], keep["iota"][:, 0:P], ACT.Abs,
                                             bias=spot_now[:, k, 0:1], scale=-1.0).then_inc(distanced, 1)
                    for k in halves(n):
                        act.wait_ge(distanced, i * U + k + 1)
                        nc.scalar.activation(hot[:, k, :], apart[:, k, :], ACT.Relu, bias=spot_now[:, k, 1:2],
                                             scale=spot_now[:, k, 2:3]).then_inc(hots, 1)

                act.sem_inc(activated, G)
                activate(0, 0)
                mark(0, 0)
                with act.Fori(0, EDGE_STEPS // U - 1) as i:
                    weigh(i, 0)
                    activate(i, 1)
                    mark(i, 1)
                    weigh(i, 1)
                    activate(i + 1, 0)
                    mark(i + 1, 0)
                weigh(EDGE_STEPS // U - 1, 0)
                activate(EDGE_STEPS // U - 1, 1)
                mark(EDGE_STEPS // U - 1, 1)
                weigh(EDGE_STEPS // U - 1, 1)

            @block.vector
            def _(dve):
                def pick_places(i, n):
                    dve.wait_ge(q_picked, i * U + n * G + G)
                    dve.wait_ge(dst_in[n], i * 16 + 16)
                    half = slice(n * G, n * G + G)
                    nc.vector.tensor_scalar(pick[:, half, :], dst_all[:, half, :], partition[:, :], None,
                                            ALU.is_equal).then_inc(picks, 1)

                def pair(i, n, k):
                    dve.wait_ge(gathered[k], i * 16 + 16)
                    nc.vector.scalar_tensor_tensor(prod[:, k, :], ps_q[:, k % G // 2, k % 2, :],
                                                   keep["q_scale"][:, 1:2], kv[:, k, 0:D], ALU.mult,
                                                   ALU.mult).then_inc(paired, 1)

                def score_step(i, k):
                    dve.wait_ge(paired, i * U + k + 1 + G)
                    dve.wait_ge(activated, i * U + k + 1 + G)
                    nc.vector.scalar_tensor_tensor(prod[:, k, :], prod[:, k, :], 1.0, d_kv[:, k, 0:D], ALU.mult,
                                                   ALU.mult, accum_out=score[:, k:k + 1]).then_inc(scored, 1)

                def weigh(i, n):
                    for k in halves(n):
                        dve.wait_ge(weighted, i * U + k + 1)
                        nc.vector.scalar_tensor_tensor(message[:, k, :], kv[:, k, D:2 * D], attn[:, k:k + 1],
                                                       d_kv[:, k, D:2 * D], ALU.mult, ALU.mult).then_inc(messaged, 1)

                def add(i, k, windows):
                    if k % 2 == 0:
                        dve.wait_ge(scattered, i * U + k + 2 + U)
                    acc = total[:, bass.ds(windows[k], 1), :].rearrange("p a f -> p (a f)")
                    dve.wait_ge(added, i * U + k + G)
                    nc.vector.tensor_tensor(acc, acc, ps_m[:, k % G // 2, k % 2, :], ALU.add).then_inc(added, 1)

                def turn(i, n, windows, next_i, ahead=True):
                    a, b = n * G, (1 - n) * G
                    dve.wait_ge(q_picked, next_i * U + b + G + U)
                    for k in range(3):
                        pair(next_i, 1 - n, b + k)
                    add(i, a, windows)
                    pair(next_i, 1 - n, b + 3)
                    add(i, a + 1, windows)
                    if ahead:
                        pick_places(i + 1, n)
                    score_step(next_i, b)
                    add(i, a + 2, windows)
                    score_step(next_i, b + 1)
                    add(i, a + 3, windows)
                    score_step(next_i, b + 2)
                    score_step(next_i, b + 3)
                    weigh(next_i, 1 - n)

                def windows_of(at):
                    return nc.values_load_multi_w_load_instructions(
                        window[0:1, at], engines=[mybir.EngineType.DVE], min_val=0, max_val=NODE_TILES - 1,
                        skip_runtime_bounds_check_because="the chip counted these windows itself")[1]

                dve.sem_inc(messaged, U)
                dve.sem_inc(added, G)
                dve.sem_inc(paired, G)
                dve.wait_ge(set_up, 1)
                pick_places(0, 0)
                pick_places(0, 1)
                dve.wait_ge(q_picked, G + U)
                for k in range(G):
                    pair(0, 0, k)
                for k in range(G):
                    score_step(0, k)
                weigh(0, 0)
                with dve.Fori(0, EDGE_STEPS // U - 1) as i:
                    windows = windows_of(bass.ds(i * U, U))
                    turn(i, 0, windows, i)
                    turn(i, 1, windows, i + 1)
                last = EDGE_STEPS // U - 1
                windows = windows_of(slice(EDGE_STEPS - U, EDGE_STEPS))
                turn(last, 0, windows, last, ahead=False)
                for k in range(G, U):
                    add(last, k, windows)


def attention_update(nc, io, keep):
    with Scope(nc, "attn") as sc:
        w = sc.sb("w", [P, HALF, D])
        b = sc.sb("b", [P, D])
        s = sc.sb("s", [P, SLOTS, D])
        x = sc.sb("x", [P, SLOTS, D])
        s_t = sc.sb("s_t", [P, SLOTS, HALF, P])
        y = sc.sb("y", [P, SLOTS, D])
        turned_ps = sc.ps("turned_ps", [P, 2, 512])
        ps = sc.ps("ps", [P, SLOTS, 512])
        norm = Norm(sc)
        result = sc.sb("result", [P, NODE_TILES, D])
        s_in, x_in = sc.sems("s_in", SLOTS), sc.sems("x_in", SLOTS)
        stored, restored = sc.sem("stored"), sc.sem("restored")
        consts, turned, s_ready, multiplied, biased, added, ready, tick = (
            sc.sem(n) for n in ("consts", "turned", "s_ready", "multiplied", "biased", "added", "ready", "tick"))
        block = sc.block()

        @block.sync
        def _(sp):
            def restore(tiles):
                columns = slice(0, RESTORED * CHUNK)
                sp.dma_start(keep["adj"][:, tiles, columns], io["adj_copy"][:, tiles, columns]).then_inc(restored, 16)

            sp.dma_start(w[:, :, :], io["w_out"].rearrange("(h p) n -> p h n", p=P)).then_inc(consts, 16)
            sp.dma_start(b[:, :], io["b_out"]).then_inc(consts, 16)
            for k in range(SLOTS):
                sp.dma_start(s[:, k, :], tile_rows(io["edge_sum"])(k)).then_inc(s_in[k], 16)
                sp.dma_start(x[:, k, :], tile_rows(io["x2"])(k)).then_inc(x_in[k], 16)
            restore(slice(0, SLOTS))
            with sp.Fori(1, ROUNDS) as i:
                for k in range(SLOTS):
                    sp.wait_ge(turned, (i - 1) * SLOTS + k + 1)
                    sp.dma_start(s[:, k, :], tile_rows(io["edge_sum"])(i * SLOTS + k)).then_inc(s_in[k], 16)
                    restore(bass.ds(i * SLOTS + k, 1))
                for k in range(SLOTS):
                    sp.wait_ge(added, (i - 1) * SLOTS + k + 1)
                    sp.dma_start(x[:, k, :], tile_rows(io["x2"])(i * SLOTS + k)).then_inc(x_in[k], 16)
            sp.wait_ge(restored, 16 * (1 + NODE_TILES - SLOTS))

        @block.tensor
        def _(pe):
            pe.wait_ge(consts, 32)
            def turn(i, k):
                pe.wait_ge(s_in[k], i * 16 + 16)
                pe.sem_inc(tick, 1)
                pe.wait_ge(s_ready, i * SLOTS + k + (2 if k == 0 else 1))
                pe.sem_inc(tick, 1)
                for h in range(HALF):
                    last = nc.tensor.transpose(turned_ps[:, k % 2, h * P:(h + 1) * P], s[:, k, h * P:(h + 1) * P],
                                               keep["ident"][:, :])
                last.then_inc(turned, 1)

            with pe.Fori(0, ROUNDS) as i:
                turn(i, 0)
                for k in range(SLOTS):
                    if k + 1 < SLOTS:
                        turn(i, k + 1)
                    pe.wait_ge(biased, i * SLOTS + k + 1)
                    pe.sem_inc(tick, 1)
                    pe.wait_ge(s_ready, i * SLOTS + k + 3)
                    pe.sem_inc(tick, 1)
                    for h in range(HALF):
                        last = nc.tensor.matmul(ps[:, k, 0:D], s_t[:, k, h, :], w[:, h, :], start=(h == 0), stop=(h == 1))
                    last.then_inc(multiplied, 1)

        @block.scalar
        def _(act):
            act.sem_inc(s_ready, 2)
            with act.Fori(0, ROUNDS) as i:
                for k in range(SLOTS):
                    act.wait_ge(biased, i * SLOTS + k + 1)
                    act.sem_inc(tick, 1)
                    act.wait_ge(turned, i * SLOTS + k + 1)
                    nc.scalar.activation(s_t[:, k, :, :].rearrange("p h n -> p (h n)"), turned_ps[:, k % 2, 0:D],
                                         ACT.Copy).then_inc(s_ready, 1)

        @block.vector
        def _(dve):
            dve.sem_inc(ready, SLOTS)
            dve.sem_inc(biased, SLOTS)
            dve.wait_ge(consts, 32)
            with dve.Fori(0, ROUNDS) as i:
                each(dve, i, [multiplied, ready], lambda k: nc.vector.tensor_tensor(
                    y[:, k, :], ps[:, k, 0:D], b[:, :], ALU.add), biased)
                for k in range(SLOTS):
                    dve.wait_ge(x_in[k], i * 16 + 16)
                    dve.wait_ge(biased, i * SLOTS + k + 1 + SLOTS)
                    nc.vector.scalar_tensor_tensor(y[:, k, :], x[:, k, :], 2.0, y[:, k, :], ALU.mult,
                                                   ALU.add).then_inc(added, 1)
                norm.on_vector(nc, dve, i, lambda k: y[:, k, :], added, lambda k: result[
                    :, bass.ds(i * SLOTS + k, 1), :].rearrange("p a f -> p (a f)"), ready)

        @block.gpsimd
        def _(pool):
            finish_rounds(nc, pool, norm, [(io["x3"], lambda i: result[:, bass.ds(i * SLOTS, SLOTS), :])], ready, SLOTS,
                          stored, tick)


def program(nc, io):
    with Scope(nc, "all") as sc:
        keep = {
            "dinv": sc.sb("dinv", [P, NODE_TILES]),
            "ident": sc.sb("ident", [P, P]),
            "x_scale": sc.sb("x_scale", [P, 2]),
            "z_scale": sc.sb("z_scale", [P, 2]),
            "q_scale": sc.sb("q_scale", [P, 2]),
            "iota": sc.sb("iota", [P, NODE_TILES * RELS], F16),
        }
        with Scope(nc, "first") as held:
            keep["adj"] = held.sb("adj", [P, NODE_TILES, NODES_P], F16)
            with Scope(nc, "steps") as st:
                keep["cells"] = st.sb("cells", [P, BUILD_STEPS + 8, 2])
                keep["window"] = st.sb("window", [1, BUILD_STEPS], I32)
                build_steps(nc, io, keep)
                histogram(nc, io, keep)
                build_matrix(nc, io, keep)
            aggregate(nc, io, keep, "agg0", io["x"], scaled=True, save=True, scales=keep["x_scale"])
            gcn_update(nc, io, keep, "gcn0", io["w1"], io["b1"], io["z1"], scales=keep["z_scale"][:, :])
            aggregate(nc, io, keep, "agg1", io["z1"], scales=keep["z_scale"])
            gcn_update(nc, io, keep, "gcn1", io["w2"], io["b2"], io["x1"], residual=io["x"])
            aggregate(nc, io, keep, "agg2", io["x1"], relations=True)
        gru_update(nc, io, keep)
        with Scope(nc, "third") as held:
            keep["q"] = held.sb("q", [P, NODE_TILES, D])
            attention_inputs(nc, io, keep)
            attention_edges(nc, io, keep)
        with Scope(nc, "second") as held:
            keep["adj"] = held.sb("adj", [P, NODE_TILES, NODES_P], F16)
            attention_update(nc, io, keep)
            aggregate(nc, io, keep, "agg3", io["x3"], scaled=True, restore=True)
        gcn_update(nc, io, keep, "gcn3", io["w3"], io["b3"], io["out"], residual=io["x3"], relu=False)


def kernel(**inputs):
    import concourse.bacc as bacc
    from concourse.bass_utils import run_bass_kernel_spmd

    a = {k: np.asarray(v) for k, v in inputs.items()}
    nc = bacc.Bacc("TRN2", target_bir_lowering=False, num_devices=1)
    arrays, io = {}, {}

    def give(name, array):
        array = np.ascontiguousarray(array)
        arrays[name] = array
        io[name] = nc.dram_tensor(name, list(array.shape), mybir.dt.from_np(array.dtype), kind="ExternalInput").ap()

    def edges(v, fill):
        return np.concatenate([v, np.full(EDGES_P - EDGES, fill, v.dtype)]).reshape(EDGE_TILES, P)

    src, dst = edges(a["src"], 0), edges(a["dst"], NO_NODE)
    give("src_t", src)
    give("dst_t", dst)
    give("next_t", np.concatenate([dst[1:, 0], np.full(1, NO_NODE, dst.dtype)]))
    give("wts_t", edges(a["edge_weight"], 0))
    give("dst_p", dst.T)
    give("rel_p", edges(a["edge_type_16"], 0).T)

    def scratch(name, shape, dt=F32, kind="Internal"):
        io[name] = nc.dram_tensor(name, list(shape), dt, kind=kind).ap()

    def nodes(v):
        return np.concatenate([v, np.zeros((NODES_P - NODES, D), v.dtype)])

    def rows(v):
        return np.broadcast_to(v.reshape(1, -1), (P, v.size))

    give("x", nodes(a["x"]))
    give("attr_t", np.concatenate([np.concatenate([a["edge_attr_64"].T, np.zeros((ATTR, EDGES_P - EDGES), np.float32)], 1),
                                   np.ones((1, EDGES_P), np.float32)]))
    give("w_dkv", np.concatenate([
        np.concatenate([a["L2_gnn_Wdk"].T, a["L2_gnn_Wdv"].T], 1),
        np.concatenate([a["L2_gnn_bdk"], a["L2_gnn_bdv"]])[None]]))
    give("relvectors", a["L1_gnn_relvectors"])
    give("w1", a["L0_gnn_W1"])
    give("b1", rows(a["L0_gnn_b1"]))
    give("w2", a["L0_gnn_W2"])
    give("b2", rows(a["L0_gnn_b2"]))
    give("w3", a["L3_gnn_W"].T)
    give("b3", rows(a["L3_gnn_b"]))
    give("w_in", a["L1_gnn_w_ih"].T)
    give("b_in", rows(a["L1_gnn_b_ih"]))
    give("w_hid", a["L1_gnn_w_hh"].T)
    give("b_hid", rows(a["L1_gnn_b_hh"]))
    give("w_qkv", np.concatenate([a["L2_gnn_Wq"].T, a["L2_gnn_Wk"].T, a["L2_gnn_Wv"].T], 1))
    give("b_qkv", rows(np.concatenate([a["L2_gnn_bq"], a["L2_gnn_bk"], a["L2_gnn_bv"]])))
    give("w_out", a["L2_gnn_Wo"].T)
    give("b_out", rows(a["L2_gnn_bo"]))
    give("ln_g", rows(a["L2_gnn_ln_g"]))
    give("ln_b", rows(a["L2_gnn_ln_b"]))

    scratch("rel_counts", [RELS, NODES_P])
    scratch("dst_place", [EDGE_STEPS, P], F16)
    scratch("adj_copy", [P, NODE_TILES, NODES_P], F16)
    scratch("agg_t", [HALF, P, NODES_P])
    for name in ("z1", "x1", "x2", "x3", "edge_sum"):
        scratch(name, [NODES_P, D])
    scratch("kv", [NODES_P, 2 * D])
    scratch("out", [NODES_P, D], kind="ExternalOutput")
    program(nc, io)
    r = run_bass_kernel_spmd(nc, [arrays], core_ids=[0])
    return r.results[0]["out"][0:NODES]
```
